# Optimizing a Trainium2 kernel written in Bass

```python
import numpy as np
import jax
import jax.numpy as jnp

def _softmax(x, axis=-1):
    return jax.nn.softmax(x, axis=axis)

def _gelu(x):
    return jax.nn.gelu(x, approximate=True)

def _silu(x):
    return jax.nn.silu(x)

def _sigmoid(x):
    return jax.nn.sigmoid(x)

def _layernorm(x, axis=-1, eps=1e-05):
    m = jnp.mean(x, axis=axis, keepdims=True)
    v = jnp.var(x, axis=axis, keepdims=True)
    return (x - m) / jnp.sqrt(v + eps)

def _scatter_add(tgt, idx, src, axis=0):
    return tgt.at[idx].add(src)

def _segment_sum(src, seg, n):
    return jax.ops.segment_sum(src, seg, n)
kernel_name = 'mk_macaron_d1_jaxref_r4_05bff1'

def setup_inputs(seed: int=0):
    np.random.seed(seed)
    _w = jnp.asarray

    def _L0_attn_setup():
        import jax, jax.numpy as jnp
        import numpy as np
        B, T, D_MODEL = (2, 256, 256)
        H, DEPTH = (8, 5)
        DH = D_MODEL // H
        key = jax.random.key(seed)
        k_x, k_wp, k_bp, k_wv, k_wo = jax.random.split(key, 5)
        x = jax.random.normal(k_x, (B, T, D_MODEL), dtype=jnp.float32)
        Wp = jax.random.normal(k_wp, (D_MODEL, H * DEPTH), dtype=jnp.float32) * 0.02
        bp = jnp.zeros((H * DEPTH,), dtype=jnp.float32)
        Wv = jax.random.normal(k_wv, (D_MODEL, D_MODEL), dtype=jnp.float32) * 0.02
        Wo = jax.random.normal(k_wo, (D_MODEL, D_MODEL), dtype=jnp.float32) * 0.02
        return {'x': x, 'Wp': Wp, 'bp': bp, 'Wv': Wv, 'Wo': Wo}
    _L0_attn_in = _L0_attn_setup()

    def _L0_ffn_setup():
        import math
        import jax, jax.numpy as jnp
        import numpy as np
        HIDDEN = 256
        INTER = 1024
        EXPERTS = 8
        B, T = (4, 512)
        EPS = 1e-12
        CAP_FACTOR = 1.0
        MIN_CAP = 4

        def layer_norm(x, g, b, eps=EPS):
            m = jnp.mean(x, axis=-1, keepdims=True)
            v = jnp.var(x, axis=-1, keepdims=True)
            return (x - m) * jax.lax.rsqrt(v + eps) * g + b

        def top1_gate(x, wg, capacity):
            logits = x @ wg
            gates = jax.nn.softmax(logits, axis=-1)
            E = wg.shape[-1]
            idx = jnp.argmax(gates, axis=-1)
            mask1 = jax.nn.one_hot(idx, E, dtype=gates.dtype)
            locations = jnp.cumsum(mask1, axis=0) - mask1
            mask1 = mask1 * (locations < capacity).astype(gates.dtype)
            gates1_s = jnp.sum(gates * mask1, axis=-1)
            loc_s = jnp.sum(locations * mask1, axis=-1).astype(jnp.int32)
            loc_oh = jax.nn.one_hot(loc_s, capacity, dtype=gates.dtype)
            combine = gates1_s[:, None, None] * mask1[:, :, None] * loc_oh[:, None, :]
            dispatch = jax.lax.stop_gradient((combine > 0).astype(x.dtype))
            return (combine, dispatch)
        key = jax.random.key(seed)
        ks = jax.random.split(key, 8)
        s = 0.02
        return {'x': jax.random.normal(ks[0], (B, T, HIDDEN), jnp.float32), 'attn_nw': jnp.ones((HIDDEN,), jnp.float32), 'attn_nb': jnp.zeros((HIDDEN,), jnp.float32), 'wg': jax.random.normal(ks[1], (HIDDEN, EXPERTS), jnp.float32) * s, 'inter_w': jax.random.normal(ks[2], (EXPERTS, HIDDEN, INTER), jnp.float32) * s, 'inter_b': jnp.zeros((EXPERTS, INTER), jnp.float32), 'output_w': jax.random.normal(ks[3], (EXPERTS, INTER, HIDDEN), jnp.float32) * s, 'output_b': jnp.zeros((EXPERTS, HIDDEN), jnp.float32), 'res_inter_w': jax.random.normal(ks[4], (HIDDEN, INTER), jnp.float32) * s, 'res_inter_b': jnp.zeros((INTER,), jnp.float32), 'res_output_w': jax.random.normal(ks[5], (INTER, HIDDEN), jnp.float32) * s, 'res_output_b': jnp.zeros((HIDDEN,), jnp.float32), 'res_coef': jax.random.normal(ks[6], (HIDDEN, 2), jnp.float32) * s}
    _L0_ffn_in = _L0_ffn_setup()
    _d = {'L0_attn_x': _L0_attn_in['x'], 'L0_attn_Wp': _L0_attn_in['Wp'], 'L0_attn_bp': _L0_attn_in['bp'], 'L0_attn_Wv': _L0_attn_in['Wv'], 'L0_attn_Wo': _L0_attn_in['Wo'], 'L0_ffn_attn_nw': _L0_ffn_in['attn_nw'], 'L0_ffn_attn_nb': _L0_ffn_in['attn_nb'], 'L0_ffn_wg': _L0_ffn_in['wg'], 'L0_ffn_inter_w': _L0_ffn_in['inter_w'], 'L0_ffn_inter_b': _L0_ffn_in['inter_b'], 'L0_ffn_output_w': _L0_ffn_in['output_w'], 'L0_ffn_output_b': _L0_ffn_in['output_b'], 'L0_ffn_res_inter_w': _L0_ffn_in['res_inter_w'], 'L0_ffn_res_inter_b': _L0_ffn_in['res_inter_b'], 'L0_ffn_res_output_w': _L0_ffn_in['res_output_w'], 'L0_ffn_res_output_b': _L0_ffn_in['res_output_b'], 'L0_ffn_res_coef': _L0_ffn_in['res_coef']}
    _x0 = _d['L0_attn_x']
    _d['L0_attn_x'] = jax.random.normal(jax.random.fold_in(jax.random.key(seed), 1), (2, 2048, 256), dtype=_x0.dtype)
    del _x0
    return _d

def reference(L0_attn_x, L0_attn_Wp, L0_attn_bp, L0_attn_Wv, L0_attn_Wo, L0_ffn_attn_nw, L0_ffn_attn_nb, L0_ffn_wg, L0_ffn_inter_w, L0_ffn_inter_b, L0_ffn_output_w, L0_ffn_output_b, L0_ffn_res_inter_w, L0_ffn_res_inter_b, L0_ffn_res_output_w, L0_ffn_res_output_b, L0_ffn_res_coef):

    def _L0_attn_ref(x, Wp, bp, Wv, Wo):
        import jax, jax.numpy as jnp
        import numpy as np
        B, T, D_MODEL = (2, 256, 256)
        H, DEPTH = (8, 5)
        DH = D_MODEL // H
        Bx, Tx, d = x.shape
        paths = jax.nn.sigmoid(x @ Wp + bp)
        paths = paths.reshape(Bx, Tx, H, DEPTH).transpose(0, 2, 1, 3)
        pq = paths[:, :, :, None, :]
        pk = paths[:, :, None, :, :]
        agree = pq * pk + (1.0 - pq) * (1.0 - pk)
        sim = jnp.cumprod(agree, axis=-1).sum(axis=-1) / DEPTH
        mask = jnp.triu(jnp.ones((Tx, Tx), dtype=bool), k=1)
        sim = jnp.where(mask[None, None], -jnp.inf, sim)
        attn = jax.nn.softmax(sim, axis=-1)
        V = (x @ Wv).reshape(Bx, Tx, H, DH).transpose(0, 2, 1, 3)
        ctx = jnp.einsum('bhqk,bhkd->bhqd', attn, V)
        ctx = ctx.transpose(0, 2, 1, 3).reshape(Bx, Tx, d)
        return ctx @ Wo

    def _L0_ffn_ref(x, attn_nw, attn_nb, wg, inter_w, inter_b, output_w, output_b, res_inter_w, res_inter_b, res_output_w, res_output_b, res_coef):
        import math
        import jax, jax.numpy as jnp
        import numpy as np
        HIDDEN = 256
        INTER = 1024
        EXPERTS = 8
        B, T = (4, 512)
        EPS = 1e-12
        CAP_FACTOR = 1.0
        MIN_CAP = 4

        def layer_norm(x, g, b, eps=EPS):
            m = jnp.mean(x, axis=-1, keepdims=True)
            v = jnp.var(x, axis=-1, keepdims=True)
            return (x - m) * jax.lax.rsqrt(v + eps) * g + b

        def top1_gate(x, wg, capacity):
            logits = x @ wg
            gates = jax.nn.softmax(logits, axis=-1)
            E = wg.shape[-1]
            idx = jnp.argmax(gates, axis=-1)
            mask1 = jax.nn.one_hot(idx, E, dtype=gates.dtype)
            locations = jnp.cumsum(mask1, axis=0) - mask1
            mask1 = mask1 * (locations < capacity).astype(gates.dtype)
            gates1_s = jnp.sum(gates * mask1, axis=-1)
            loc_s = jnp.sum(locations * mask1, axis=-1).astype(jnp.int32)
            loc_oh = jax.nn.one_hot(loc_s, capacity, dtype=gates.dtype)
            combine = gates1_s[:, None, None] * mask1[:, :, None] * loc_oh[:, None, :]
            dispatch = jax.lax.stop_gradient((combine > 0).astype(x.dtype))
            return (combine, dispatch)
        Bx, Tx, M = x.shape
        S = Bx * Tx
        E = wg.shape[-1]
        capacity = max(MIN_CAP, math.ceil(S / E * CAP_FACTOR))
        residual = x.reshape(S, M)
        attn_out = layer_norm(residual, attn_nw, attn_nb)
        combine, dispatch = top1_gate(attn_out, wg, capacity)
        dispatched = jnp.einsum('sec,sm->ecm', dispatch, attn_out)
        h = jax.nn.gelu(jnp.einsum('ecm,emi->eci', dispatched, inter_w) + inter_b[:, None, :], approximate=True)
        expert_out = jnp.einsum('eci,eim->ecm', h, output_w) + output_b[:, None, :]
        moe_out = jnp.einsum('sec,ecm->sm', combine, expert_out)
        rh = jax.nn.gelu(attn_out @ res_inter_w + res_inter_b, approximate=True)
        res_mlp_out = rh @ res_output_w + res_output_b
        coef = jax.nn.softmax(attn_out @ res_coef, axis=-1)
        out = res_mlp_out * coef[:, :1] + moe_out * coef[:, 1:]
        out = out + residual
        return out.reshape(Bx, Tx, M)
    x = L0_attn_x
    x = x + 0.5 * _L0_ffn_ref(_layernorm(x, axis=-1), L0_ffn_attn_nw, L0_ffn_attn_nb, L0_ffn_wg, L0_ffn_inter_w, L0_ffn_inter_b, L0_ffn_output_w, L0_ffn_output_b, L0_ffn_res_inter_w, L0_ffn_res_inter_b, L0_ffn_res_output_w, L0_ffn_res_output_b, L0_ffn_res_coef)
    x = x + _L0_attn_ref(_layernorm(x, axis=-1), L0_attn_Wp, L0_attn_bp, L0_attn_Wv, L0_attn_Wo)
    x = x + 0.5 * _L0_ffn_ref(_layernorm(x, axis=-1), L0_ffn_attn_nw, L0_ffn_attn_nb, L0_ffn_wg, L0_ffn_inter_w, L0_ffn_inter_b, L0_ffn_output_w, L0_ffn_output_b, L0_ffn_res_inter_w, L0_ffn_res_inter_b, L0_ffn_res_output_w, L0_ffn_res_output_b, L0_ffn_res_coef)
    return x

_drawn_inputs = setup_inputs


def setup_inputs(seed=0):
    import zlib

    import numpy as np

    out = dict(_drawn_inputs(seed))
    spreads = {'L0_attn_bp': (0.0, 0.8),
     'L0_ffn_attn_nw': (1.0, 0.6),
     'L0_ffn_attn_nb': (0.0, 0.8),
     'L0_ffn_inter_b': (0.0, 0.8),
     'L0_ffn_output_b': (0.0, 0.8),
     'L0_ffn_res_inter_b': (0.0, 0.769),
     'L0_ffn_res_output_b': (0.0, 0.283)}
    factors = {'L0_attn_Wp': 8.0,
     'L0_attn_Wv': 8.0,
     'L0_attn_Wo': 8.0,
     'L0_ffn_wg': 6.76,
     'L0_ffn_inter_w': 8.0,
     'L0_ffn_output_w': 8.0,
     'L0_ffn_res_coef': 5.495}
    for name, (base, spread) in spreads.items():
        noise = np.random.default_rng([zlib.crc32(name.encode()), seed]).standard_normal(out[name].shape)
        drawn = base * np.exp(spread * noise) if base else spread * noise
        out[name] = jnp.asarray(drawn.astype(out[name].dtype))
    for name, factor in factors.items():
        out[name] = (out[name] * factor).astype(out[name].dtype)
    return out
```

```python
from contextlib import ExitStack
from math import sqrt

import concourse.bass as bass
from concourse import mybir

F32, F32R, F16, I32, U32 = (mybir.dt.float32, mybir.dt.float32r, mybir.dt.float16, mybir.dt.int32,
                            mybir.dt.uint32)
ALU = mybir.AluOpType
ACT = mybir.ActivationFunctionType
AX = mybir.AxisListType.X

P = 128
D = 256
KD = D // P
BATCH, SEQ = 2, 2048
TOKENS = BATCH * SEQ
NT = TOKENS // P
TT = 4
CH = TT * P
NC = TOKENS // CH
INTER = 1024
NK = INTER // P
NE = 8
CAP = TOKENS // NE
assert CAP == CH
NG = NE + 2
LN_EPS, FFN_EPS = 1e-5, 1e-12
H, DEPTH, DH = 8, 5, 32
NF = 2 ** DEPTH
HG = 4
QC = SEQ // CH
MASKED = -30000.0
UP_BANKS, H_RING, HS_RING = 2, 2, 4
AHEAD = 2


def subset_coefficient(m):
    return sum(0.5 ** d for d in range(max(m, 1), DEPTH + 1)) / DEPTH


def whole(ap, n):
    return ap.rearrange("(a n) -> a n", a=1).to_broadcast([n, ap.shape[0]])


def macaron(nc, x, Wp, bp, Wv, Wo, nw, nb, wg, inter_w, inter_b, output_w, output_b,
            res_inter_w, res_inter_b, res_output_w, res_output_b, res_coef, out):
    x_tiles = x.rearrange("b (t p) d -> p (b t) d", p=P)
    out_tiles = out.rearrange("b (t p) d -> p (b t) d", p=P)
    slots_in = nc.dram_tensor("slots_in", [2 * TOKENS, D], F32).ap()
    slots_out = nc.dram_tensor("slots_out", [TOKENS, D], F32).ap()

    with ExitStack() as top:
        def sb(name, shape, dt=F32):
            return top.enter_context(nc.sbuf_tensor(name, shape, dt))

        mem = dict(
            x_all=sb("x_all", [P, NT, D]),
            id32=sb("id32", [P, P]), id16=sb("id16", [P, P], F16),
            mask16=sb("mask16", [P, P], F16),
            before16=sb("before16", [P, P], F16),
            ones16=sb("ones16", [P, P], F16), ones32=sb("ones32", [P, DH]),
            minus_half=sb("minus_half", [P, 2 * TT]),
            rank=sb("rank", [P, NE]),
            trash=sb("trash", [P, NT]),
            same_expert=sb("same_expert", [P, NE, NT]),
            vecT=sb("vecT", [P, NE * NK + NK + 2 * KD]),
            wgc=sb("wgc", [P, KD, NG]),
            gather_at=sb("gather_at", [P, NT], U32), moe_w=sb("moe_w", [P, NT]),
        )
        constants(nc, mem, wg, res_coef, nw, nb, inter_b, res_inter_b, slots_in)
        for layer in range(2):
            dense_block(nc, mem, layer, x_tiles if layer == 0 else None, res_inter_w, res_output_w,
                        res_output_b, slots_in)
            expert_block(nc, mem, layer, inter_w, output_w, output_b, slots_in, slots_out)
            if layer == 0:
                attention_block(nc, mem, Wp, bp, Wv, Wo, slots_out)
            else:
                last_block(nc, mem, slots_out, out_tiles)


def constants(nc, mem, wg, res_coef, nw, nb, inter_b, res_inter_b, slots_in):
    id32, id16, mask16, before16 = mem["id32"], mem["id16"], mem["mask16"], mem["before16"]
    NV = NE * NK + NK + 2 * KD
    with ExitStack() as ctx:
        rows = ctx.enter_context(nc.sbuf_tensor("vec_rows", [NV, P], F32))
        ids = ctx.enter_context(nc.sbuf_tensor("token_ids", [P, NT], I32))
        ranks = ctx.enter_context(nc.sbuf_tensor("rank_ids", [P, NE], I32))
        zeros = ctx.enter_context(nc.sbuf_tensor("zeros", [P, 4, D], F32))
        vec_ps = ctx.enter_context(nc.psum_tensor("vec_ps", [P, NV], F32))
        loaded = ctx.enter_context(nc.semaphore("c_loaded"))
        filled = ctx.enter_context(nc.semaphore("c_filled"))
        made = ctx.enter_context(nc.semaphore("c_made"))
        turned = ctx.enter_context(nc.semaphore("c_turned"))
        zeroed = ctx.enter_context(nc.semaphore("c_zeroed"))
        block = ctx.enter_context(nc.Block())

        @block.sync
        def _(sp):
            n0 = NE * NK
            sp.dma_start(rows[0:n0, :], inter_b.rearrange("e (k p) -> (e k) p", p=P)).then_inc(loaded, 16)
            sp.dma_start(rows[n0:n0 + NK, :], res_inter_b.rearrange("(k p) -> k p", p=P)).then_inc(loaded, 16)
            sp.dma_start(rows[n0 + NK:n0 + NK + KD, :], nw.rearrange("(k p) -> k p", p=P)).then_inc(loaded, 16)
            sp.dma_start(rows[n0 + NK + KD:NV, :], nb.rearrange("(k p) -> k p", p=P)).then_inc(loaded, 16)
            with nc.allow_non_contiguous_dma("router weights, once"):
                sp.dma_start(mem["wgc"][:, :, 0:NE], wg.rearrange("(k p) e -> p k e", p=P)).then_inc(loaded, 16)
                sp.dma_start(mem["wgc"][:, :, NE:NG], res_coef.rearrange("(k p) e -> p k e", p=P)).then_inc(loaded, 16)
            sp.wait_ge(filled, 6)
            n = TOKENS // (P * 4)
            for i in range(n):
                sp.dma_start(slots_in[i * 4 * P:(i + 1) * 4 * P, :].rearrange("(p a) d -> p a d", a=4),
                             zeros[:]).then_inc(zeroed, 16)
            sp.wait_ge(zeroed, 16 * n)
            sp.wait_ge(loaded, 96)

        @block.gpsimd
        def _(pool):
            pool.memset(id32[:], 0.0).then_inc(filled, 1)
            pool.memset(id16[:], 0.0).then_inc(filled, 1)
            pool.memset(mask16[:], 0.0).then_inc(filled, 1)
            pool.memset(before16[:], 1.0).then_inc(filled, 1)
            pool.memset(mem["same_expert"][:], 1.0).then_inc(filled, 1)
            pool.memset(zeros[:], 0.0).then_inc(filled, 1)
            pool.memset(mem["ones16"][:], 1.0)
            pool.memset(mem["ones32"][:], 1.0)
            pool.memset(mem["minus_half"][:], -0.5)
            pool.wait_ge(filled, 6)
            for m in (id32, id16):
                pool.affine_select(out=m[:], in_=m[:], compare_op=ALU.not_equal, fill=1.0, base=0,
                                   pattern=[[-1, P]], channel_multiplier=1).then_inc(filled, 1)
            pool.affine_select(out=mask16[:], in_=mask16[:], compare_op=ALU.is_ge, fill=MASKED, base=0,
                               pattern=[[1, P]], channel_multiplier=-1)
            pool.affine_select(out=before16[:], in_=before16[:], compare_op=ALU.is_ge, fill=0.0, base=-1,
                               pattern=[[1, P]], channel_multiplier=-1)
            pool.memset(mem["same_expert"][:, :, 0:1], 0.0)
            pool.iota(ids[:], pattern=[[P, NT]], base=TOKENS, channel_multiplier=1).then_inc(filled, 1)
            pool.iota(ranks[:], pattern=[[-1, NE]], base=NE, channel_multiplier=0).then_inc(filled, 1)
            pool.wait_ge(filled, 10)
            pool.tensor_copy(mem["trash"][:], ids[:])
            pool.tensor_copy(mem["rank"][:], ranks[:]).then_inc(made, 1)

        @block.tensor
        def _(pe):
            pe.wait_ge(filled, 7)
            pe.wait_ge(loaded, 96)
            nc.tensor.transpose(vec_ps[:], rows[:], id32[0:NV, 0:NV]).then_inc(turned, 1)

        @block.vector
        def _(dve):
            dve.wait_ge(turned, 1)
            nc.vector.tensor_copy(mem["vecT"][:], vec_ps[:]).then_inc(made, 1)


class Mlp:

    def __init__(self, nc, ctx, tag):
        def sb(name, shape, dt=F32):
            return ctx.enter_context(nc.sbuf_tensor(f"{tag}_{name}", shape, dt))

        def sem(name):
            return ctx.enter_context(nc.semaphore(f"{tag}_{name}"))

        self.nc = nc
        self.x_hi, self.x_lo = sb("x_hi", [P, KD, CH], F32R), sb("x_lo", [P, KD, CH], F32R)
        self.h = sb("h", [P, H_RING, CH])
        self.h_hi, self.h_lo = sb("h_hi", [P, HS_RING, CH], F32R), sb("h_lo", [P, HS_RING, CH], F32R)
        self.up_ps = [ctx.enter_context(nc.psum_tensor(f"{tag}_up{i}", [P, CH], F32)) for i in range(UP_BANKS)]
        self.down_ps = [ctx.enter_context(nc.psum_tensor(f"{tag}_down{i}", [P, CH], F32)) for i in range(TT)]
        self.side = [ctx.enter_context(nc.psum_tensor(f"{tag}_side{i}", [P, CH], F32)) for i in range(2)]
        self.x_split = sem("x_split")
        self.x_hid = sem("x_hid")
        self.up_done = sem("up_done")
        self.gelu_done = sem("gelu_done")
        self.h_hid = sem("h_hid")
        self.h_split = sem("h_split")
        self.down_done = sem("down_done")
        self.evacuated = sem("evacuated")

    def split_x(self, dve, c, source):
        nc = self.nc
        if not (isinstance(c, int) and c == 0):
            dve.wait_ge(self.up_done, c * NK)
        nc.vector.tensor_copy(self.x_hi[:], source).then_inc(self.x_hid, 1)
        dve.wait_ge(self.x_hid, c + 1)
        nc.vector.tensor_tensor(self.x_lo[:], source, self.x_hi[:], ALU.subtract).then_inc(self.x_split, 1)

    def up(self, pe, c, k, w1_hi, w1_lo, first):
        nc = self.nc
        if not (first and k < UP_BANKS):
            pe.wait_ge(self.gelu_done, c * NK + (k - UP_BANKS + 1))
        bank = self.up_ps[k % UP_BANKS]
        n = 0
        for w, xs in ((w1_hi, self.x_hi), (w1_lo, self.x_hi), (w1_hi, self.x_lo)):
            for kd in range(KD):
                last = nc.tensor.matmul(bank[:], w(kd), xs[:, kd, :], start=(n == 0), stop=(n == 3 * KD - 1))
                n += 1
        last.then_inc(self.up_done, 1)

    def gelu(self, act, c, k, bias, first):
        act.wait_ge(self.up_done, c * NK + (k + 1))
        if not (first and k < H_RING):
            act.wait_ge(self.h_split, c * NK + (k - H_RING + 1))
        self.nc.scalar.activation(self.h[:, k % H_RING, :], self.up_ps[k % UP_BANKS][:],
                                  ACT.Gelu_apprx_tanh, bias=bias).then_inc(self.gelu_done, 1)

    def split_h(self, dve, c, k, first):
        nc = self.nc
        dve.wait_ge(self.gelu_done, c * NK + (k + 1))
        if not (first and k < HS_RING):
            dve.wait_ge(self.down_done, c * NK + (k - HS_RING + 1))
        h, hi, lo = self.h[:, k % H_RING, :], self.h_hi[:, k % HS_RING, :], self.h_lo[:, k % HS_RING, :]
        nc.vector.tensor_copy(hi, h).then_inc(self.h_hid, 1)
        dve.wait_ge(self.h_hid, c * NK + (k + 1))
        nc.vector.tensor_tensor(lo, h, hi, ALU.subtract).then_inc(self.h_split, 1)

    def down(self, pe, c, k, w2_hi, w2_lo, first):
        nc = self.nc
        pe.wait_ge(self.h_split, c * NK + (k + 1))
        if k == 0 and not first:
            pe.wait_ge(self.evacuated, c)
        for t in range(TT):
            hi = self.h_hi[:, k % HS_RING, t * P:(t + 1) * P]
            lo = self.h_lo[:, k % HS_RING, t * P:(t + 1) * P]
            bank = self.down_ps[t][:, 0:D]
            nc.tensor.matmul(bank, hi, w2_hi, start=(k == 0), stop=False)
            nc.tensor.matmul(bank, hi, w2_lo, start=False, stop=False)
            last = nc.tensor.matmul(bank, lo, w2_hi, start=False, stop=(k == NK - 1))
        last.then_inc(self.down_done, 1)

    def tensor_chunk(self, pe, c, weights, first=False, beside=None, release=None):
        pe.wait_ge(self.x_split, c + 1)
        for s in range(NK + AHEAD):
            if s < NK:
                w1_hi, w1_lo, _, _ = weights(pe, s, True)
                self.up(pe, c, s, w1_hi, w1_lo, first)
            if s >= AHEAD:
                k = s - AHEAD
                _, _, w2_hi, w2_lo = weights(pe, k, False)
                self.down(pe, c, k, w2_hi, w2_lo, first)
                if beside and k in beside:
                    beside[k]()


def split_sems(ctx, nc, tag, names):
    return {n: ctx.enter_context(nc.semaphore(f"{tag}_{n}")) for n in names.split()}


def wait_carried(nc, dve, scratch, sem, value):
    dve.wait_ge(sem, value)
    nc.vector.memset(scratch, 0.0)


A_CHAIN = 4
E_CHAIN = TT


def dense_block(nc, mem, layer, x_tiles, res_w1, res_w2, res_b2, slots_in):
    tag = f"d{layer}"
    x_all, wgc, vecT = mem["x_all"], mem["wgc"], mem["vecT"]
    with ExitStack() as ctx:
        def sb(name, shape, dt=F32):
            return ctx.enter_context(nc.sbuf_tensor(f"{tag}_{name}", shape, dt))

        m = Mlp(nc, ctx, tag)
        y_all = sb("y_all", [P, NT, D])
        aT_all = sb("aT_all", [P, KD, TOKENS])
        y = sb("y", [P, TT, D])
        aT = sb("aT", [P, KD, CH])
        w1 = [sb(f"w1_{n}", [P, KD, INTER], F32R) for n in ("hi", "lo")]
        w2 = [sb(f"w2_{n}", [P, NK, D], F32R) for n in ("hi", "lo")]
        raw1 = aT_all[:, 0, TOKENS - KD * INTER:].rearrange("p (k n) -> p k n", k=KD)
        raw2 = aT_all[:, 1, TOKENS - NK * D:].rearrange("p (k n) -> p k n", k=NK)
        b2 = sb("b2", [P, D])
        idle = sb("idle", [P, 1])
        stats, mv = sb("stats", [P, TT, 6]), sb("mv", [P, TT, 2])
        var, rstd = sb("var", [P, 2, TT]), sb("rstd", [P, 2, TT])
        lin = sb("lin", [P, 2, TT])
        logits = sb("logits", [P, NT, NG])
        dif, th = sb("dif", [P, TT]), sb("th", [P, TT])
        c0, c1 = sb("c0", [P, NT]), sb("c1", [P, NT])
        part = sb("part", [P, TT, D])
        top, eq = sb("top", [P, NT]), sb("eq", [P, NT, NE])
        lm, ex = sb("lm", [P, NT, NE]), sb("ex", [P, NT, NE])
        best, hot, hot16 = sb("best", [P, NT]), sb("hot", [P, NT, NE]), sb("hot16", [P, NT, NE], F16)
        incl, locs = sb("incl", [P, NE, NT]), sb("locs", [P, NE, NT])
        loc, keep, base = sb("loc", [P, NT]), sb("keep", [P, NT]), sb("base", [P, NT])
        t0, t1, rec = sb("t0", [P, NT]), sb("t1", [P, NT]), sb("rec", [P, NT])
        scatter_at = sb("scatter_at", [P, NT], U32)

        s = split_sems(ctx, nc, tag, "w_in w_hid w_split chain var_ready rstd_ready y_ready turned aT_ready "
                       "logits_done dif_ready th_ready mixed empty_chain gate lm_ready ex_ready hot_ready "
                       "counted scatter_ready scattered base_ready")
        x_in = [ctx.enter_context(nc.semaphore(f"{tag}_x_in{i}")) for i in range(NC)] if x_tiles is not None else None
        NB = NE * NK + NK
        gain = [vecT[:, NB + k:NB + k + 1] for k in range(KD)]
        shift = [vecT[:, NB + KD + k:NB + KD + k + 1] for k in range(KD)]
        b1 = [vecT[:, NE * NK + k:NE * NK + k + 1] for k in range(NK)]
        block = ctx.enter_context(nc.Block())

        @block.sync
        def _(sp):
            def load_x(c):
                sp.dma_start(x_all[:, c * TT:(c + 1) * TT, :], x_tiles[:, c * TT:(c + 1) * TT, :]).then_inc(x_in[c], 16)

            for c in range(2) if x_in else ():
                load_x(c)
            sp.dma_start(raw1, res_w1.rearrange("(k p) n -> p k n", p=P)).then_inc(s["w_in"], 16)
            sp.dma_start(raw2, res_w2.rearrange("(k p) n -> p k n", p=P)).then_inc(s["w_in"], 16)
            sp.dma_start(b2[:], whole(res_b2, P)).then_inc(s["w_in"], 16)
            for c in range(2, NC) if x_in else ():
                load_x(c)

        @block.gpsimd
        def _(pool):
            def rstd_of(a):
                pool.wait_ge(s["var_ready"], a + 1)
                nc.gpsimd.tensor_tensor(rstd[:].rearrange("p a t -> p (a t)"), var[:].rearrange("p a t -> p (a t)"),
                                        mem["minus_half"][:], ALU.pow).then_inc(s["rstd_ready"], 1)
            with pool.Fori(0, NC) as a:
                rstd_of(a)
            pool.wait_ge(s["scatter_ready"], 1)
            for t in range(NT):
                nc.gpsimd.indirect_dma_start(
                    out=slots_in, out_offset=bass.IndirectOffsetOnAxis(ap=scatter_at[:, t:t + 1], axis=0),
                    in_=y_all[:, t, :], in_offset=None).then_inc(s["scattered"], 16)
            pool.wait_ge(s["scattered"], 16 * NT)

        @block.vector
        def _(dve):
            v = nc.vector

            def stats_of(a):
                if x_in and isinstance(a, int) and a < 2:
                    dve.wait_ge(x_in[a], 16)
                for t in range(TT):
                    i = v.bn_stats(stats[:, t, :], x_all[:, a * TT + t, :])
                i.then_inc(s["chain"], 1)
                wait_carried(nc, dve, idle[:], s["chain"], a * A_CHAIN + 1)
                for t in range(TT):
                    i = v.bn_aggr(mv[:, t, :], stats[:, t, :])
                i.then_inc(s["chain"], 1)
                dve.wait_ge(s["chain"], a * A_CHAIN + 2)
                v.tensor_scalar(var[:, 0, :], mv[:, :, 1], LN_EPS, None, ALU.add)
                v.tensor_scalar(var[:, 1, :], mv[:, :, 1], 1.0 + FFN_EPS, FFN_EPS * LN_EPS, ALU.mult,
                                ALU.add).then_inc(s["var_ready"], 1)

            def rows_of(a):
                dve.wait_ge(s["rstd_ready"], a + 1)
                if not (isinstance(a, int) and a == 0):
                    dve.wait_ge(s["turned"], a)
                for t in range(TT):
                    i = v.tensor_scalar(y[:, t, :], x_all[:, a * TT + t, :], mv[:, t, 0:1], rstd[:, 1, t:t + 1],
                                        ALU.subtract, ALU.mult)
                i.then_inc(s["y_ready"], 1)
                for t in range(TT):
                    v.tensor_scalar(y_all[:, a * TT + t, :], x_all[:, a * TT + t, :], mv[:, t, 0:1],
                                    rstd[:, 1, t:t + 1], ALU.subtract, ALU.mult)
                v.tensor_scalar(lin[:, 0, :], rstd[:, 0, :], 0.5, 1.0, ALU.mult, ALU.add)
                v.scalar_tensor_tensor(lin[:, 1, :], mv[:, :, 0], -0.5, rstd[:, 0, :], ALU.mult,
                                       ALU.mult).then_inc(s["chain"], 1)
                dve.wait_ge(s["chain"], a * A_CHAIN + 3)
                for t in range(TT):
                    i = v.tensor_scalar(x_all[:, a * TT + t, :], x_all[:, a * TT + t, :], lin[:, 0, t:t + 1],
                                        lin[:, 1, t:t + 1], ALU.mult, ALU.add)
                i.then_inc(s["base_ready"], 1)

            def logits_of(a):
                dve.wait_ge(s["logits_done"], a + 1)
                v.tensor_copy(logits[:, bass.ds(a * TT, TT), :],
                              m.side[0][:, 0:TT * NG].rearrange("p (t g) -> p t g", g=NG)).then_inc(s["chain"], 1)
                dve.wait_ge(s["chain"], a * A_CHAIN + 4)
                v.tensor_tensor(dif[:], logits[:, bass.ds(a * TT, TT), NE], logits[:, bass.ds(a * TT, TT), NE + 1],
                                ALU.subtract).then_inc(s["dif_ready"], 1)

            def mix_of(a):
                dve.wait_ge(s["th_ready"], a + 1)
                v.tensor_scalar(c0[:, bass.ds(a * TT, TT)], th[:], 0.25, 0.25, ALU.mult, ALU.add)
                v.tensor_scalar(c1[:, bass.ds(a * TT, TT)], th[:], -0.25, 0.25, ALU.mult, ALU.add).then_inc(s["mixed"], 1)

            def empty(c):
                dve.wait_ge(m.down_done, c * NK + NK)
                for t in range(TT):
                    i = v.tensor_tensor(part[:, t, :], m.down_ps[t][:, 0:D], b2[:], ALU.add)
                i.then_inc(m.evacuated, 1)
                dve.wait_ge(m.evacuated, c + 1)
                for t in range(TT):
                    i = v.scalar_tensor_tensor(x_all[:, c * TT + t, :], part[:, t, :], c0[:, bass.ds(c * TT + t, 1)],
                                               x_all[:, c * TT + t, :], ALU.mult, ALU.add)
                i.then_inc(s["empty_chain"], 1)

            def mlp(c, first=False, beside=None):
                m.split_x(dve, c, aT_all[:, :, bass.ds(c * CH, CH)])
                for k in range(NK):
                    m.split_h(dve, c, k, first)
                    for f in (beside or {}).get(k, ()):
                        f()
                empty(c)

            def norm_beside(a):
                return {0: [lambda: stats_of(a)], 1: [lambda: rows_of(a)], 3: [lambda: logits_of(a)],
                        4: [lambda: mix_of(a), lambda: stats_of(a + 1)], 5: [lambda: rows_of(a + 1)],
                        7: [lambda: logits_of(a + 1), lambda: mix_of(a + 1)]}

            stats_of(0)
            dve.wait_ge(s["w_in"], 48)
            v.tensor_copy(w1[0][:], raw1)
            v.tensor_copy(w2[0][:], raw2).then_inc(s["w_hid"], 1)
            rows_of(0)
            dve.wait_ge(s["w_hid"], 1)
            v.tensor_tensor(w1[1][:], raw1, w1[0][:], ALU.subtract)
            v.tensor_tensor(w2[1][:], raw2, w2[0][:], ALU.subtract).then_inc(s["w_split"], 1)
            logits_of(0)
            stats_of(1)
            mix_of(0)
            rows_of(1)
            logits_of(1)
            mix_of(1)
            for c in range(2, 4) if x_in else ():
                dve.wait_ge(x_in[c], 16)
            dve.wait_ge(s["aT_ready"], 1)
            mlp(0, True, norm_beside(2))
            for c in range(4, NC) if x_in else ():
                dve.wait_ge(x_in[c], 16)
            with dve.Fori(1, 3) as c:
                dve.wait_ge(s["aT_ready"], c + 1)
                mlp(c, False, norm_beside(c * 2 + 2))

            chain = [0]

            def link(i):
                chain[0] += 1
                i.then_inc(s["gate"], 1)
                dve.wait_ge(s["gate"], chain[0])

            def bc_e(ap):
                return ap.unsqueeze(2).to_broadcast([P, NT, NE])

            rank = mem["rank"][:].unsqueeze(1).to_broadcast([P, NT, NE])
            gates = logits[:, :, 0:NE]

            def choose():
                link(v.tensor_reduce(top[:], gates, AX, ALU.max))
                v.tensor_tensor(lm[:], gates, bc_e(top[:]), ALU.subtract).then_inc(s["lm_ready"], 1)
                link(v.tensor_tensor(eq[:], gates, bc_e(top[:]), ALU.is_equal))
                link(v.tensor_tensor(eq[:], eq[:], rank, ALU.mult))
                link(v.tensor_reduce(best[:], eq[:], AX, ALU.max))
                link(v.tensor_tensor(hot[:], rank, bc_e(best[:]), ALU.is_equal))
                v.tensor_copy(hot16[:], hot[:]).then_inc(s["hot_ready"], 1)
                link(v.tensor_scalar(base[:], best[:], float(-CAP), float(NE * CAP), ALU.mult, ALU.add))

            def place():
                dve.wait_ge(s["counted"], 1)
                before = m.side[0][:, 0:NE * NT].rearrange("p (e t) -> p e t", e=NE)
                total = m.side[1][:, 0:NE * NT].rearrange("p (e t) -> p e t", e=NE)
                flat = "p e t -> p (e t)"
                link(v.tensor_tensor_scan(incl[:].rearrange(flat), mem["same_expert"][:].rearrange(flat),
                                          m.side[1][:, 0:NE * NT], 0.0, ALU.mult, ALU.add))
                link(v.tensor_tensor(locs[:], incl[:], total, ALU.subtract))
                link(v.tensor_tensor(locs[:], locs[:], before, ALU.add))
                link(v.tensor_tensor(eq[:], locs[:].rearrange("p e t -> p t e"), hot[:], ALU.mult))
                link(v.tensor_reduce(loc[:], eq[:], AX, ALU.add))

            def address():
                link(v.tensor_scalar(keep[:], loc[:], float(CAP), None, ALU.is_lt))
                link(v.tensor_tensor(t0[:], loc[:], keep[:], ALU.mult))
                link(v.tensor_tensor(t0[:], t0[:], base[:], ALU.add))
                v.tensor_copy(mem["gather_at"][:], t0[:])
                link(v.tensor_tensor(t1[:], loc[:], base[:], ALU.add))
                link(v.tensor_tensor(t1[:], t1[:], mem["trash"][:], ALU.subtract))
                link(v.tensor_tensor(t1[:], t1[:], keep[:], ALU.mult))
                link(v.tensor_tensor(t1[:], t1[:], mem["trash"][:], ALU.add))
                v.tensor_copy(scatter_at[:], t1[:]).then_inc(s["scatter_ready"], 1)

            def weigh():
                dve.wait_ge(s["ex_ready"], 1)
                link(v.tensor_reduce(t0[:], ex[:], AX, ALU.add))
                link(v.reciprocal(rec[:], t0[:]))
                link(v.tensor_tensor(rec[:], rec[:], keep[:], ALU.mult))
                link(v.tensor_tensor(mem["moe_w"][:], rec[:], c1[:], ALU.mult))

            dve.wait_ge(s["aT_ready"], 4)
            dve.wait_ge(s["mixed"], NC)
            mlp(3, False, {0: [choose], 2: [place], 3: [address], 5: [weigh]})
            with dve.Fori(4, NC) as c:
                mlp(c)

        @block.scalar
        def _(act):
            def aT_of(a):
                act.wait_ge(s["turned"], a + 1)
                if not (isinstance(a, int) and a == 0):
                    act.wait_ge(s["logits_done"], a)
                for kd in range(KD):
                    nc.scalar.activation(aT[:, kd, :], m.side[kd][:], ACT.Identity, bias=shift[kd], scale=gain[kd])
                    i = nc.scalar.activation(aT_all[:, kd, bass.ds(a * CH, CH)], m.side[kd][:], ACT.Identity,
                                             bias=shift[kd], scale=gain[kd])
                i.then_inc(s["aT_ready"], 1)

            def th_of(a):
                act.wait_ge(s["dif_ready"], a + 1)
                nc.scalar.activation(th[:], dif[:], ACT.Tanh, scale=0.5).then_inc(s["th_ready"], 1)

            def mlp(c, first=False, beside=None):
                for k in range(NK):
                    m.gelu(act, c, k, b1[k], first)
                    for f in (beside or {}).get(k, ()):
                        f()

            def norm_beside(a):
                return {2: [lambda: aT_of(a)], 4: [lambda: th_of(a)], 6: [lambda: aT_of(a + 1)],
                        7: [lambda: th_of(a + 1)]}

            def ex_all():
                act.wait_ge(s["lm_ready"], 1)
                nc.scalar.activation(ex[:], lm[:], ACT.Exp).then_inc(s["ex_ready"], 1)

            aT_of(0)
            th_of(0)
            aT_of(1)
            th_of(1)
            mlp(0, True, norm_beside(2))
            with act.Fori(1, 3) as c:
                mlp(c, False, norm_beside(c * 2 + 2))
            mlp(3, False, {2: [ex_all]})
            with act.Fori(4, NC) as c:
                mlp(c)

        @block.tensor
        def _(pe):
            def turn(a):
                pe.wait_ge(s["y_ready"], a + 1)
                if not (isinstance(a, int) and a == 0):
                    pe.wait_ge(s["aT_ready"], a)
                    pe.wait_ge(s["dif_ready"], a)
                for kd in range(KD):
                    for t in range(TT):
                        i = nc.tensor.transpose(m.side[kd][:, t * P:(t + 1) * P], y[:, t, kd * P:(kd + 1) * P],
                                                mem["id32"][:])
                i.then_inc(s["turned"], 1)

            def route(a):
                pe.wait_ge(s["aT_ready"], a + 1)
                for t in range(TT):
                    for kd in range(KD):
                        i = nc.tensor.matmul(m.side[0][:, t * NG:(t + 1) * NG], aT[:, kd, t * P:(t + 1) * P],
                                             wgc[:, kd, :], start=(kd == 0), stop=(kd == KD - 1))
                i.then_inc(s["logits_done"], 1)

            def count():
                pe.wait_ge(s["hot_ready"], 1)
                hot_et = hot16[:].rearrange("p t e -> p e t")
                nc.tensor.matmul(m.side[0][:, 0:NE * NT].rearrange("p (e t) -> p e t", e=NE), mem["before16"][:],
                                 hot_et, start=True, stop=True)
                nc.tensor.matmul(m.side[1][:, 0:NE * NT].rearrange("p (e t) -> p e t", e=NE), mem["ones16"][:],
                                 hot_et, start=True, stop=True).then_inc(s["counted"], 1)

            def weights(pe, k, is_up):
                n = slice(k * P, (k + 1) * P)
                return (lambda kd: w1[0][:, kd, n]), (lambda kd: w1[1][:, kd, n]), w2[0][:, k, :], w2[1][:, k, :]

            def norm_beside(a):
                return {1: lambda: turn(a), 3: lambda: route(a), 5: lambda: turn(a + 1),
                        6: lambda: route(a + 1)}

            turn(0)
            route(0)
            turn(1)
            route(1)
            pe.wait_ge(s["w_split"], 1)
            m.tensor_chunk(pe, 0, weights, True, norm_beside(2))
            with pe.Fori(1, 3) as c:
                m.tensor_chunk(pe, c, weights, False, norm_beside(c * 2 + 2))
            m.tensor_chunk(pe, 3, weights, False, {0: count})
            with pe.Fori(4, NC) as c:
                m.tensor_chunk(pe, c, weights)


W_RING, W_AHEAD = 4, 3


def expert_block(nc, mem, layer, inter_w, output_w, output_b, slots_in, slots_out):
    tag = f"e{layer}"
    vecT = mem["vecT"]
    HALF = NK // 2
    with ExitStack() as ctx:
        def sb(name, shape, dt=F32):
            return ctx.enter_context(nc.sbuf_tensor(f"{tag}_{name}", shape, dt))

        m = Mlp(nc, ctx, tag)
        rows = sb("rows", [P, TT, D])
        aT = sb("aT", [P, KD, CH])
        raw1 = sb("raw1", [P, 2, KD, HALF * P])
        raw2 = sb("raw2", [P, 2, HALF, D])
        w1 = [sb(f"w1_{n}", [P, W_RING, KD, P], F32R) for n in ("hi", "lo")]
        w2 = [sb(f"w2_{n}", [P, W_RING, D], F32R) for n in ("hi", "lo")]
        b2 = sb("b2", [P, NE, D])
        done = sb("done", [P, TT, D])
        s = split_sems(ctx, nc, tag, "b_in rows_in turned aT_ready w_hid w_split stored")
        w_in = [ctx.enter_context(nc.semaphore(f"{tag}_w_in{i}")) for i in range(2)]
        NB = NE * NK + NK
        gain = [vecT[:, NB + k:NB + k + 1] for k in range(KD)]
        shift = [vecT[:, NB + KD + k:NB + KD + k + 1] for k in range(KD)]
        in_rows = slots_in.rearrange("(c t p) d -> c p t d", t=TT, p=P)
        out_rows = slots_out.rearrange("(c t p) d -> c p t d", t=TT, p=P)
        w1_rows = inter_w.rearrange("e (k p) n -> e p k n", p=P)
        w2_rows = output_w.rearrange("e (k p) n -> e p k n", p=P)
        block = ctx.enter_context(nc.Block())

        @block.sync
        def _(sp):
            def load_half(e, half, first):
                if not first:
                    sp.wait_ge(s["w_split"], (e - 1) * NK + (half + 1) * HALF)
                sp.dma_start(raw1[:, half, :, :], w1_rows[e, :, :, half * HALF * P:(half + 1) * HALF * P]).then_inc(w_in[half], 16)
                sp.dma_start(raw2[:, half, :, :], w2_rows[e, :, half * HALF:(half + 1) * HALF, :]).then_inc(w_in[half], 16)

            def load_rows(e, first):
                if not first:
                    sp.wait_ge(s["turned"], e)
                sp.dma_start(rows[:], in_rows[e]).then_inc(s["rows_in"], 16)

            load_rows(0, True)
            load_half(0, 0, True)
            load_half(0, 1, True)
            sp.dma_start(b2[:], output_b.rearrange("(a e) n -> a e n", a=1).to_broadcast([P, NE, D])).then_inc(s["b_in"], 16)
            with sp.Fori(1, NE) as e:
                load_rows(e, False)
                load_half(e, 0, False)
                load_half(e, 1, False)

        @block.gpsimd
        def _(pool):
            with pool.Fori(0, NE) as e:
                pool.wait_ge(m.evacuated, e + 1)
                nc.gpsimd.dma_start(out_rows[e], done[:]).then_inc(s["stored"], 16)
            pool.wait_ge(s["stored"], 16 * NE)

        @block.vector
        def _(dve):
            v = nc.vector

            def split_w(e, k):
                n = e * NK + k
                k, e = k % NK, e + k // NK
                r, half, q = k % W_RING, k // HALF, k % HALF
                if k % HALF == 0:
                    dve.wait_ge(w_in[half], (e + 1) * 32)
                a1, a2 = raw1[:, half, :, q * P:(q + 1) * P], raw2[:, half, q, :]
                v.tensor_copy(w1[0][:, r, :, :], a1)
                v.tensor_copy(w2[0][:, r, :], a2).then_inc(s["w_hid"], 1)
                dve.wait_ge(s["w_hid"], n + 1)
                v.tensor_tensor(w1[1][:, r, :, :], a1, w1[0][:, r, :, :], ALU.subtract)
                v.tensor_tensor(w2[1][:, r, :], a2, w2[0][:, r, :], ALU.subtract).then_inc(s["w_split"], 1)

            def expert(e, first=False, last=False):
                dve.wait_ge(s["aT_ready"], e + 1)
                m.split_x(dve, e, aT[:])
                for k in range(NK):
                    m.split_h(dve, e, k, first)
                    if not (last and k + W_AHEAD >= NK):
                        if not (first and k + W_AHEAD < W_RING):
                            dve.wait_ge(m.down_done, e * NK + (k + W_AHEAD - W_RING + 1))
                        split_w(e, k + W_AHEAD)
                dve.wait_ge(m.down_done, e * NK + NK)
                if first:
                    dve.wait_ge(s["b_in"], 16)
                else:
                    dve.wait_ge(s["stored"], e * 16)
                for t in range(TT):
                    i = v.tensor_tensor(done[:, t, :], m.down_ps[t][:, 0:D], b2[:, e, :], ALU.add)
                i.then_inc(m.evacuated, 1)

            for k in range(W_AHEAD):
                split_w(0, k)
            expert(0, first=True)
            with dve.Fori(1, NE - 1) as e:
                expert(e)
            expert(NE - 1, last=True)

        @block.scalar
        def _(act):
            def aT_of(e, first=False):
                act.wait_ge(s["turned"], e + 1)
                if not first:
                    act.wait_ge(m.x_split, e)
                for kd in range(KD):
                    i = nc.scalar.activation(aT[:, kd, :], m.side[kd][:], ACT.Identity, bias=shift[kd], scale=gain[kd])
                i.then_inc(s["aT_ready"], 1)

            def expert(e, first=False, last=False):
                for k in range(NK):
                    m.gelu(act, e, k, vecT[:, bass.ds(e * NK + k, 1)], first)
                    if k == 4 and not last:
                        aT_of(e + 1)

            aT_of(0, True)
            expert(0, first=True)
            with act.Fori(1, NE - 1) as e:
                expert(e)
            expert(NE - 1, last=True)

        @block.tensor
        def _(pe):
            def turn(e, first=False):
                pe.wait_ge(s["rows_in"], (e + 1) * 16)
                if not first:
                    pe.wait_ge(s["aT_ready"], e)
                for kd in range(KD):
                    for t in range(TT):
                        i = nc.tensor.transpose(m.side[kd][:, t * P:(t + 1) * P], rows[:, t, kd * P:(kd + 1) * P],
                                                mem["id32"][:])
                i.then_inc(s["turned"], 1)

            def expert(e, first=False, last=False):
                def weights(pe, k, is_up):
                    r = k % W_RING
                    if is_up:
                        pe.wait_ge(s["w_split"], e * NK + (k + 1))
                    return (lambda kd: w1[0][:, r, kd, :]), (lambda kd: w1[1][:, r, kd, :]), w2[0][:, r, :], w2[1][:, r, :]
                m.tensor_chunk(pe, e, weights, first, None if last else {2: lambda: turn(e + 1)})

            turn(0, True)
            expert(0, first=True)
            with pe.Fori(1, NE - 1) as e:
                expert(e)
            expert(NE - 1, last=True)


NP2 = HG // 2
PAIRS = [(c, g, j, hp) for c in range(QC) for g in range(H // HG) for j in range(TT * (c + 1)) for hp in range(NP2)]
P_RING = 4
NPROJ = D + H * DEPTH


def combine_rows(nc, mem, dve, moe, gathered, combined, n, c):
    half = c % 2
    dve.wait_ge(gathered[half], (n - half) * 32 + 64)
    for t in range(TT):
        i = nc.vector.scalar_tensor_tensor(mem["x_all"][:, n * TT + t, :], moe[:, half, t, :],
                                           mem["moe_w"][:, bass.ds(n * TT + t, 1)], mem["x_all"][:, n * TT + t, :],
                                           ALU.mult, ALU.add)
    i.then_inc(combined, 1)


def gather_rows(nc, mem, pool, moe, gathered, combined, slots_out, n):
    if n >= 2:
        pool.wait_ge(combined, n - 1)
    for t in range(TT):
        at = n * TT + t
        nc.gpsimd.indirect_dma_start(
            out=moe[:, n % 2, t, :], out_offset=None, in_=slots_out,
            in_offset=bass.IndirectOffsetOnAxis(ap=mem["gather_at"][:, at:at + 1], axis=0)).then_inc(gathered[n % 2], 16)


def attention_block(nc, mem, Wp, bp, Wv, Wo, slots_out):
    x_all = mem["x_all"]
    with ExitStack() as ctx:
        def sb(name, shape, dt=F32):
            return ctx.enter_context(nc.sbuf_tensor(f"a_{name}", shape, dt))

        def ps(name, shape):
            return ctx.enter_context(nc.psum_tensor(f"a_{name}", shape, F32))

        KT = sb("KT", [P, H, SEQ], F16)
        QT = sb("QT", [P, 2, H, CH], F16)
        V = sb("V", [P, SEQ // P, D])
        probs = sb("probs", [P, P_RING, 2, CH])
        wvp, wo = sb("wvp", [P, KD, NPROJ]), sb("wo", [P, KD, D])
        bpb = sb("bpb", [P, H * DEPTH])
        moe = sb("moe", [P, 2, TT, D])
        idle = sb("idle", [P, 1])
        stats, mv = sb("stats", [P, TT, 6]), sb("mv", [P, TT, 2])
        var, rstd = sb("var", [P, TT]), sb("rstd", [P, TT])
        y, yT = sb("y", [P, TT, D]), sb("yT", [P, KD, CH])
        z, th = sb("z", [P, TT, H * DEPTH]), sb("th", [P, TT, H * DEPTH])
        mono, coef = sb("mono", [P, TT * H, NF]), sb("coef", [P, NF])
        feat, hl = sb("feat", [P, TT * H, NF]), sb("hl", [P, TT * H, 2, NF], F16)
        Kf, Qf = sb("Kf", [P, TT * H, 4 * NF], F16), sb("Qf", [P, TT * H, 4 * NF], F16)
        cc, dd, rr = (sb(n, [P, H // HG, CH]) for n in ("cc", "dd", "rr"))
        ctxn = sb("ctxn", [P, H // HG, CH])
        S = [ps(f"S{i}", [P, 2, CH]) for i in range(2)]
        cx = [ps(f"cx{i}", [P, CH]) for i in range(2)]
        misc = [ps(f"misc{i}", [P, CH]) for i in range(2)]

        s = split_sems(ctx, nc, "a", "w_in chain combined var_ready rstd_ready y_ready turned yT_ready proj_done "
                       "proj_read th_ready f_ready fT_done feat_read s_done exp_done pv_done cx_free "
                       "norm_chain ctx_ready wo_done added coef_ready f_ready_chain")
        gathered = [ctx.enter_context(nc.semaphore(f"a_gathered{i}")) for i in range(2)]
        block = ctx.enter_context(nc.Block())
        NPAIR = len(PAIRS)

        def first_pair(c):
            return next(i for i, q in enumerate(PAIRS) if q[0] == c)

        def beside(c):
            n = 4 * TT * (c + 1)
            at = {}
            if c:
                at[5] = ("wo",)
            if c + 1 < QC:
                at[1 if c == 0 else 7] = ("turn",)
                at[3 if c == 0 else 9] = ("proj",)
                for h in range(H):
                    at[n // 2 - 1 + h] = ("feat", h)
            return at

        @block.sync
        def _(sp):
            sp.dma_start(wvp[:, :, 0:D], Wv.rearrange("(k p) n -> p k n", p=P)).then_inc(s["w_in"], 16)
            sp.dma_start(wvp[:, :, D:NPROJ], Wp.rearrange("(k p) n -> p k n", p=P)).then_inc(s["w_in"], 16)
            sp.dma_start(wo[:], Wo.rearrange("(k p) n -> p k n", p=P)).then_inc(s["w_in"], 16)
            sp.dma_start(bpb[:], whole(bp, P)).then_inc(s["w_in"], 16)
            sp.wait_ge(s["w_in"], 64)

        @block.gpsimd
        def _(pool):
            gather_rows(nc, mem, pool, moe, gathered, s["combined"], slots_out, 0)
            gather_rows(nc, mem, pool, moe, gathered, s["combined"], slots_out, 1)
            nc.gpsimd.memset(coef[:, 0:1], sqrt(subset_coefficient(0)))
            for m in range(1, DEPTH + 1):
                i = nc.gpsimd.memset(coef[:, 2 ** (m - 1):2 ** m], sqrt(subset_coefficient(m)))
            nc.gpsimd.memset(mono[:, :, 0:1], 1.0).then_inc(s["coef_ready"], 1)
            for n in range(NC):
                pool.wait_ge(s["var_ready"], n + 1)
                nc.gpsimd.tensor_tensor(rstd[:], var[:], mem["minus_half"][:, 0:TT], ALU.pow).then_inc(s["rstd_ready"], 1)
                if n + 2 < NC:
                    gather_rows(nc, mem, pool, moe, gathered, s["combined"], slots_out, n + 2)

        @block.tensor
        def _(pe):
            def turn(b, c):
                n = b * QC + c
                pe.wait_ge(s["y_ready"], n + 1)
                if c == 1:
                    pe.wait_ge(s["feat_read"], n * H)
                if c >= 2:
                    pe.wait_ge(s["added"], n - 1)
                for kd in range(KD):
                    for t in range(TT):
                        i = nc.tensor.transpose(misc[kd][:, t * P:(t + 1) * P], y[:, t, kd * P:(kd + 1) * P],
                                                mem["id32"][:])
                i.then_inc(s["turned"], 1)

            def project(b, c):
                n = b * QC + c
                pe.wait_ge(s["yT_ready"], n + 1)
                if c == 0:
                    pe.wait_ge(s["w_in"], 64)
                for t in range(TT):
                    if t >= 2:
                        pe.wait_ge(s["proj_read"], n * TT + (t - 1))
                    for kd in range(KD):
                        i = nc.tensor.matmul(misc[t % 2][:, 0:NPROJ], yT[:, kd, t * P:(t + 1) * P], wvp[:, kd, :],
                                             start=(kd == 0), stop=(kd == KD - 1))
                    i.then_inc(s["proj_done"], 1)

            def turn_features(b, c, h):
                n = b * QC + c
                if h == 0:
                    pe.wait_ge(s["f_ready"], n + 1)
                if h < 2:
                    pe.wait_ge(s["proj_read"], n * TT + (3 + h))
                else:
                    pe.wait_ge(s["feat_read"], n * H + (h - 1))
                bank = misc[h % 2][:].bitcast(F16)
                for side, f in enumerate((Kf, Qf)):
                    for t in range(TT):
                        at = side * CH + t * P
                        i = nc.tensor.transpose(bank[:, at:at + P], f[:, t * H + h, :], mem["id16"][:])
                i.then_inc(s["fT_done"], 1)

            def output(b, c):
                n = b * QC + c
                pe.wait_ge(s["ctx_ready"], (n + 1) * 2)
                pe.wait_ge(s["feat_read"], (b * QC + min(c + 2, QC)) * H)
                for t in range(TT):
                    for g in range(H // HG):
                        i = nc.tensor.matmul(misc[t // 2][:, (t % 2) * D:(t % 2 + 1) * D], ctxn[:, g, t * P:(t + 1) * P],
                                             wo[:, g, :], start=(g == 0), stop=(g == H // HG - 1))
                i.then_inc(s["wo_done"], 1)

            def scores(b, p):
                c, g, j, hp = PAIRS[p]
                lo = max(j - TT * c, 0) * P
                if p == first_pair(c):
                    pe.wait_ge(s["feat_read"], (b * QC + c + 1) * H)
                if p >= 2:
                    pe.wait_ge(s["exp_done"], b * NPAIR + (p - 1))
                for i in range(2):
                    h = g * HG + hp * 2 + i
                    out = S[p % 2][:, i, :]
                    diag = j >= TT * c
                    last = nc.tensor.matmul(out[:, lo:CH], KT[:, h, j * P:(j + 1) * P], QT[:, c % 2, h, lo:CH],
                                            start=True, stop=not diag)
                    if diag:
                        last = nc.tensor.matmul(out[:, lo:lo + P], mem["id16"][:], mem["mask16"][:], start=False, stop=True)
                last.then_inc(s["s_done"], 1)

            def contexts(b, p):
                c, g, j, hp = PAIRS[p]
                lo = max(j - TT * c, 0) * P
                pe.wait_ge(s["exp_done"], b * NPAIR + (p + 1))
                if j == 0 and hp == 0 and (c, g) != (0, 0):
                    pe.wait_ge(s["cx_free"], (b * QC + c) * 2 + g)
                flags = dict(start=(j == 0), stop=(j == TT * (c + 1) - 1))
                for what in range(2):
                    for i in range(2):
                        h = g * HG + hp * 2 + i
                        q = 32 * (i + 2 * (what ^ hp))
                        w = mem["ones32"][:] if what else V[:, j, h * DH:(h + 1) * DH]
                        last = nc.tensor.matmul(cx[hp][q:q + DH, lo:CH], w, probs[:, p % P_RING, i, lo:CH], **flags)
                last.then_inc(s["pv_done"], 1)

            with pe.Fori(0, BATCH) as b:
                turn(b, 0)
                project(b, 0)
                for h in range(H):
                    turn_features(b, 0, h)
                for c in range(QC):
                    at, p0 = beside(c), first_pair(c)
                    n = 4 * TT * (c + 1)
                    scores(b, p0)
                    for p in range(p0, p0 + n):
                        if p + 1 < p0 + n:
                            scores(b, p + 1)
                        contexts(b, p)
                        what = at.get(p - p0)
                        if what == ("wo",):
                            output(b, c - 1)
                        elif what == ("turn",):
                            turn(b, c + 1)
                        elif what == ("proj",):
                            project(b, c + 1)
                        elif what:
                            turn_features(b, c + 1, what[1])
                output(b, QC - 1)

        @block.scalar
        def _(act):
            def yT_of(b, c):
                act.wait_ge(s["turned"], b * QC + (c + 1))
                for kd in range(KD):
                    i = nc.scalar.copy(yT[:, kd, :], misc[kd][:])
                i.then_inc(s["yT_ready"], 1)

            def th_of(b, c):
                act.wait_ge(s["proj_read"], (b * QC + (c + 1)) * TT)
                nc.scalar.activation(th[:], z[:], ACT.Tanh, scale=0.5).then_inc(s["th_ready"], 1)

            def exps(b, p):
                c, g, j, hp = PAIRS[p]
                lo = max(j - TT * c, 0) * P
                act.wait_ge(s["s_done"], b * NPAIR + (p + 1))
                if p >= P_RING:
                    act.wait_ge(s["pv_done"], b * NPAIR + (p - P_RING + 1))
                nc.scalar.activation(probs[:, p % P_RING, :, lo:CH], S[p % 2][:, :, lo:CH], ACT.Exp).then_inc(s["exp_done"], 1)

            with act.Fori(0, BATCH) as b:
                yT_of(b, 0)
                th_of(b, 0)
                for c in range(QC):
                    at, p0 = beside(c), first_pair(c)
                    at = {k: v[0] for k, v in at.items()}
                    for k in range(4 * TT * (c + 1)):
                        exps(b, p0 + k)
                        if at.get(k - 1) == "turn":
                            yT_of(b, c + 1)
                        if at.get(k - 2) == "proj":
                            th_of(b, c + 1)

        @block.vector
        def _(dve):
            v = nc.vector
            CHAIN, FCHAIN = 2, DEPTH + 3

            def rows_of(b, c):
                n = b * QC + c
                combine_rows(nc, mem, dve, moe, gathered, s["combined"], n, c)
                wait_carried(nc, dve, idle[:], s["combined"], n + 1)
                for t in range(TT):
                    i = v.bn_stats(stats[:, t, :], x_all[:, n * TT + t, :])
                i.then_inc(s["chain"], 1)
                wait_carried(nc, dve, idle[:], s["chain"], n * CHAIN + 1)
                for t in range(TT):
                    i = v.bn_aggr(mv[:, t, :], stats[:, t, :])
                i.then_inc(s["chain"], 1)
                dve.wait_ge(s["chain"], n * CHAIN + 2)
                v.tensor_scalar(var[:], mv[:, :, 1], LN_EPS, None, ALU.add).then_inc(s["var_ready"], 1)
                dve.wait_ge(s["rstd_ready"], n + 1)
                if c:
                    dve.wait_ge(s["turned"], n)
                for t in range(TT):
                    i = v.tensor_scalar(y[:, t, :], x_all[:, n * TT + t, :], mv[:, t, 0:1], rstd[:, t:t + 1],
                                        ALU.subtract, ALU.mult)
                i.then_inc(s["y_ready"], 1)

            def read_projection(b, c):
                n = b * QC + c
                if c == 0:
                    dve.wait_ge(s["w_in"], 64)
                for t in range(TT):
                    dve.wait_ge(s["proj_done"], n * TT + (t + 1))
                    v.tensor_copy(V[:, TT * c + t, :], misc[t % 2][:, 0:D])
                    v.tensor_tensor(z[:, t, :], misc[t % 2][:, D:NPROJ], bpb[:], ALU.add).then_inc(s["proj_read"], 1)

            def features(b, c):
                n = b * QC + c
                dve.wait_ge(s["th_ready"], n + 1)
                if c == 0:
                    dve.wait_ge(s["coef_ready"], 1)
                k = [0]

                def link(i):
                    k[0] += 1
                    i.then_inc(s["f_ready_chain"], 1)
                    dve.wait_ge(s["f_ready_chain"], n * FCHAIN + k[0])

                thv = th[:].rearrange("p t (h d) -> p (t h) d", d=DEPTH)
                for d in range(DEPTH):
                    w = 2 ** d
                    link(v.tensor_tensor(mono[:, :, w:2 * w], mono[:, :, 0:w],
                                         thv[:, :, d:d + 1].to_broadcast([P, TT * H, w]), ALU.mult))
                link(v.tensor_tensor(feat[:], mono[:], coef[:].unsqueeze(1).to_broadcast([P, TT * H, NF]), ALU.mult))
                link(v.tensor_copy(hl[:, :, 0, :], feat[:]))
                link(v.tensor_tensor(hl[:, :, 1, :], feat[:], hl[:, :, 0, :], ALU.subtract))
                assert k[0] == FCHAIN
                both = hl[:].rearrange("p n a f -> p n (a f)").unsqueeze(2).to_broadcast([P, TT * H, 2, 2 * NF])
                v.tensor_copy(Kf[:].rearrange("p n (r f) -> p n r f", r=2), both)
                for a in range(2):
                    i = v.tensor_copy(Qf[:].rearrange("p n (a r f) -> p n a r f", a=2, r=2)[:, :, a],
                                      hl[:, :, a, :].unsqueeze(2).to_broadcast([P, TT * H, 2, NF]))
                i.then_inc(s["f_ready"], 1)

            def read_features(b, c, h):
                dve.wait_ge(s["fT_done"], (b * QC + c) * H + (h + 1))
                bank = misc[h % 2][:].bitcast(F16)
                v.tensor_copy(KT[:, h, c * CH:(c + 1) * CH], bank[:, 0:CH])
                v.tensor_copy(QT[:, c % 2, h, :], bank[:, CH:2 * CH]).then_inc(s["feat_read"], 1)

            def read_contexts(b, c, g):
                n = (b * QC + c) * 2 + g
                last = max(i for i, q in enumerate(PAIRS) if q[:2] == (c, g))
                dve.wait_ge(s["pv_done"], b * NPAIR + (last + 1))
                h = P // 2
                v.tensor_copy(dd[0:h, g, :], cx[0][h:P, :])
                v.tensor_copy(dd[h:P, g, :], cx[1][0:h, :])
                v.tensor_copy(cc[0:h, g, :], cx[0][0:h, :])
                v.tensor_copy(cc[h:P, g, :], cx[1][h:P, :]).then_inc(s["cx_free"], 1)

            def divide(b, c, g):
                n = (b * QC + c) * 2 + g
                dve.wait_ge(s["cx_free"], n + 1)
                v.reciprocal(rr[:, g, :], dd[:, g, :]).then_inc(s["norm_chain"], 1)
                dve.wait_ge(s["norm_chain"], n + 1)
                v.tensor_tensor(ctxn[:, g, :], cc[:, g, :], rr[:, g, :], ALU.mult).then_inc(s["ctx_ready"], 1)

            def add_output(b, c):
                n = b * QC + c
                dve.wait_ge(s["wo_done"], n + 1)
                for i in range(2):
                    rows = x_all[:, bass.ds(n * TT + 2 * i, 2), :]
                    last = v.tensor_tensor(rows, rows, misc[i][:].rearrange("p (t d) -> p t d", d=D), ALU.add)
                last.then_inc(s["added"], 1)

            with dve.Fori(0, BATCH) as b:
                rows_of(b, 0)
                read_projection(b, 0)
                features(b, 0)
                for h in range(H):
                    read_features(b, 0, h)
                for c in range(QC):
                    more = c + 1 < QC
                    if more:
                        rows_of(b, c + 1)
                    if c:
                        add_output(b, c - 1)
                    if more:
                        read_projection(b, c + 1)
                        features(b, c + 1)
                    read_contexts(b, c, 0)
                    if more:
                        for h in range(H):
                            read_features(b, c + 1, h)
                    divide(b, c, 0)
                    read_contexts(b, c, 1)
                    divide(b, c, 1)
                add_output(b, QC - 1)


def last_block(nc, mem, slots_out, out_tiles):
    with ExitStack() as ctx:
        moe = ctx.enter_context(nc.sbuf_tensor("l_moe", [P, 2, TT, D], F32))
        gathered = [ctx.enter_context(nc.semaphore(f"l_gathered{i}")) for i in range(2)]
        combined = ctx.enter_context(nc.semaphore("l_combined"))
        stored = ctx.enter_context(nc.semaphore("l_stored"))
        block = ctx.enter_context(nc.Block())

        @block.gpsimd
        def _(pool):
            for n in range(NC):
                gather_rows(nc, mem, pool, moe, gathered, combined, slots_out, n)

        @block.vector
        def _(dve):
            for n in range(NC):
                combine_rows(nc, mem, dve, moe, gathered, combined, n, n)

        @block.sync
        def _(sp):
            for n in range(NC):
                sp.wait_ge(combined, n + 1)
                rows = slice(n * TT, (n + 1) * TT)
                sp.dma_start(out_tiles[:, rows, :], mem["x_all"][:, rows, :]).then_inc(stored, 16)
            sp.wait_ge(stored, 16 * NC)


_INS = ["L0_attn_x", "L0_attn_Wp", "L0_attn_bp", "L0_attn_Wv", "L0_attn_Wo", "L0_ffn_attn_nw", "L0_ffn_attn_nb",
        "L0_ffn_wg", "L0_ffn_inter_w", "L0_ffn_inter_b", "L0_ffn_output_w", "L0_ffn_output_b",
        "L0_ffn_res_inter_w", "L0_ffn_res_inter_b", "L0_ffn_res_output_w", "L0_ffn_res_output_b", "L0_ffn_res_coef"]


def kernel(**inputs):
    import numpy as _np
    import concourse.bacc as _bacc
    from concourse import mybir as _mybir
    from concourse.bass_utils import run_bass_kernel_spmd as _run

    nc = _bacc.Bacc("TRN2", target_bir_lowering=False, num_devices=1)
    arrays, args = {}, []
    for name in _INS:
        a = _np.ascontiguousarray(inputs[name])
        arrays[f"in_{name}"] = a
        args.append(nc.dram_tensor(f"in_{name}", a.shape, _mybir.dt.from_np(a.dtype), kind="ExternalInput").ap())
    args.append(nc.dram_tensor("out_0", (BATCH, SEQ, D), _mybir.dt.from_np(_np.dtype("float32")),
                               kind="ExternalOutput").ap())
    macaron(nc, *args)
    r = _run(nc, [arrays], core_ids=[0])
    return r.results[0]["out_0"]
```

```python
from contextlib import ExitStack
from math import sqrt

import concourse.bass as bass
from concourse import mybir

F32, F32R, F16, I32, U32 = (mybir.dt.float32, mybir.dt.float32r, mybir.dt.float16, mybir.dt.int32,
                            mybir.dt.uint32)
ALU = mybir.AluOpType
ACT = mybir.ActivationFunctionType
AX = mybir.AxisListType.X

P = 128
D = 256
KD = D // P
BATCH, SEQ = 2, 2048
TOKENS = BATCH * SEQ
NT = TOKENS // P
TT = 4
CH = TT * P
NC = TOKENS // CH
INTER = 1024
NK = INTER // P
NE = 8
CAP = TOKENS // NE
assert CAP == CH
NG = NE + 2
LN_EPS, FFN_EPS = 1e-5, 1e-12
H, DEPTH, DH = 8, 5, 32
NF = 2 ** DEPTH
ROW = D + 1
HG = 4
QC = SEQ // CH
MASKED = -30000.0
UP_BANKS, H_RING, HS_RING = 2, 2, 4
AHEAD = 2


def subset_coefficient(m):
    return sum(0.5 ** d for d in range(max(m, 1), DEPTH + 1)) / DEPTH


def whole(ap, n):
    return ap.rearrange("(a n) -> a n", a=1).to_broadcast([n, ap.shape[0]])


def macaron(nc, x, Wp, bp, Wv, Wo, nw, nb, wg, inter_w, inter_b, output_w, output_b,
            res_inter_w, res_inter_b, res_output_w, res_output_b, res_coef, out):
    x_tiles = x.rearrange("b (t p) d -> p (b t) d", p=P)
    out_tiles = out.rearrange("b (t p) d -> p (b t) d", p=P)
    slots_in = nc.dram_tensor("slots_in", [2 * TOKENS, ROW], F32).ap()
    moe_rows = nc.dram_tensor("moe_rows", [2 * TOKENS, D], F32).ap()

    with ExitStack() as top:
        def sb(name, shape, dt=F32):
            return top.enter_context(nc.sbuf_tensor(name, shape, dt))

        mem = dict(
            x_all=sb("x_all", [P, NT, D]),
            id32=sb("id32", [P, P]), id16=sb("id16", [P, P], F16),
            mask16=sb("mask16", [P, P], F16),
            before16=sb("before16", [P, P], F16),
            ones16=sb("ones16", [P, P], F16), ones32=sb("ones32", [P, DH]),
            minus_half=sb("minus_half", [P, 2 * TT]),
            rank=sb("rank", [P, NE]),
            spare=sb("spare", [P, NT]),
            same_expert=sb("same_expert", [P, NE, NT]),
            vecT=sb("vecT", [P, NE * NK + NK + 2 * KD]),
            wgc=sb("wgc", [P, KD, NG]),
            moe_w=sb("moe_w", [P, NT]),
        )
        x_in = [top.enter_context(nc.semaphore(f"x_in{i}")) for i in range(3)]
        constants(nc, mem, wg, res_coef, nw, nb, inter_b, res_inter_b, x_tiles, x_in)
        for layer in range(2):
            with ExitStack() as ffn:
                aT_all = ffn.enter_context(nc.sbuf_tensor(f"aT_all{layer}", [P, KD, TOKENS], F32))
                w_in = [ffn.enter_context(nc.semaphore(f"e{layer}_w_in{i}")) for i in range(2)]
                rows_in = ffn.enter_context(nc.semaphore(f"e{layer}_rows_in"))
                feed = ExpertFeed(nc, aT_all, w_in, rows_in, inter_w, output_w, slots_in)
                dense_block(nc, mem, layer, aT_all, feed, x_tiles if layer == 0 else None, x_in, res_inter_w,
                            res_output_w, res_output_b, slots_in, moe_rows)
                expert_block(nc, mem, layer, feed, output_b, moe_rows)
            if layer == 0:
                attention_block(nc, mem, Wp, bp, Wv, Wo, moe_rows)
            else:
                last_block(nc, mem, moe_rows, out_tiles)


def load_x(nc, mem, sp, x_tiles, x_in, c):
    rows = slice(c * TT, (c + 1) * TT)
    sp.dma_start(mem["x_all"][:, rows, :], x_tiles[:, rows, :]).then_inc(x_in[min(c, 2)], 16)


def constants(nc, mem, wg, res_coef, nw, nb, inter_b, res_inter_b, x_tiles, x_in):
    id32, id16, mask16, before16 = mem["id32"], mem["id16"], mem["mask16"], mem["before16"]
    NV = NE * NK + NK + 2 * KD
    with ExitStack() as ctx:
        rows = ctx.enter_context(nc.sbuf_tensor("vec_rows", [NV, P], F32))
        ids = ctx.enter_context(nc.sbuf_tensor("token_ids", [P, NT], I32))
        ranks = ctx.enter_context(nc.sbuf_tensor("rank_ids", [P, NE], I32))
        vec_ps = ctx.enter_context(nc.psum_tensor("vec_ps", [P, NV], F32))
        loaded = ctx.enter_context(nc.semaphore("c_loaded"))
        filled = ctx.enter_context(nc.semaphore("c_filled"))
        made = ctx.enter_context(nc.semaphore("c_made"))
        turned = ctx.enter_context(nc.semaphore("c_turned"))
        block = ctx.enter_context(nc.Block())

        @block.sync
        def _(sp):
            n0 = NE * NK
            load_x(nc, mem, sp, x_tiles, x_in, 0)
            sp.dma_start(rows[0:n0, :], inter_b.rearrange("e (k p) -> (e k) p", p=P)).then_inc(loaded, 16)
            sp.dma_start(rows[n0:n0 + NK, :], res_inter_b.rearrange("(k p) -> k p", p=P)).then_inc(loaded, 16)
            sp.dma_start(rows[n0 + NK:n0 + NK + KD, :], nw.rearrange("(k p) -> k p", p=P)).then_inc(loaded, 16)
            sp.dma_start(rows[n0 + NK + KD:NV, :], nb.rearrange("(k p) -> k p", p=P)).then_inc(loaded, 16)
            with nc.allow_non_contiguous_dma("router weights, once"):
                sp.dma_start(mem["wgc"][:, :, 0:NE], wg.rearrange("(k p) e -> p k e", p=P)).then_inc(loaded, 16)
                sp.dma_start(mem["wgc"][:, :, NE:NG], res_coef.rearrange("(k p) e -> p k e", p=P)).then_inc(loaded, 16)
            load_x(nc, mem, sp, x_tiles, x_in, 1)
            sp.wait_ge(loaded, 96)

        @block.gpsimd
        def _(pool):
            pool.memset(id32[:], 0.0).then_inc(filled, 1)
            pool.memset(id16[:], 0.0).then_inc(filled, 1)
            pool.memset(mask16[:], 0.0).then_inc(filled, 1)
            pool.memset(before16[:], 1.0).then_inc(filled, 1)
            pool.memset(mem["same_expert"][:], 1.0).then_inc(filled, 1)
            pool.memset(mem["ones16"][:], 1.0)
            pool.memset(mem["ones32"][:], 1.0)
            pool.memset(mem["minus_half"][:], -0.5)
            pool.wait_ge(filled, 5)
            for m in (id32, id16):
                pool.affine_select(out=m[:], in_=m[:], compare_op=ALU.not_equal, fill=1.0, base=0,
                                   pattern=[[-1, P]], channel_multiplier=1).then_inc(filled, 1)
            pool.affine_select(out=mask16[:], in_=mask16[:], compare_op=ALU.is_ge, fill=MASKED, base=0,
                               pattern=[[1, P]], channel_multiplier=-1)
            pool.affine_select(out=before16[:], in_=before16[:], compare_op=ALU.is_ge, fill=0.0, base=-1,
                               pattern=[[1, P]], channel_multiplier=-1)
            pool.memset(mem["same_expert"][:, :, 0:1], 0.0)
            pool.iota(ids[:], pattern=[[P, NT]], base=TOKENS, channel_multiplier=1).then_inc(filled, 1)
            pool.iota(ranks[:], pattern=[[-1, NE]], base=NE, channel_multiplier=0).then_inc(filled, 1)
            pool.wait_ge(filled, 9)
            pool.tensor_copy(mem["spare"][:], ids[:])
            pool.tensor_copy(mem["rank"][:], ranks[:]).then_inc(made, 1)

        @block.tensor
        def _(pe):
            pe.wait_ge(filled, 6)
            pe.wait_ge(loaded, 96)
            nc.tensor.transpose(vec_ps[:], rows[:], id32[0:NV, 0:NV]).then_inc(turned, 1)

        @block.vector
        def _(dve):
            dve.wait_ge(turned, 1)
            nc.vector.tensor_copy(mem["vecT"][:], vec_ps[:]).then_inc(made, 1)


class Mlp:

    def __init__(self, nc, ctx, tag):
        def sb(name, shape, dt=F32):
            return ctx.enter_context(nc.sbuf_tensor(f"{tag}_{name}", shape, dt))

        def sem(name):
            return ctx.enter_context(nc.semaphore(f"{tag}_{name}"))

        self.nc = nc
        self.x_hi, self.x_lo = sb("x_hi", [P, KD, CH], F32R), sb("x_lo", [P, KD, CH], F32R)
        self.h = sb("h", [P, H_RING, CH])
        self.h_hi, self.h_lo = sb("h_hi", [P, HS_RING, CH], F32R), sb("h_lo", [P, HS_RING, CH], F32R)
        self.up_ps = [ctx.enter_context(nc.psum_tensor(f"{tag}_up{i}", [P, CH], F32)) for i in range(UP_BANKS)]
        self.down_ps = [ctx.enter_context(nc.psum_tensor(f"{tag}_down{i}", [P, CH], F32)) for i in range(TT)]
        self.side = [ctx.enter_context(nc.psum_tensor(f"{tag}_side{i}", [P, CH], F32)) for i in range(2)]
        self.x_split = sem("x_split")
        self.x_hid = sem("x_hid")
        self.up_done = sem("up_done")
        self.gelu_done = sem("gelu_done")
        self.h_split = sem("h_split")
        self.down_done = sem("down_done")
        self.evacuated = sem("evacuated")

    def split_x_hi(self, dve, c, source):
        if not (isinstance(c, int) and c == 0):
            dve.wait_ge(self.up_done, c * NK)
        self.nc.vector.tensor_copy(self.x_hi[:], source).then_inc(self.x_hid, 1)

    def split_x_lo(self, dve, c, source):
        dve.wait_ge(self.x_hid, c + 1)
        self.nc.vector.tensor_tensor(self.x_lo[:], source, self.x_hi[:], ALU.subtract).then_inc(self.x_split, 1)

    def up(self, pe, c, k, w1_hi, w1_lo, first):
        nc = self.nc
        if not (first and k < UP_BANKS):
            pe.wait_ge(self.gelu_done, c * NK + (k - UP_BANKS + 1))
        bank = self.up_ps[k % UP_BANKS]
        n = 0
        for w, xs in ((w1_hi, self.x_hi), (w1_lo, self.x_hi), (w1_hi, self.x_lo)):
            if k == 0:
                pe.wait_ge(self.x_hid if xs is self.x_hi else self.x_split, c + 1)
            for kd in range(KD):
                last = nc.tensor.matmul(bank[:], w(kd), xs[:, kd, :], start=(n == 0), stop=(n == 3 * KD - 1))
                n += 1
        last.then_inc(self.up_done, 1)

    def gelu(self, act, c, k, bias, first):
        act.wait_ge(self.up_done, c * NK + (k + 1))
        if not (first and k < H_RING):
            act.wait_ge(self.h_split, c * NK + (k - H_RING + 1))
        if not (first and k < HS_RING):
            act.wait_ge(self.down_done, c * NK + (k - HS_RING + 1))
        for to in (self.h[:, k % H_RING, :], self.h_hi[:, k % HS_RING, :]):
            i = self.nc.scalar.activation(to, self.up_ps[k % UP_BANKS][:], ACT.Gelu_apprx_tanh, bias=bias)
        i.then_inc(self.gelu_done, 1)

    def split_h(self, dve, c, k, first):
        nc = self.nc
        dve.wait_ge(self.gelu_done, c * NK + (k + 1))
        if not (first and k < HS_RING):
            dve.wait_ge(self.down_done, c * NK + (k - HS_RING + 1))
        h, hi, lo = self.h[:, k % H_RING, :], self.h_hi[:, k % HS_RING, :], self.h_lo[:, k % HS_RING, :]
        nc.vector.tensor_tensor(lo, h, hi, ALU.subtract).then_inc(self.h_split, 1)

    def down(self, pe, c, k, w2_hi, w2_lo, first):
        nc = self.nc
        pe.wait_ge(self.h_split, c * NK + (k + 1))
        if k == 0 and not first:
            pe.wait_ge(self.evacuated, c)
        for t in range(TT):
            hi = self.h_hi[:, k % HS_RING, t * P:(t + 1) * P]
            lo = self.h_lo[:, k % HS_RING, t * P:(t + 1) * P]
            bank = self.down_ps[t][:, 0:D]
            nc.tensor.matmul(bank, hi, w2_hi, start=(k == 0), stop=False)
            nc.tensor.matmul(bank, hi, w2_lo, start=False, stop=False)
            last = nc.tensor.matmul(bank, lo, w2_hi, start=False, stop=(k == NK - 1))
        last.then_inc(self.down_done, 1)

    def tensor_chunk(self, pe, c, weights, first=False, beside=None):
        for s in range(NK + AHEAD):
            if s < NK:
                w1_hi, w1_lo, _, _ = weights(pe, s, True)
                self.up(pe, c, s, w1_hi, w1_lo, first)
            if s >= AHEAD:
                k = s - AHEAD
                _, _, w2_hi, w2_lo = weights(pe, k, False)
                self.down(pe, c, k, w2_hi, w2_lo, first)
                if beside and k in beside:
                    beside[k]()


def split_sems(ctx, nc, tag, names):
    return {n: ctx.enter_context(nc.semaphore(f"{tag}_{n}")) for n in names.split()}


def wait_carried(nc, dve, scratch, sem, value):
    dve.wait_ge(sem, value)
    nc.vector.memset(scratch, 0.0)


def dense_block(nc, mem, layer, aT_all, feed, x_tiles, x_in, res_w1, res_w2, res_b2, slots_in,
                moe_rows):
    tag = f"d{layer}"
    x_all, wgc, vecT = mem["x_all"], mem["wgc"], mem["vecT"]
    with ExitStack() as ctx:
        def sb(name, shape, dt=F32):
            return ctx.enter_context(nc.sbuf_tensor(f"{tag}_{name}", shape, dt))

        m = Mlp(nc, ctx, tag)
        y_all = sb("y_all", [P, NT, ROW])
        y = sb("y", [P, TT, D])
        aT = sb("aT", [P, KD, CH])
        w1 = [sb(f"w1_{n}", [P, KD, INTER], F32R) for n in ("hi", "lo")]
        w2 = [sb(f"w2_{n}", [P, NK, D], F32R) for n in ("hi", "lo")]
        raw1 = aT_all[:, 0, TOKENS - KD * INTER:].rearrange("p (k n) -> p k n", k=KD)
        raw2 = aT_all[:, 1, TOKENS - NK * D:].rearrange("p (k n) -> p k n", k=NK)
        b2 = sb("b2", [P, D])
        zeros = sb("zeros", [P, ROW])
        idle = sb("idle", [P, 1])
        stats, mv = sb("stats", [P, TT, 6]), sb("mv", [P, TT, 2])
        var, rstd = sb("var", [P, 2, TT]), sb("rstd", [P, 2, TT])
        lin = sb("lin", [P, 2, TT])
        logits = sb("logits", [P, NT, NG])
        dif, th = sb("dif", [P, TT]), sb("th", [P, TT])
        c0, c1 = sb("c0", [P, NT]), sb("c1", [P, NT])
        part = sb("part", [P, TT, D])
        top, eq = sb("top", [P, NT]), sb("eq", [P, NT, NE])
        lm, ex = sb("lm", [P, NT, NE]), sb("ex", [P, NT, NE])
        best, hot, hot16 = sb("best", [P, NT]), sb("hot", [P, NT, NE]), sb("hot16", [P, NT, NE], F16)
        incl, locs = sb("incl", [P, NE, NT]), sb("locs", [P, NE, NT])
        loc, keep, base = sb("loc", [P, NT]), sb("keep", [P, NT]), sb("base", [P, NT])
        t0, t1, rec = sb("t0", [P, NT]), sb("t1", [P, NT]), sb("rec", [P, NT])
        scatter_at = sb("scatter_at", [P, NT], U32)

        s = split_sems(ctx, nc, tag, "stat_chain var_ready rstd_ready y_ready y_kept turned aT_ready lin_ready "
                       "logits_done logits_read dif_ready th_ready mixed updated gate lm_ready ex_ready hot_ready "
                       "counted scatter_ready scattered b2_in zeros_ready zeroed")
        w_in = [ctx.enter_context(nc.semaphore(f"{tag}_w_in{i}")) for i in range(2)]
        w_hid = [ctx.enter_context(nc.semaphore(f"{tag}_w_hid{i}")) for i in range(2)]
        w_split = [ctx.enter_context(nc.semaphore(f"{tag}_w_split{i}")) for i in range(2)]
        NB = NE * NK + NK
        gain = [vecT[:, NB + k:NB + k + 1] for k in range(KD)]
        shift = [vecT[:, NB + KD + k:NB + KD + k + 1] for k in range(KD)]
        b1 = [vecT[:, NE * NK + k:NE * NK + k + 1] for k in range(NK)]
        block = ctx.enter_context(nc.Block())

        @block.sync
        def _(sp):
            sp.dma_start(raw1, res_w1.rearrange("(k p) n -> p k n", p=P)).then_inc(w_in[0], 16)
            sp.dma_start(raw2, res_w2.rearrange("(k p) n -> p k n", p=P)).then_inc(w_in[1], 16)
            sp.dma_start(b2[:], whole(res_b2, P)).then_inc(s["b2_in"], 16)
            if x_tiles is not None:
                for c in range(2, NC):
                    load_x(nc, mem, sp, x_tiles, x_in, c)
            sp.wait_ge(s["zeros_ready"], 1)
            for rows, width in ((slots_in, ROW),) + (((moe_rows, D),) if x_tiles is not None else ()):
                for i in range(TOKENS // CH):
                    sp.dma_start(rows[i * CH:(i + 1) * CH, :].rearrange("(p a) d -> p a d", a=TT),
                                 zeros[:, 0:width].unsqueeze(1).to_broadcast([P, TT, width])).then_inc(s["zeroed"], 16)
            feed.load_weights(sp, 0, [(m.x_split, feed.WEIGHT_CHUNKS)] * 2)
            feed.load_rows(sp, 0, [(m.x_split, feed.ROW_CHUNKS), (s["scattered"], 16 * NT)])

        @block.gpsimd
        def _(pool):
            nc.gpsimd.memset(zeros[:], 0.0).then_inc(s["zeros_ready"], 1)
            nc.gpsimd.tensor_scalar(y_all[:, :, D], mem["spare"][:], 1.0 - TOKENS, None, ALU.add)

            def norm(a):
                pool.wait_ge(s["var_ready"], a + 1)
                nc.gpsimd.tensor_tensor(rstd[:].rearrange("p a t -> p (a t)"), var[:].rearrange("p a t -> p (a t)"),
                                        mem["minus_half"][:], ALU.pow).then_inc(s["rstd_ready"], 1)
                pool.wait_ge(s["y_ready"], a + 1)
                nc.gpsimd.tensor_copy(y_all[:, bass.ds(a * TT, TT), 0:D], y[:]).then_inc(s["y_kept"], 1)

            with pool.Fori(0, NC) as a:
                norm(a)
            pool.wait_ge(s["y_kept"], NC)
            pool.wait_ge(s["scatter_ready"], 1)
            pool.wait_ge(s["zeroed"], 16 * (TOKENS // CH) * (2 if x_tiles is not None else 1))
            for t in range(NT):
                nc.gpsimd.indirect_dma_start(
                    out=slots_in, out_offset=bass.IndirectOffsetOnAxis(ap=scatter_at[:, t:t + 1], axis=0),
                    in_=y_all[:, t, :], in_offset=None).then_inc(s["scattered"], 16)
            pool.wait_ge(s["scattered"], 16 * NT)

        @block.vector
        def _(dve):
            v = nc.vector

            def stats_of(a):
                for t in range(TT):
                    i = v.bn_stats(stats[:, t, :], x_all[:, a * TT + t, :])
                i.then_inc(s["stat_chain"], 1)
                wait_carried(nc, dve, idle[:], s["stat_chain"], a * 2 + 1)
                for t in range(TT):
                    i = v.bn_aggr(mv[:, t, :], stats[:, t, :])
                i.then_inc(s["stat_chain"], 1)
                dve.wait_ge(s["stat_chain"], a * 2 + 2)
                v.tensor_scalar(var[:, 0, :], mv[:, :, 1], LN_EPS, None, ALU.add)
                v.tensor_scalar(var[:, 1, :], mv[:, :, 1], 1.0 + FFN_EPS, FFN_EPS * LN_EPS, ALU.mult,
                                ALU.add).then_inc(s["var_ready"], 1)

            def y_of(a):
                dve.wait_ge(s["rstd_ready"], a + 1)
                if not (isinstance(a, int) and a == 0):
                    dve.wait_ge(s["turned"], a)
                    dve.wait_ge(s["y_kept"], a)
                for t in range(TT):
                    i = v.tensor_scalar(y[:, t, :], x_all[:, a * TT + t, :], mv[:, t, 0:1], rstd[:, 1, t:t + 1],
                                        ALU.subtract, ALU.mult)
                i.then_inc(s["y_ready"], 1)

            def x_of(a):
                v.tensor_scalar(lin[:, 0, :], rstd[:, 0, :], 0.5, 1.0, ALU.mult, ALU.add)
                v.scalar_tensor_tensor(lin[:, 1, :], mv[:, :, 0], -0.5, rstd[:, 0, :], ALU.mult,
                                       ALU.mult).then_inc(s["lin_ready"], 1)
                dve.wait_ge(s["lin_ready"], a + 1)
                for t in range(TT):
                    v.tensor_scalar(x_all[:, a * TT + t, :], x_all[:, a * TT + t, :], lin[:, 0, t:t + 1],
                                    lin[:, 1, t:t + 1], ALU.mult, ALU.add)

            def logits_of(a):
                dve.wait_ge(s["logits_done"], a + 1)
                v.tensor_copy(logits[:, bass.ds(a * TT, TT), :],
                              m.side[0][:, 0:TT * NG].rearrange("p (t g) -> p t g", g=NG)).then_inc(s["logits_read"], 1)
                dve.wait_ge(s["logits_read"], a + 1)
                v.tensor_tensor(dif[:], logits[:, bass.ds(a * TT, TT), NE], logits[:, bass.ds(a * TT, TT), NE + 1],
                                ALU.subtract).then_inc(s["dif_ready"], 1)

            def mix_of(a):
                dve.wait_ge(s["th_ready"], a + 1)
                v.tensor_scalar(c0[:, bass.ds(a * TT, TT)], th[:], 0.25, 0.25, ALU.mult, ALU.add)
                v.tensor_scalar(c1[:, bass.ds(a * TT, TT)], th[:], -0.25, 0.25, ALU.mult, ALU.add).then_inc(s["mixed"], 1)

            def empty(c):
                dve.wait_ge(m.down_done, c * NK + NK)
                for t in range(TT):
                    i = v.tensor_tensor(part[:, t, :], m.down_ps[t][:, 0:D], b2[:], ALU.add)
                i.then_inc(m.evacuated, 1)
                dve.wait_ge(m.evacuated, c + 1)
                for t in range(TT):
                    i = v.scalar_tensor_tensor(x_all[:, c * TT + t, :], part[:, t, :], c0[:, bass.ds(c * TT + t, 1)],
                                               x_all[:, c * TT + t, :], ALU.mult, ALU.add)
                i.then_inc(s["updated"], 1)

            def rows_T(c):
                return aT_all[:, :, bass.ds(c * CH, CH)]

            def mlp(c, first=False, beside=None, last=False):
                for k in range(NK):
                    if k == NK - 1 and not last:
                        dve.wait_ge(s["aT_ready"], c + 2)
                        m.split_x_hi(dve, c + 1, rows_T(c + 1))
                    m.split_h(dve, c, k, first)
                    if k == NK - 1 and not last:
                        m.split_x_lo(dve, c + 1, rows_T(c + 1))
                    for f in (beside or {}).get(k, ()):
                        f()
                empty(c)

            def norms(c):
                p, a, b = c * 2, c * 2 + 1, c * 2 + 2
                at = {1: [lambda: y_of(a)], 2: [lambda: logits_of(p), lambda: x_of(a)],
                      4: [lambda: mix_of(p)], 6: [lambda: logits_of(a)]}
                at[0] = [lambda: stats_of(a)]
                if not (isinstance(c, int) and c == 0):
                    at[0].insert(0, lambda: mix_of(p - 1))
                if not (isinstance(c, int) and b == NC):
                    at[4].append(lambda: stats_of(b))
                    at[5] = [lambda: y_of(b)]
                    at[6].append(lambda: x_of(b))
                return at

            dve.wait_ge(x_in[0], 16)
            stats_of(0)
            y_of(0)
            x_of(0)
            for w, raw, hid, split in ((w1, raw1, w_hid[0], w_split[0]), (w2, raw2, w_hid[1], w_split[1])):
                dve.wait_ge(hid, 1)
                v.tensor_tensor(w[1][:], raw, w[0][:], ALU.subtract).then_inc(split, 1)
                if w is w1:
                    dve.wait_ge(s["aT_ready"], 1)
                    m.split_x_hi(dve, 0, rows_T(0))
                    m.split_x_lo(dve, 0, rows_T(0))
            dve.wait_ge(x_in[1], 16)
            dve.wait_ge(x_in[2], 16 * (NC - 2))
            dve.wait_ge(s["b2_in"], 16)
            mlp(0, True, norms(0))
            with dve.Fori(1, 3) as c:
                mlp(c, False, norms(c))
            mlp(3, False, norms(3))

            chain = [0]

            def link(i):
                chain[0] += 1
                i.then_inc(s["gate"], 1)
                dve.wait_ge(s["gate"], chain[0])

            def bc_e(ap):
                return ap.unsqueeze(2).to_broadcast([P, NT, NE])

            rank = mem["rank"][:].unsqueeze(1).to_broadcast([P, NT, NE])
            gates = logits[:, :, 0:NE]

            def choose():
                link(v.tensor_reduce(top[:], gates, AX, ALU.max))
                v.tensor_tensor(lm[:], gates, bc_e(top[:]), ALU.subtract).then_inc(s["lm_ready"], 1)
                link(v.tensor_tensor(eq[:], gates, bc_e(top[:]), ALU.is_equal))
                link(v.tensor_tensor(eq[:], eq[:], rank, ALU.mult))
                link(v.tensor_reduce(best[:], eq[:], AX, ALU.max))
                link(v.tensor_tensor(hot[:], rank, bc_e(best[:]), ALU.is_equal))
                v.tensor_copy(hot16[:], hot[:]).then_inc(s["hot_ready"], 1)
                link(v.tensor_scalar(base[:], best[:], float(-CAP), float(NE * CAP), ALU.mult, ALU.add))

            def place():
                dve.wait_ge(s["counted"], 1)
                before = m.side[0][:, 0:NE * NT].rearrange("p (e t) -> p e t", e=NE)
                total = m.side[1][:, 0:NE * NT].rearrange("p (e t) -> p e t", e=NE)
                flat = "p e t -> p (e t)"
                link(v.tensor_tensor_scan(incl[:].rearrange(flat), mem["same_expert"][:].rearrange(flat),
                                          m.side[1][:, 0:NE * NT], 0.0, ALU.mult, ALU.add))
                link(v.tensor_tensor(locs[:], incl[:], total, ALU.subtract))
                link(v.tensor_tensor(locs[:], locs[:], before, ALU.add))
                link(v.tensor_tensor(eq[:], locs[:].rearrange("p e t -> p t e"), hot[:], ALU.mult))
                link(v.tensor_reduce(loc[:], eq[:], AX, ALU.add))

            def address():
                link(v.tensor_scalar(keep[:], loc[:], float(CAP), None, ALU.is_lt))
                link(v.tensor_tensor(t1[:], loc[:], base[:], ALU.add))
                link(v.tensor_tensor(t1[:], t1[:], mem["spare"][:], ALU.subtract))
                link(v.tensor_tensor(t1[:], t1[:], keep[:], ALU.mult))
                link(v.tensor_tensor(t1[:], t1[:], mem["spare"][:], ALU.add))
                v.tensor_copy(scatter_at[:], t1[:]).then_inc(s["scatter_ready"], 1)

            def weigh():
                dve.wait_ge(s["ex_ready"], 1)
                link(v.tensor_reduce(t0[:], ex[:], AX, ALU.add))
                link(v.reciprocal(rec[:], t0[:]))
                link(v.tensor_tensor(rec[:], rec[:], keep[:], ALU.mult))
                link(v.tensor_tensor(mem["moe_w"][:], rec[:], c1[:], ALU.mult))

            mlp(4, False, {0: [lambda: mix_of(NC - 1), choose], 2: [place], 3: [address], 5: [weigh]})
            with dve.Fori(5, NC - 1) as c:
                mlp(c)
            mlp(NC - 1, last=True)

        @block.scalar
        def _(act):
            def aT_of(a):
                act.wait_ge(s["turned"], a + 1)
                if not (isinstance(a, int) and a == 0):
                    act.wait_ge(s["logits_done"], a)
                for kd in range(KD):
                    nc.scalar.activation(aT[:, kd, :], m.side[kd][:], ACT.Identity, bias=shift[kd], scale=gain[kd])
                    i = nc.scalar.activation(aT_all[:, kd, bass.ds(a * CH, CH)], m.side[kd][:], ACT.Identity,
                                             bias=shift[kd], scale=gain[kd])
                i.then_inc(s["aT_ready"], 1)

            def th_of(a):
                act.wait_ge(s["dif_ready"], a + 1)
                nc.scalar.activation(th[:], dif[:], ACT.Tanh, scale=0.5).then_inc(s["th_ready"], 1)

            def mlp(c, first=False, beside=None):
                for k in range(NK):
                    m.gelu(act, c, k, b1[k], first)
                    for f in (beside or {}).get(k, ()):
                        f()

            def norms(c):
                p, a, b = c * 2, c * 2 + 1, c * 2 + 2
                at = {3: [lambda: th_of(p)], 4: [lambda: aT_of(a)], 7: [lambda: th_of(a)]}
                if not (isinstance(c, int) and b == NC):
                    at[7].insert(0, lambda: aT_of(b))
                return at

            def ex_all():
                act.wait_ge(s["lm_ready"], 1)
                nc.scalar.activation(ex[:], lm[:], ACT.Exp).then_inc(s["ex_ready"], 1)

            for w, raw, came, hid in ((w1, raw1, w_in[0], w_hid[0]), (w2, raw2, w_in[1], w_hid[1])):
                act.wait_ge(came, 16)
                nc.scalar.copy(w[0][:], raw).then_inc(hid, 1)
                if w is w1:
                    aT_of(0)
            mlp(0, True, norms(0))
            with act.Fori(1, 3) as c:
                mlp(c, False, norms(c))
            mlp(3, False, norms(3))
            mlp(4, False, {2: [ex_all]})
            with act.Fori(5, NC) as c:
                mlp(c)

        @block.tensor
        def _(pe):
            def turn(a):
                pe.wait_ge(s["y_ready"], a + 1)
                if not (isinstance(a, int) and a == 0):
                    pe.wait_ge(s["aT_ready"], a)
                    pe.wait_ge(s["dif_ready"], a)
                for kd in range(KD):
                    for t in range(TT):
                        i = nc.tensor.transpose(m.side[kd][:, t * P:(t + 1) * P], y[:, t, kd * P:(kd + 1) * P],
                                                mem["id32"][:])
                i.then_inc(s["turned"], 1)

            def route(a):
                pe.wait_ge(s["aT_ready"], a + 1)
                for t in range(TT):
                    for kd in range(KD):
                        i = nc.tensor.matmul(m.side[0][:, t * NG:(t + 1) * NG], aT[:, kd, t * P:(t + 1) * P],
                                             wgc[:, kd, :], start=(kd == 0), stop=(kd == KD - 1))
                i.then_inc(s["logits_done"], 1)

            def count():
                pe.wait_ge(s["hot_ready"], 1)
                hot_et = hot16[:].rearrange("p t e -> p e t")
                nc.tensor.matmul(m.side[0][:, 0:NE * NT].rearrange("p (e t) -> p e t", e=NE), mem["before16"][:],
                                 hot_et, start=True, stop=True)
                nc.tensor.matmul(m.side[1][:, 0:NE * NT].rearrange("p (e t) -> p e t", e=NE), mem["ones16"][:],
                                 hot_et, start=True, stop=True).then_inc(s["counted"], 1)

            def weights(pe, k, is_up, first=False):
                if first and k == 0:
                    pe.wait_ge(w_split[0 if is_up else 1], 1)
                n = slice(k * P, (k + 1) * P)
                return (lambda kd: w1[0][:, kd, n]), (lambda kd: w1[1][:, kd, n]), w2[0][:, k, :], w2[1][:, k, :]

            def norms(c):
                p, a, b = c * 2, c * 2 + 1, c * 2 + 2
                at = {0: lambda: route(p), 2: lambda: turn(a), 4: lambda: route(a)}
                if not (isinstance(c, int) and b == NC):
                    at[6] = lambda: turn(b)
                return at

            turn(0)
            m.tensor_chunk(pe, 0, lambda pe, k, is_up: weights(pe, k, is_up, True), True, norms(0))
            with pe.Fori(1, 3) as c:
                m.tensor_chunk(pe, c, weights, False, norms(c))
            m.tensor_chunk(pe, 3, weights, False, norms(3))
            m.tensor_chunk(pe, 4, weights, False, {1: count})
            with pe.Fori(5, NC) as c:
                m.tensor_chunk(pe, c, weights)


W_RING, W_AHEAD = 8, 4


class ExpertFeed:
    WEIGHT_CHUNKS = NC // 2
    ROW_CHUNKS = NC // 2 + -(-TT * ROW // CH)

    def __init__(self, nc, aT_all, w_in, rows_in, inter_w, output_w, slots_in):
        n = self.WEIGHT_CHUNKS * CH
        assert n == KD * INTER == NK * D
        self.raw1 = aT_all[:, 0, 0:n].rearrange("p (h k n) -> p h k n", h=2, k=KD)
        self.raw2 = aT_all[:, 1, 0:n].rearrange("p (h k d) -> p h k d", h=2, d=D)
        self.rows = aT_all[:, 0, n:n + TT * ROW].rearrange("p (t d) -> p t d", d=ROW)
        self.w_in, self.rows_in = w_in, rows_in
        self.w1_rows = inter_w.rearrange("e (k p) n -> e p k n", p=P)
        self.w2_rows = output_w.rearrange("e (k p) n -> e p k n", p=P)
        self.in_rows = slots_in.rearrange("(c t p) d -> c p t d", t=TT, p=P)

    def load_weights(self, sp, e, waits):
        HALF = NK // 2
        for half, (sem, value) in enumerate(waits):
            sp.wait_ge(sem, value)
            sp.dma_start(self.raw1[:, half], self.w1_rows[e, :, :, half * HALF * P:(half + 1) * HALF * P]).then_inc(self.w_in[half], 16)
            sp.dma_start(self.raw2[:, half], self.w2_rows[e, :, half * HALF:(half + 1) * HALF, :]).then_inc(self.w_in[half], 16)

    def load_rows(self, sp, e, waits):
        for sem, value in waits:
            sp.wait_ge(sem, value)
        sp.dma_start(self.rows, self.in_rows[e]).then_inc(self.rows_in, 16)


def expert_block(nc, mem, layer, feed, output_b, moe_rows):
    tag = f"e{layer}"
    vecT = mem["vecT"]
    HALF = NK // 2
    with ExitStack() as ctx:
        def sb(name, shape, dt=F32):
            return ctx.enter_context(nc.sbuf_tensor(f"{tag}_{name}", shape, dt))

        m = Mlp(nc, ctx, tag)
        aT = sb("aT", [P, KD, CH])
        rows, raw1, raw2, w_in = feed.rows, feed.raw1, feed.raw2, feed.w_in
        w1 = [sb(f"w1_{n}", [P, W_RING, KD, P], F32R) for n in ("hi", "lo")]
        w2 = [sb(f"w2_{n}", [P, W_RING, D], F32R) for n in ("hi", "lo")]
        b2 = sb("b2", [P, NE, D])
        done = sb("done", [P, TT, D])
        empty, token = sb("empty", [P, TT]), sb("token", [P, TT])
        idle = sb("idle", [P, 1])
        to = sb("to", [P, TT], U32)
        s = split_sems(ctx, nc, tag, "b_in idled token_chain token_read to_ready turned aT_ready w_hid w_split stored")
        NB = NE * NK + NK
        gain = [vecT[:, NB + k:NB + k + 1] for k in range(KD)]
        shift = [vecT[:, NB + KD + k:NB + KD + k + 1] for k in range(KD)]
        block = ctx.enter_context(nc.Block())

        @block.sync
        def _(sp):
            sp.dma_start(b2[:], output_b.rearrange("(a e) n -> a e n", a=1).to_broadcast([P, NE, D])).then_inc(s["b_in"], 16)
            with sp.Fori(1, NE) as e:
                feed.load_rows(sp, e, [(s["turned"], e), (s["token_read"], e)])
                feed.load_weights(sp, e, [(s["w_split"], (e - 1) * NK + (half + 1) * HALF) for half in range(2)])

        @block.gpsimd
        def _(pool):
            def give_back(e, first=False):
                if not first:
                    pool.wait_ge(s["idled"], e)
                pool.wait_ge(s["to_ready"], e + 1)
                pool.wait_ge(m.evacuated, e + 1)
                nc.gpsimd.tensor_tensor(idle[:], mem["minus_half"][:, 0:1], mem["minus_half"][:, 0:1],
                                        ALU.mult).then_inc(s["idled"], 1)
                for t in range(TT):
                    nc.gpsimd.indirect_dma_start(
                        out=moe_rows, out_offset=bass.IndirectOffsetOnAxis(ap=to[:, t:t + 1], axis=0),
                        in_=done[:, t, :], in_offset=None).then_inc(s["stored"], 16)

            give_back(0, first=True)
            with pool.Fori(1, NE) as e:
                give_back(e)
            pool.wait_ge(s["stored"], 16 * TT * NE)

        @block.vector
        def _(dve):
            v = nc.vector

            def split_w(e, k):
                n = e * NK + k
                k, e = k % NK, e + k // NK
                r, half, q = k % W_RING, k // HALF, k % HALF
                if k % HALF == 0:
                    dve.wait_ge(w_in[half], (e + 1) * 32)
                a1, a2 = raw1[:, half, :, q * P:(q + 1) * P], raw2[:, half, q, :]
                v.tensor_copy(w1[0][:, r, :, :], a1)
                v.tensor_copy(w2[0][:, r, :], a2).then_inc(s["w_hid"], 1)
                dve.wait_ge(s["w_hid"], n + 1)
                v.tensor_tensor(w1[1][:, r, :, :], a1, w1[0][:, r, :, :], ALU.subtract)
                v.tensor_tensor(w2[1][:, r, :], a2, w2[0][:, r, :], ALU.subtract).then_inc(s["w_split"], 1)

            def tokens_of(e):
                dve.wait_ge(feed.rows_in, (e + 1) * 16)
                marks = rows[:, :, D]
                v.tensor_scalar(empty[:], marks, 0.0, None, ALU.is_equal).then_inc(s["token_chain"], 1)
                dve.wait_ge(s["token_chain"], e * 2 + 1)
                v.scalar_tensor_tensor(empty[:], mem["spare"][:, bass.ds(e * TT, TT)], 1.0, empty[:], ALU.add,
                                       ALU.mult).then_inc(s["token_chain"], 1)
                dve.wait_ge(s["token_chain"], e * 2 + 2)
                v.scalar_tensor_tensor(token[:], marks, -1.0, empty[:], ALU.add, ALU.add).then_inc(s["token_read"], 1)

            def expert(e, first=False, last=False):
                for k in range(NK):
                    if k == 4:
                        dve.wait_ge(s["token_read"], e + 1)
                        if not first:
                            dve.wait_ge(s["stored"], e * 16 * TT)
                        v.tensor_copy(to[:], token[:]).then_inc(s["to_ready"], 1)
                        if not last:
                            dve.wait_ge(s["to_ready"], e + 1)
                            tokens_of(e + 1)
                    if k == NK - 1 and not last:
                        dve.wait_ge(s["aT_ready"], e + 2)
                        m.split_x_hi(dve, e + 1, aT[:])
                    m.split_h(dve, e, k, first)
                    if k == NK - 1 and not last:
                        m.split_x_lo(dve, e + 1, aT[:])
                    if not (last and k + W_AHEAD >= NK):
                        if not (first and k + W_AHEAD < W_RING):
                            dve.wait_ge(m.down_done, e * NK + (k + W_AHEAD - W_RING + 1))
                        split_w(e, k + W_AHEAD)
                dve.wait_ge(m.down_done, e * NK + NK)
                if first:
                    dve.wait_ge(s["b_in"], 16)
                for t in range(TT):
                    i = v.tensor_tensor(done[:, t, :], m.down_ps[t][:, 0:D], b2[:, e, :], ALU.add)
                i.then_inc(m.evacuated, 1)

            tokens_of(0)
            for k in range(2):
                split_w(0, k)
            dve.wait_ge(s["aT_ready"], 1)
            m.split_x_hi(dve, 0, aT[:])
            m.split_x_lo(dve, 0, aT[:])
            for k in range(2, W_AHEAD):
                split_w(0, k)
            expert(0, first=True)
            with dve.Fori(1, NE - 1) as e:
                expert(e)
            expert(NE - 1, last=True)

        @block.scalar
        def _(act):
            def aT_of(e, first=False):
                act.wait_ge(s["turned"], e + 1)
                if not first:
                    act.wait_ge(m.x_split, e)
                for kd in range(KD):
                    i = nc.scalar.activation(aT[:, kd, :], m.side[kd][:], ACT.Identity, bias=shift[kd], scale=gain[kd])
                i.then_inc(s["aT_ready"], 1)

            def expert(e, first=False, last=False):
                for k in range(NK):
                    m.gelu(act, e, k, vecT[:, bass.ds(e * NK + k, 1)], first)
                    if k == 4 and not last:
                        aT_of(e + 1)

            aT_of(0, True)
            expert(0, first=True)
            with act.Fori(1, NE - 1) as e:
                expert(e)
            expert(NE - 1, last=True)

        @block.tensor
        def _(pe):
            def turn(e, first=False):
                pe.wait_ge(feed.rows_in, (e + 1) * 16)
                if not first:
                    pe.wait_ge(s["aT_ready"], e)
                for kd in range(KD):
                    for t in range(TT):
                        i = nc.tensor.transpose(m.side[kd][:, t * P:(t + 1) * P], rows[:, t, kd * P:(kd + 1) * P],
                                                mem["id32"][:])
                i.then_inc(s["turned"], 1)

            def expert(e, first=False, last=False):
                def weights(pe, k, is_up):
                    r = k % W_RING
                    if is_up:
                        pe.wait_ge(s["w_split"], e * NK + (k + 1))
                    return (lambda kd: w1[0][:, r, kd, :]), (lambda kd: w1[1][:, r, kd, :]), w2[0][:, r, :], w2[1][:, r, :]
                m.tensor_chunk(pe, e, weights, first, None if last else {2: lambda: turn(e + 1)})

            turn(0, True)
            expert(0, first=True)
            with pe.Fori(1, NE - 1) as e:
                expert(e)
            expert(NE - 1, last=True)


NP2 = HG // 2
PAIRS = [(c, g, j, hp) for c in range(QC) for g in range(H // HG) for j in range(TT * (c + 1)) for hp in range(NP2)]
P_RING = 4
NPROJ = D + H * DEPTH


def combine_rows(nc, mem, dve, moe, came, value, combined, n):
    dve.wait_ge(came, value)
    for t in range(TT):
        i = nc.vector.scalar_tensor_tensor(mem["x_all"][:, n * TT + t, :], moe[:, t, :],
                                           mem["moe_w"][:, bass.ds(n * TT + t, 1)], mem["x_all"][:, n * TT + t, :],
                                           ALU.mult, ALU.add)
    i.then_inc(combined, 1)


def chunk_rows(moe_rows, n, chunks=1):
    return moe_rows[n * chunks * CH:(n + 1) * chunks * CH, :].rearrange("(t p) d -> p t d", p=P)


def attention_block(nc, mem, Wp, bp, Wv, Wo, moe_rows):
    x_all = mem["x_all"]
    with ExitStack() as ctx:
        def sb(name, shape, dt=F32):
            return ctx.enter_context(nc.sbuf_tensor(f"a_{name}", shape, dt))

        def ps(name, shape):
            return ctx.enter_context(nc.psum_tensor(f"a_{name}", shape, F32))

        KT = sb("KT", [P, H, SEQ], F16)
        QT = sb("QT", [P, 2, H, CH], F16)
        V = sb("V", [P, SEQ // P, D])
        probs = sb("probs", [P, P_RING, 2, CH])
        wvp, wo = sb("wvp", [P, KD, NPROJ]), sb("wo", [P, KD, D])
        bpb = sb("bpb", [P, H * DEPTH])
        moe = sb("moe", [P, 2, TT, D])
        idle = sb("idle", [P, 1])
        stats, mv = sb("stats", [P, TT, 6]), sb("mv", [P, TT, 2])
        var, rstd = sb("var", [P, TT]), sb("rstd", [P, TT])
        y, yT = sb("y", [P, TT, D]), sb("yT", [P, KD, CH])
        z, th = sb("z", [P, TT, H * DEPTH]), sb("th", [P, TT, H * DEPTH])
        mono, coef = sb("mono", [P, TT * H, NF]), sb("coef", [P, NF])
        feat, hl = sb("feat", [P, TT * H, NF]), sb("hl", [P, TT * H, 2, NF], F16)
        Kf, Qf = sb("Kf", [P, TT * H, 4 * NF], F16), sb("Qf", [P, TT * H, 4 * NF], F16)
        cc, dd, rr = (sb(n, [P, H // HG, CH]) for n in ("cc", "dd", "rr"))
        ctxn = sb("ctxn", [P, H // HG, CH])
        S = [ps(f"S{i}", [P, 2, CH]) for i in range(2)]
        cx = [ps(f"cx{i}", [P, CH]) for i in range(2)]
        misc = [ps(f"misc{i}", [P, CH]) for i in range(2)]

        s = split_sems(ctx, nc, "a", "w_in chain combined var_ready rstd_ready y_ready turned yT_ready proj_done "
                       "proj_read th_ready f_ready fT_done feat_read s_done exp_done pv_done cx_free "
                       "norm_chain ctx_ready wo_done added coef_ready f_ready_chain")
        moe_in = [ctx.enter_context(nc.semaphore(f"a_moe_in{i}")) for i in range(2)]
        block = ctx.enter_context(nc.Block())
        NPAIR = len(PAIRS)

        def first_pair(c):
            return next(i for i, q in enumerate(PAIRS) if q[0] == c)

        def beside(c):
            n = 4 * TT * (c + 1)
            at = {}
            if c:
                at[5] = ("wo",)
            if c + 1 < QC:
                at[1 if c == 0 else 7] = ("turn",)
                at[3 if c == 0 else 9] = ("proj",)
                for h in range(H):
                    at[n // 2 - 1 + h] = ("feat", h)
            return at

        @block.sync
        def _(sp):
            def load_moe(n):
                sp.dma_start(moe[:, n % 2, :, :], chunk_rows(moe_rows, n)).then_inc(moe_in[n % 2], 16)

            load_moe(0)
            sp.dma_start(wvp[:, :, 0:D], Wv.rearrange("(k p) n -> p k n", p=P)).then_inc(s["w_in"], 16)
            sp.dma_start(wvp[:, :, D:NPROJ], Wp.rearrange("(k p) n -> p k n", p=P)).then_inc(s["w_in"], 16)
            sp.dma_start(wo[:], Wo.rearrange("(k p) n -> p k n", p=P)).then_inc(s["w_in"], 16)
            sp.dma_start(bpb[:], whole(bp, P)).then_inc(s["w_in"], 16)
            load_moe(1)
            for n in range(2, NC):
                sp.wait_ge(s["combined"], n - 1)
                load_moe(n)

        @block.gpsimd
        def _(pool):
            nc.gpsimd.memset(coef[:, 0:1], sqrt(subset_coefficient(0)))
            for m in range(1, DEPTH + 1):
                i = nc.gpsimd.memset(coef[:, 2 ** (m - 1):2 ** m], sqrt(subset_coefficient(m)))
            nc.gpsimd.memset(mono[:, :, 0:1], 1.0).then_inc(s["coef_ready"], 1)
            for n in range(NC):
                pool.wait_ge(s["var_ready"], n + 1)
                nc.gpsimd.tensor_tensor(rstd[:], var[:], mem["minus_half"][:, 0:TT], ALU.pow).then_inc(s["rstd_ready"], 1)

        @block.tensor
        def _(pe):
            def turn(b, c):
                n = b * QC + c
                pe.wait_ge(s["y_ready"], n + 1)
                if c == 1:
                    pe.wait_ge(s["feat_read"], n * H)
                if c >= 2:
                    pe.wait_ge(s["added"], n - 1)
                for kd in range(KD):
                    for t in range(TT):
                        i = nc.tensor.transpose(misc[kd][:, t * P:(t + 1) * P], y[:, t, kd * P:(kd + 1) * P],
                                                mem["id32"][:])
                i.then_inc(s["turned"], 1)

            def project(b, c):
                n = b * QC + c
                pe.wait_ge(s["yT_ready"], n + 1)
                if c == 0:
                    pe.wait_ge(s["w_in"], 64)
                for t in range(TT):
                    if t >= 2:
                        pe.wait_ge(s["proj_read"], n * TT + (t - 1))
                    for kd in range(KD):
                        i = nc.tensor.matmul(misc[t % 2][:, 0:NPROJ], yT[:, kd, t * P:(t + 1) * P], wvp[:, kd, :],
                                             start=(kd == 0), stop=(kd == KD - 1))
                    i.then_inc(s["proj_done"], 1)

            def turn_features(b, c, h):
                n = b * QC + c
                if h == 0:
                    pe.wait_ge(s["f_ready"], n + 1)
                if h < 2:
                    pe.wait_ge(s["proj_read"], n * TT + (3 + h))
                else:
                    pe.wait_ge(s["feat_read"], n * H + (h - 1))
                bank = misc[h % 2][:].bitcast(F16)
                for side, f in enumerate((Kf, Qf)):
                    for t in range(TT):
                        at = side * CH + t * P
                        i = nc.tensor.transpose(bank[:, at:at + P], f[:, t * H + h, :], mem["id16"][:])
                i.then_inc(s["fT_done"], 1)

            def output(b, c):
                n = b * QC + c
                pe.wait_ge(s["ctx_ready"], (n + 1) * 2)
                pe.wait_ge(s["feat_read"], (b * QC + min(c + 2, QC)) * H)
                for t in range(TT):
                    for g in range(H // HG):
                        i = nc.tensor.matmul(misc[t // 2][:, (t % 2) * D:(t % 2 + 1) * D], ctxn[:, g, t * P:(t + 1) * P],
                                             wo[:, g, :], start=(g == 0), stop=(g == H // HG - 1))
                i.then_inc(s["wo_done"], 1)

            def scores(b, p):
                c, g, j, hp = PAIRS[p]
                lo = max(j - TT * c, 0) * P
                if p == first_pair(c):
                    pe.wait_ge(s["feat_read"], (b * QC + c + 1) * H)
                if p >= 2:
                    pe.wait_ge(s["exp_done"], b * NPAIR + (p - 1))
                for i in range(2):
                    h = g * HG + hp * 2 + i
                    out = S[p % 2][:, i, :]
                    diag = j >= TT * c
                    last = nc.tensor.matmul(out[:, lo:CH], KT[:, h, j * P:(j + 1) * P], QT[:, c % 2, h, lo:CH],
                                            start=True, stop=not diag)
                    if diag:
                        last = nc.tensor.matmul(out[:, lo:lo + P], mem["id16"][:], mem["mask16"][:], start=False, stop=True)
                last.then_inc(s["s_done"], 1)

            def contexts(b, p):
                c, g, j, hp = PAIRS[p]
                lo = max(j - TT * c, 0) * P
                pe.wait_ge(s["exp_done"], b * NPAIR + (p + 1))
                if j == 0 and hp == 0 and (c, g) != (0, 0):
                    pe.wait_ge(s["cx_free"], (b * QC + c) * 2 + g)
                flags = dict(start=(j == 0), stop=(j == TT * (c + 1) - 1))
                for what in range(2):
                    for i in range(2):
                        h = g * HG + hp * 2 + i
                        q = 32 * (i + 2 * (what ^ hp))
                        w = mem["ones32"][:] if what else V[:, j, h * DH:(h + 1) * DH]
                        last = nc.tensor.matmul(cx[hp][q:q + DH, lo:CH], w, probs[:, p % P_RING, i, lo:CH], **flags)
                last.then_inc(s["pv_done"], 1)

            with pe.Fori(0, BATCH) as b:
                turn(b, 0)
                project(b, 0)
                for h in range(H):
                    turn_features(b, 0, h)
                for c in range(QC):
                    at, p0 = beside(c), first_pair(c)
                    n = 4 * TT * (c + 1)
                    scores(b, p0)
                    for p in range(p0, p0 + n):
                        if p + 1 < p0 + n:
                            scores(b, p + 1)
                        contexts(b, p)
                        what = at.get(p - p0)
                        if what == ("wo",):
                            output(b, c - 1)
                        elif what == ("turn",):
                            turn(b, c + 1)
                        elif what == ("proj",):
                            project(b, c + 1)
                        elif what:
                            turn_features(b, c + 1, what[1])
                output(b, QC - 1)

        @block.scalar
        def _(act):
            def yT_of(b, c):
                act.wait_ge(s["turned"], b * QC + (c + 1))
                for kd in range(KD):
                    i = nc.scalar.copy(yT[:, kd, :], misc[kd][:])
                i.then_inc(s["yT_ready"], 1)

            def th_of(b, c):
                act.wait_ge(s["proj_read"], (b * QC + (c + 1)) * TT)
                nc.scalar.activation(th[:], z[:], ACT.Tanh, scale=0.5).then_inc(s["th_ready"], 1)

            def exps(b, p):
                c, g, j, hp = PAIRS[p]
                lo = max(j - TT * c, 0) * P
                act.wait_ge(s["s_done"], b * NPAIR + (p + 1))
                if p >= P_RING:
                    act.wait_ge(s["pv_done"], b * NPAIR + (p - P_RING + 1))
                nc.scalar.activation(probs[:, p % P_RING, :, lo:CH], S[p % 2][:, :, lo:CH], ACT.Exp).then_inc(s["exp_done"], 1)

            with act.Fori(0, BATCH) as b:
                yT_of(b, 0)
                th_of(b, 0)
                for c in range(QC):
                    at, p0 = beside(c), first_pair(c)
                    at = {k: v[0] for k, v in at.items()}
                    for k in range(4 * TT * (c + 1)):
                        exps(b, p0 + k)
                        if at.get(k - 1) == "turn":
                            yT_of(b, c + 1)
                        if at.get(k - 2) == "proj":
                            th_of(b, c + 1)

        @block.vector
        def _(dve):
            v = nc.vector
            CHAIN, FCHAIN = 2, DEPTH + 3

            def rows_of(b, c):
                n = b * QC + c
                combine_rows(nc, mem, dve, moe[:, c % 2, :, :], moe_in[c % 2], (n - c % 2) * 8 + 16, s["combined"], n)
                wait_carried(nc, dve, idle[:], s["combined"], n + 1)
                for t in range(TT):
                    i = v.bn_stats(stats[:, t, :], x_all[:, n * TT + t, :])
                i.then_inc(s["chain"], 1)
                wait_carried(nc, dve, idle[:], s["chain"], n * CHAIN + 1)
                for t in range(TT):
                    i = v.bn_aggr(mv[:, t, :], stats[:, t, :])
                i.then_inc(s["chain"], 1)
                dve.wait_ge(s["chain"], n * CHAIN + 2)
                v.tensor_scalar(var[:], mv[:, :, 1], LN_EPS, None, ALU.add).then_inc(s["var_ready"], 1)
                dve.wait_ge(s["rstd_ready"], n + 1)
                if c:
                    dve.wait_ge(s["turned"], n)
                for t in range(TT):
                    i = v.tensor_scalar(y[:, t, :], x_all[:, n * TT + t, :], mv[:, t, 0:1], rstd[:, t:t + 1],
                                        ALU.subtract, ALU.mult)
                i.then_inc(s["y_ready"], 1)

            def read_projection(b, c):
                n = b * QC + c
                if c == 0:
                    dve.wait_ge(s["w_in"], 64)
                for t in range(TT):
                    dve.wait_ge(s["proj_done"], n * TT + (t + 1))
                    v.tensor_copy(V[:, TT * c + t, :], misc[t % 2][:, 0:D])
                    v.tensor_tensor(z[:, t, :], misc[t % 2][:, D:NPROJ], bpb[:], ALU.add).then_inc(s["proj_read"], 1)

            def features(b, c):
                n = b * QC + c
                dve.wait_ge(s["th_ready"], n + 1)
                if c == 0:
                    dve.wait_ge(s["coef_ready"], 1)
                k = [0]

                def link(i):
                    k[0] += 1
                    i.then_inc(s["f_ready_chain"], 1)
                    dve.wait_ge(s["f_ready_chain"], n * FCHAIN + k[0])

                thv = th[:].rearrange("p t (h d) -> p (t h) d", d=DEPTH)
                for d in range(DEPTH):
                    w = 2 ** d
                    link(v.tensor_tensor(mono[:, :, w:2 * w], mono[:, :, 0:w],
                                         thv[:, :, d:d + 1].to_broadcast([P, TT * H, w]), ALU.mult))
                link(v.tensor_tensor(feat[:], mono[:], coef[:].unsqueeze(1).to_broadcast([P, TT * H, NF]), ALU.mult))
                link(v.tensor_copy(hl[:, :, 0, :], feat[:]))
                link(v.tensor_tensor(hl[:, :, 1, :], feat[:], hl[:, :, 0, :], ALU.subtract))
                assert k[0] == FCHAIN
                both = hl[:].rearrange("p n a f -> p n (a f)").unsqueeze(2).to_broadcast([P, TT * H, 2, 2 * NF])
                v.tensor_copy(Kf[:].rearrange("p n (r f) -> p n r f", r=2), both)
                for a in range(2):
                    i = v.tensor_copy(Qf[:].rearrange("p n (a r f) -> p n a r f", a=2, r=2)[:, :, a],
                                      hl[:, :, a, :].unsqueeze(2).to_broadcast([P, TT * H, 2, NF]))
                i.then_inc(s["f_ready"], 1)

            def read_features(b, c, h):
                dve.wait_ge(s["fT_done"], (b * QC + c) * H + (h + 1))
                bank = misc[h % 2][:].bitcast(F16)
                v.tensor_copy(KT[:, h, c * CH:(c + 1) * CH], bank[:, 0:CH])
                v.tensor_copy(QT[:, c % 2, h, :], bank[:, CH:2 * CH]).then_inc(s["feat_read"], 1)

            def read_contexts(b, c, g):
                n = (b * QC + c) * 2 + g
                last = max(i for i, q in enumerate(PAIRS) if q[:2] == (c, g))
                dve.wait_ge(s["pv_done"], b * NPAIR + (last + 1))
                h = P // 2
                v.tensor_copy(dd[0:h, g, :], cx[0][h:P, :])
                v.tensor_copy(dd[h:P, g, :], cx[1][0:h, :])
                v.tensor_copy(cc[0:h, g, :], cx[0][0:h, :])
                v.tensor_copy(cc[h:P, g, :], cx[1][h:P, :]).then_inc(s["cx_free"], 1)

            def divide(b, c, g):
                n = (b * QC + c) * 2 + g
                dve.wait_ge(s["cx_free"], n + 1)
                v.reciprocal(rr[:, g, :], dd[:, g, :]).then_inc(s["norm_chain"], 1)
                dve.wait_ge(s["norm_chain"], n + 1)
                v.tensor_tensor(ctxn[:, g, :], cc[:, g, :], rr[:, g, :], ALU.mult).then_inc(s["ctx_ready"], 1)

            def add_output(b, c):
                n = b * QC + c
                dve.wait_ge(s["wo_done"], n + 1)
                for i in range(2):
                    rows = x_all[:, bass.ds(n * TT + 2 * i, 2), :]
                    last = v.tensor_tensor(rows, rows, misc[i][:].rearrange("p (t d) -> p t d", d=D), ALU.add)
                last.then_inc(s["added"], 1)

            with dve.Fori(0, BATCH) as b:
                rows_of(b, 0)
                read_projection(b, 0)
                features(b, 0)
                for h in range(H):
                    read_features(b, 0, h)
                for c in range(QC):
                    more = c + 1 < QC
                    if more:
                        rows_of(b, c + 1)
                    if c:
                        add_output(b, c - 1)
                    if more:
                        read_projection(b, c + 1)
                        features(b, c + 1)
                    read_contexts(b, c, 0)
                    if more:
                        for h in range(H):
                            read_features(b, c + 1, h)
                    divide(b, c, 0)
                    read_contexts(b, c, 1)
                    divide(b, c, 1)
                add_output(b, QC - 1)


def last_block(nc, mem, moe_rows, out_tiles):
    with ExitStack() as ctx:
        moe = ctx.enter_context(nc.sbuf_tensor("l_moe", [P, NT, D], F32))
        moe_in = [ctx.enter_context(nc.semaphore(f"l_moe_in{n}")) for n in range(NC // 2)]
        combined = ctx.enter_context(nc.semaphore("l_combined"))
        stored = ctx.enter_context(nc.semaphore("l_stored"))
        block = ctx.enter_context(nc.Block())

        @block.scalar
        def _(act):
            for n in range(NC // 2):
                act.dma_start(moe[:, n * 2 * TT:(n + 1) * 2 * TT, :], chunk_rows(moe_rows, n, 2)).then_inc(moe_in[n], 16)

        @block.vector
        def _(dve):
            for n in range(NC):
                combine_rows(nc, mem, dve, moe[:, n * TT:(n + 1) * TT, :], moe_in[n // 2], 16, combined, n)

        @block.sync
        def _(sp):
            for n in range(NC):
                sp.wait_ge(combined, n + 1)
                rows = slice(n * TT, (n + 1) * TT)
                sp.dma_start(out_tiles[:, rows, :], mem["x_all"][:, rows, :]).then_inc(stored, 16)
            sp.wait_ge(stored, 16 * NC)


_INS = ["L0_attn_x", "L0_attn_Wp", "L0_attn_bp", "L0_attn_Wv", "L0_attn_Wo", "L0_ffn_attn_nw", "L0_ffn_attn_nb",
        "L0_ffn_wg", "L0_ffn_inter_w", "L0_ffn_inter_b", "L0_ffn_output_w", "L0_ffn_output_b",
        "L0_ffn_res_inter_w", "L0_ffn_res_inter_b", "L0_ffn_res_output_w", "L0_ffn_res_output_b", "L0_ffn_res_coef"]


def kernel(**inputs):
    import numpy as _np
    import concourse.bacc as _bacc
    from concourse import mybir as _mybir
    from concourse.bass_utils import run_bass_kernel_spmd as _run

    nc = _bacc.Bacc("TRN2", target_bir_lowering=False, num_devices=1)
    arrays, args = {}, []
    for name in _INS:
        a = _np.ascontiguousarray(inputs[name])
        arrays[f"in_{name}"] = a
        args.append(nc.dram_tensor(f"in_{name}", a.shape, _mybir.dt.from_np(a.dtype), kind="ExternalInput").ap())
    args.append(nc.dram_tensor("out_0", (BATCH, SEQ, D), _mybir.dt.from_np(_np.dtype("float32")),
                               kind="ExternalOutput").ap())
    macaron(nc, *args)
    r = _run(nc, [arrays], core_ids=[0])
    return r.results[0]["out_0"]
```

```python
from contextlib import ExitStack
from math import sqrt

import concourse.bass as bass
from concourse import mybir

F32, F32R, F16, I32, U32 = (mybir.dt.float32, mybir.dt.float32r, mybir.dt.float16, mybir.dt.int32,
                            mybir.dt.uint32)
ALU = mybir.AluOpType
ACT = mybir.ActivationFunctionType
AX = mybir.AxisListType.X

P = 128
D = 256
KD = D // P
BATCH, SEQ = 2, 2048
TOKENS = BATCH * SEQ
NT = TOKENS // P
TT = 4
CH = TT * P
NC = TOKENS // CH
INTER = 1024
NK = INTER // P
NE = 8
CAP = TOKENS // NE
assert CAP == CH
NG = NE + 2
LN_EPS, FFN_EPS = 1e-5, 1e-12
H, DEPTH, DH = 8, 5, 32
NF = 2 ** DEPTH
ROW = D + 2
HG = 4
QC = SEQ // CH
MASKED = -30000.0
UP_BANKS = 2
H_RING, HS_RING = 2, 4
AHEAD = 2
EARLY = -1


def subset_coefficient(m):
    return sum(0.5 ** d for d in range(max(m, 1), DEPTH + 1)) / DEPTH


def whole(ap, n):
    return ap.rearrange("(a n) -> a n", a=1).to_broadcast([n, ap.shape[0]])


def macaron(nc, x, Wp, bp, Wv, Wo, nw, nb, wg, inter_w, inter_b, output_w, output_b,
            res_inter_w, res_inter_b, res_output_w, res_output_b, res_coef, out):
    x_tiles = x.rearrange("b (t p) d -> p (b t) d", p=P)
    slots_in = nc.dram_tensor("slots_in", [2 * TOKENS, ROW], F32).ap()
    moe_rows = nc.dram_tensor("moe_rows", [TOKENS + CAP, D], F32).ap()

    with ExitStack() as top:
        def sb(name, shape, dt=F32):
            return top.enter_context(nc.sbuf_tensor(name, shape, dt))

        mem = dict(
            x_all=sb("x_all", [P, NT, D]),
            id32=sb("id32", [P, P]), id16=sb("id16", [P, P], F16),
            mask16=sb("mask16", [P, P], F16),
            before16=sb("before16", [P, P], F16),
            ones16=sb("ones16", [P, P], F16), ones32=sb("ones32", [P, DH]),
            minus_half=sb("minus_half", [P, 2 * TT]),
            mv=sb("mv", [P, TT, 2]), var=sb("var", [P, 2, TT]), rstd=sb("rstd", [P, 2, TT]),
            y=sb("y", [P, TT, D]),
            rank=sb("rank", [P, NE]),
            spare=sb("spare", [P, NT]),
            same_expert=sb("same_expert", [P, NE, NT]),
            vecT=sb("vecT", [P, NE * NK + NK + 2 * KD]),
            wgc=sb("wgc", [P, KD, NG]),
            w1_first=sb("w1_first", [P, KD, INTER // 2]),
        )
        x_in = [top.enter_context(nc.semaphore(f"x_in{i}")) for i in range(3)]
        w1_in = top.enter_context(nc.semaphore("w1_in"))
        constants(nc, mem, wg, res_coef, nw, nb, inter_b, res_inter_b, res_inter_w, x_tiles, x_in, w1_in)
        for layer in range(2):
            ffn_block(nc, mem, layer, x_tiles, x_in, res_inter_w, res_output_w, res_output_b, inter_w, output_w,
                      output_b, slots_in, moe_rows, out, w1_in)
            if layer == 0:
                attention_block(nc, mem, Wp, bp, Wv, Wo, moe_rows)


def load_x(nc, mem, sp, x_tiles, x_in, c):
    rows = slice(c * TT, (c + 1) * TT)
    sp.dma_start(mem["x_all"][:, rows, :], x_tiles[:, rows, :]).then_inc(x_in[min(c, 2)], 16)


def constants(nc, mem, wg, res_coef, nw, nb, inter_b, res_inter_b, res_inter_w, x_tiles, x_in, w1_in):
    id32, id16, mask16, before16 = mem["id32"], mem["id16"], mem["mask16"], mem["before16"]
    NV = NE * NK + NK + 2 * KD
    with ExitStack() as ctx:
        rows = ctx.enter_context(nc.sbuf_tensor("vec_rows", [NV, P], F32))
        ids = ctx.enter_context(nc.sbuf_tensor("token_ids", [P, NT], I32))
        ranks = ctx.enter_context(nc.sbuf_tensor("rank_ids", [P, NE], I32))
        vec_ps = ctx.enter_context(nc.psum_tensor("vec_ps", [P, NV], F32))
        loaded = ctx.enter_context(nc.semaphore("c_loaded"))
        filled = ctx.enter_context(nc.semaphore("c_filled"))
        made = ctx.enter_context(nc.semaphore("c_made"))
        turned = ctx.enter_context(nc.semaphore("c_turned"))
        block = ctx.enter_context(nc.Block())

        @block.sync
        def _(sp):
            n0 = NE * NK
            load_x(nc, mem, sp, x_tiles, x_in, 0)
            sp.dma_start(rows[0:n0, :], inter_b.rearrange("e (k p) -> (e k) p", p=P)).then_inc(loaded, 16)
            sp.dma_start(rows[n0:n0 + NK, :], res_inter_b.rearrange("(k p) -> k p", p=P)).then_inc(loaded, 16)
            sp.dma_start(rows[n0 + NK:n0 + NK + KD, :], nw.rearrange("(k p) -> k p", p=P)).then_inc(loaded, 16)
            sp.dma_start(rows[n0 + NK + KD:NV, :], nb.rearrange("(k p) -> k p", p=P)).then_inc(loaded, 16)
            with nc.allow_non_contiguous_dma("router weights, once"):
                sp.dma_start(mem["wgc"][:, :, 0:NE], wg.rearrange("(k p) e -> p k e", p=P)).then_inc(loaded, 16)
                sp.dma_start(mem["wgc"][:, :, NE:NG], res_coef.rearrange("(k p) e -> p k e", p=P)).then_inc(loaded, 16)
            sp.dma_start(mem["w1_first"][:], res_inter_w.rearrange("(k p) n -> p k n", p=P)[:, :, 0:INTER // 2]).then_inc(w1_in, 16)
            load_x(nc, mem, sp, x_tiles, x_in, 1)
            sp.wait_ge(loaded, 96)

        @block.gpsimd
        def _(pool):
            pool.memset(id32[:], 0.0).then_inc(filled, 1)
            pool.memset(id16[:], 0.0).then_inc(filled, 1)
            pool.memset(mask16[:], 0.0).then_inc(filled, 1)
            pool.memset(before16[:], 1.0).then_inc(filled, 1)
            pool.memset(mem["same_expert"][:], 1.0).then_inc(filled, 1)
            pool.memset(mem["ones16"][:], 1.0)
            pool.memset(mem["ones32"][:], 1.0)
            pool.memset(mem["minus_half"][:], -0.5)
            pool.wait_ge(filled, 5)
            for m in (id32, id16):
                pool.affine_select(out=m[:], in_=m[:], compare_op=ALU.not_equal, fill=1.0, base=0,
                                   pattern=[[-1, P]], channel_multiplier=1).then_inc(filled, 1)
            pool.affine_select(out=mask16[:], in_=mask16[:], compare_op=ALU.is_ge, fill=MASKED, base=0,
                               pattern=[[1, P]], channel_multiplier=-1)
            pool.affine_select(out=before16[:], in_=before16[:], compare_op=ALU.is_ge, fill=0.0, base=-1,
                               pattern=[[1, P]], channel_multiplier=-1)
            pool.memset(mem["same_expert"][:, :, 0:1], 0.0)
            pool.iota(ids[:], pattern=[[P, NT]], base=TOKENS, channel_multiplier=1).then_inc(filled, 1)
            pool.iota(ranks[:], pattern=[[-1, NE]], base=NE, channel_multiplier=0).then_inc(filled, 1)
            pool.wait_ge(filled, 9)
            pool.tensor_copy(mem["spare"][:], ids[:])
            pool.tensor_copy(mem["rank"][:], ranks[:]).then_inc(made, 1)

        @block.tensor
        def _(pe):
            pe.wait_ge(filled, 6)
            pe.wait_ge(loaded, 96)
            nc.tensor.transpose(vec_ps[:], rows[:], id32[0:NV, 0:NV]).then_inc(turned, 1)

        @block.vector
        def _(dve):
            dve.wait_ge(turned, 1)
            nc.vector.tensor_copy(mem["vecT"][:], vec_ps[:]).then_inc(made, 1)


class Mlp:

    def __init__(self, nc, ctx, tag):
        def sb(name, shape, dt=F32):
            return ctx.enter_context(nc.sbuf_tensor(f"{tag}_{name}", shape, dt))

        def sem(name):
            return ctx.enter_context(nc.semaphore(f"{tag}_{name}"))

        self.nc = nc
        self.x_hi, self.x_lo = sb("x_hi", [P, KD, CH], F32R), sb("x_lo", [P, KD, CH], F32R)
        self.h = sb("h", [P, H_RING, CH])
        self.h_hi, self.h_lo = sb("h_hi", [P, HS_RING, CH], F32R), sb("h_lo", [P, HS_RING, CH], F32R)
        self.up_ps = [ctx.enter_context(nc.psum_tensor(f"{tag}_up{i}", [P, CH], F32)) for i in range(UP_BANKS)]
        self.down_ps = [ctx.enter_context(nc.psum_tensor(f"{tag}_down{i}", [P, CH], F32)) for i in range(TT)]
        self.side = [ctx.enter_context(nc.psum_tensor(f"{tag}_side{i}", [P, CH], F32)) for i in range(2)]
        self.x_hid = sem("x_hid")
        self.x_split = sem("x_split")
        self.up_done = sem("up_done")
        self.gelu_done = sem("gelu_done")
        self.h_split = sem("h_split")
        self.down_done = sem("down_done")
        self.evacuated = sem("evacuated")

    def split_x_hi(self, dve, c, source):
        if not (isinstance(c, int) and c == 0):
            dve.wait_ge(self.up_done, c * NK)
        self.nc.vector.tensor_copy(self.x_hi[:], source).then_inc(self.x_hid, 1)

    def split_x_lo(self, dve, c, source):
        dve.wait_ge(self.x_hid, c + 1)
        self.nc.vector.tensor_tensor(self.x_lo[:], source, self.x_hi[:], ALU.subtract).then_inc(self.x_split, 1)

    def up(self, pe, c, k, w1_hi, w1_lo, first):
        nc = self.nc
        if not (first and k < UP_BANKS):
            pe.wait_ge(self.gelu_done, c * NK + (k - UP_BANKS + 1))
        bank = self.up_ps[k % UP_BANKS]
        n = 0
        for w, xs in ((w1_hi, self.x_hi), (w1_lo, self.x_hi), (w1_hi, self.x_lo)):
            if k == 0:
                pe.wait_ge(self.x_hid if xs is self.x_hi else self.x_split, c + 1)
            for kd in range(KD):
                last = nc.tensor.matmul(bank[:], w(kd), xs[:, kd, :], start=(n == 0), stop=(n == 3 * KD - 1))
                n += 1
        last.then_inc(self.up_done, 1)

    def gelu(self, act, c, k, bias, first):
        act.wait_ge(self.up_done, c * NK + (k + 1))
        if not (first and k < H_RING):
            act.wait_ge(self.h_split, c * NK + (k - H_RING + 1))
        if not (first and k < HS_RING):
            act.wait_ge(self.down_done, c * NK + (k - HS_RING + 1))
        for to in (self.h[:, k % H_RING, :], self.h_hi[:, k % HS_RING, :]):
            i = self.nc.scalar.activation(to, self.up_ps[k % UP_BANKS][:], ACT.Gelu_apprx_tanh, bias=bias)
        i.then_inc(self.gelu_done, 1)

    def split_h(self, dve, c, k, first):
        nc = self.nc
        dve.wait_ge(self.gelu_done, c * NK + (k + 1))
        if not (first and k < HS_RING):
            dve.wait_ge(self.down_done, c * NK + (k - HS_RING + 1))
        h, hi, lo = self.h[:, k % H_RING, :], self.h_hi[:, k % HS_RING, :], self.h_lo[:, k % HS_RING, :]
        nc.vector.tensor_tensor(lo, h, hi, ALU.subtract).then_inc(self.h_split, 1)

    def down(self, pe, c, k, w2_hi, w2_lo, first):
        nc = self.nc
        pe.wait_ge(self.h_split, c * NK + (k + 1))
        if k == 0 and not first:
            pe.wait_ge(self.evacuated, c)
        for t in range(TT):
            hi = self.h_hi[:, k % HS_RING, t * P:(t + 1) * P]
            lo = self.h_lo[:, k % HS_RING, t * P:(t + 1) * P]
            bank = self.down_ps[t][:, 0:D]
            nc.tensor.matmul(bank, hi, w2_hi, start=(k == 0), stop=False)
            nc.tensor.matmul(bank, hi, w2_lo, start=False, stop=False)
            last = nc.tensor.matmul(bank, lo, w2_hi, start=False, stop=(k == NK - 1))
        last.then_inc(self.down_done, 1)

    def tensor_chunk(self, pe, c, weights, first=False, beside=None):
        for s in range(NK + AHEAD):
            if beside and s == UP_BANKS and EARLY in beside:
                beside[EARLY]()
            if s < NK:
                w1_hi, w1_lo, _, _ = weights(pe, s, True)
                self.up(pe, c, s, w1_hi, w1_lo, first)
            if s >= AHEAD:
                k = s - AHEAD
                _, _, w2_hi, w2_lo = weights(pe, k, False)
                self.down(pe, c, k, w2_hi, w2_lo, first)
                if beside and k in beside:
                    beside[k]()


def split_sems(ctx, nc, tag, names):
    return {n: ctx.enter_context(nc.semaphore(f"{tag}_{n}")) for n in names.split()}


def wait_carried(nc, dve, scratch, sem, value):
    dve.wait_ge(sem, value)
    nc.vector.memset(scratch, 0.0)


W_RING, W_AHEAD = 8, 4


class ExpertFeed:
    WEIGHT_CHUNKS = NC // 2
    ROW_CHUNKS = NC // 2 + -(-TT * ROW // CH)

    def __init__(self, nc, aT_all, w_in, rows_in, inter_w, output_w, slots_in):
        n = self.WEIGHT_CHUNKS * CH
        assert n == KD * INTER == NK * D
        self.raw1 = aT_all[:, 0, 0:n].rearrange("p (h k n) -> p h k n", h=2, k=KD)
        self.raw2 = aT_all[:, 1, 0:n].rearrange("p (h k d) -> p h k d", h=2, d=D)
        self.rows = aT_all[:, 0, n:n + TT * ROW].rearrange("p (t d) -> p t d", d=ROW)
        self.w_in, self.rows_in = w_in, rows_in
        self.w1_rows = inter_w.rearrange("e (k p) n -> e p k n", p=P)
        self.w2_rows = output_w.rearrange("e (k p) n -> e p k n", p=P)
        self.in_rows = slots_in.rearrange("(c t p) d -> c p t d", t=TT, p=P)

    def load_half(self, sp, e, half, sem, value):
        HALF = NK // 2
        sp.wait_ge(sem, value)
        sp.dma_start(self.raw1[:, half], self.w1_rows[e, :, :, half * HALF * P:(half + 1) * HALF * P]).then_inc(self.w_in[half], 16)
        sp.dma_start(self.raw2[:, half], self.w2_rows[e, :, half * HALF:(half + 1) * HALF, :]).then_inc(self.w_in[half], 16)

    def load_rows(self, sp, e, waits):
        for sem, value in waits:
            sp.wait_ge(sem, value)
        sp.dma_start(self.rows, self.in_rows[e]).then_inc(self.rows_in, 16)


def ffn_block(nc, mem, layer, x_tiles, x_in, res_w1, res_w2, res_b2, inter_w, output_w, output_b, slots_in,
              moe_rows, out, w1_in):
    last_layer = layer == 1
    NORMED = layer
    to_rows = out if last_layer else moe_rows
    tag = f"f{layer}"
    x_all, wgc, vecT = mem["x_all"], mem["wgc"], mem["vecT"]
    with ExitStack() as ctx:
        def sb(name, shape, dt=F32):
            return ctx.enter_context(nc.sbuf_tensor(f"{tag}_{name}", shape, dt))

        m = Mlp(nc, ctx, tag)
        aT_all = sb("aT_all", [P, KD, TOKENS])
        with nc.sbuf_tensor(f"{tag}_y_all", [P, NT, ROW], F32) as y_all:
            pass
        ew1 = [sb(f"ew1_{n}", [P, W_RING, KD, P], F32R) for n in ("hi", "lo")]
        ew2 = [sb(f"ew2_{n}", [P, W_RING, D], F32R) for n in ("hi", "lo")]
        sb("y_all_rest", [P, NT * ROW - 2 * W_RING * (KD * P + D)])
        aT = sb("aT", [P, KD, CH])
        w1 = [sb(f"w1_{n}", [P, KD, INTER], F32R) for n in ("hi", "lo")]
        w2 = [sb(f"w2_{n}", [P, NK, D], F32R) for n in ("hi", "lo")]
        raw1 = aT_all[:, 0, TOKENS - KD * INTER:].rearrange("p (k n) -> p k n", k=KD)
        raw2 = aT_all[:, 1, TOKENS - NK * D:].rearrange("p (k n) -> p k n", k=NK)
        b2 = sb("b2", [P, D])
        zeros = sb("zeros", [P, ROW])
        idle = sb("idle", [P, 1])
        stats = sb("stats", [P, TT, 6])
        mv, var, rstd, y = mem["mv"], mem["var"], mem["rstd"], mem["y"]
        lin = sb("lin", [P, 2, TT])
        logits = sb("logits", [P, NT, NG])
        dif, th = sb("dif", [P, TT]), sb("th", [P, TT])
        c0, c1 = sb("c0", [P, NT]), sb("c1", [P, NT])
        part = sb("part", [P, TT, D])
        eb2 = sb("eb2", [P, 2, D])
        vacant, token, weight = (sb(n, [P, TT]) for n in ("vacant", "token", "weight"))
        weight_now = sb("weight_now", [P, TT])
        pool_idle = sb("pool_idle", [P, 1])
        to = sb("to", [P, TT], U32)
        top, eq = sb("top", [P, NT]), sb("eq", [P, NT, NE])
        lm, ex = sb("lm", [P, NT, NE]), sb("ex", [P, NT, NE])
        best, hot, hot16 = sb("best", [P, NT]), sb("hot", [P, NT, NE]), sb("hot16", [P, NT, NE], F16)
        incl, locs = sb("incl", [P, NE, NT]), sb("locs", [P, NE, NT])
        loc, keep, base = sb("loc", [P, NT]), sb("keep", [P, NT]), sb("base", [P, NT])
        t0, t1, rec = sb("t0", [P, NT]), sb("t1", [P, NT]), sb("rec", [P, NT])
        scatter_at = sb("scatter_at", [P, NT], U32)

        s = split_sems(ctx, nc, tag, "stat_chain var_ready rstd_ready y_ready y_kept turned aT_all_ready aT_ready lin_ready "
                       "logits_done logits_read dif_ready th_ready updated gate lm_ready ex_ready hot_ready "
                       "counted scatter_ready scattered b2_in zeros_ready zeroed w_hid w_split x_out rows_in e_turned "
                       "e_aT_ready e_hid e_split done_ready idled token_chain token_read to_ready stored")
        eb2_in = [ctx.enter_context(nc.semaphore(f"{tag}_eb2_in{i}")) for i in range(2)]
        e_in = [ctx.enter_context(nc.semaphore(f"{tag}_e_in{i}")) for i in range(2)]
        feed = ExpertFeed(nc, aT_all, e_in, s["rows_in"], inter_w, output_w, slots_in)
        cols = [slice(0, INTER // 2), slice(INTER // 2, INTER)]
        pieces = [([w[:, :, cols[0]] for w in w1], mem["w1_first"][:]), ([w[:] for w in w2], raw2),
                  ([w[:, :, cols[1]] for w in w1], raw1[:, :, cols[1]])]
        w_in = [w1_in] + [ctx.enter_context(nc.semaphore(f"{tag}_w_in{i}")) for i in range(1, 3)]
        NB = NE * NK + NK
        gain = [vecT[:, NB + k:NB + k + 1] for k in range(KD)]
        shift = [vecT[:, NB + KD + k:NB + KD + k + 1] for k in range(KD)]
        b1 = [vecT[:, NE * NK + k:NE * NK + k + 1] for k in range(NK)]
        block = ctx.enter_context(nc.Block())

        @block.sync
        def _(sp):
            w1_rows, w2_rows = (w.rearrange("(k p) n -> p k n", p=P) for w in (res_w1, res_w2))
            sp.dma_start(pieces[1][1], w2_rows).then_inc(w_in[1], 16)
            sp.dma_start(pieces[2][1], w1_rows[:, :, cols[1]]).then_inc(w_in[2], 16)
            sp.dma_start(b2[:], whole(res_b2, P)).then_inc(s["b2_in"], 16)
            if layer == 0:
                for c in range(2, NC):
                    load_x(nc, mem, sp, x_tiles, x_in, c)
            sp.wait_ge(s["zeros_ready"], 1)
            for rows, width in ((slots_in, ROW),) + (((moe_rows, D),) if layer == 0 else ()):
                for i in range(TOKENS // CH):
                    sp.dma_start(rows[i * CH:(i + 1) * CH, :].rearrange("(p a) d -> p a d", a=TT),
                                 zeros[:, 0:width].unsqueeze(1).to_broadcast([P, TT, width])).then_inc(s["zeroed"], 16)

            def store_x(c, at):
                if last_layer:
                    sp.wait_ge(s["updated"], c + 1)
                    sp.dma_start(out[at:at + CH, :].rearrange("(t p) d -> p t d", p=P),
                                 x_all[:, c * TT:(c + 1) * TT, :]).then_inc(s["x_out"], 16)

            def load_eb2(e, half):
                sp.dma_start(eb2[:, half, :], output_b[e].rearrange("(a n) -> a n", a=1).to_broadcast([P, D])).then_inc(eb2_in[half], 16)

            HALF = NK // 2
            store_x(0, TOKENS)
            for c in range(4):
                store_x(c, c * CH)
            for half in range(2):
                feed.load_half(sp, 0, half, m.x_split, feed.WEIGHT_CHUNKS)
                load_eb2(half, half)
            for c in (4, 5):
                store_x(c, c * CH)
            feed.load_rows(sp, 0, [(m.x_split, feed.ROW_CHUNKS), (s["scattered"], 16 * NT)])
            feed.load_rows(sp, 1, [(s["e_turned"], 1), (s["token_read"], 1)])
            feed.load_half(sp, 1, 0, s["e_split"], HALF)
            for c in (6, 7):
                store_x(c, c * CH)
            feed.load_half(sp, 1, 1, s["e_split"], 2 * HALF)
            with sp.Fori(1, NE // 2) as i:
                for half in range(2):
                    e = i * 2 + half
                    feed.load_rows(sp, e, [(s["e_turned"], e), (s["token_read"], e)])
                    feed.load_half(sp, e, 0, s["e_split"], (e - 1) * NK + HALF)
                    sp.wait_ge(m.evacuated, NC + (e - 1))
                    load_eb2(e, half)
                    feed.load_half(sp, e, 1, s["e_split"], (e - 1) * NK + 2 * HALF)

        @block.gpsimd
        def _(pool):
            nc.gpsimd.memset(zeros[:], 0.0).then_inc(s["zeros_ready"], 1)
            nc.gpsimd.tensor_scalar(y_all[:, :, D], mem["spare"][:], 1.0 - TOKENS, None, ALU.add)

            def norm(a):
                if not (isinstance(a, int) and a < NORMED):
                    pool.wait_ge(s["var_ready"], a + 1 - NORMED)
                    nc.gpsimd.tensor_tensor(rstd[:].rearrange("p a t -> p (a t)"), var[:].rearrange("p a t -> p (a t)"),
                                            mem["minus_half"][:], ALU.pow).then_inc(s["rstd_ready"], 1)
                    pool.wait_ge(s["y_ready"], a + 1 - NORMED)
                nc.gpsimd.tensor_copy(y_all[:, bass.ds(a * TT, TT), 0:D], y[:]).then_inc(s["y_kept"], 1)

            norm(0)
            with pool.Fori(1, NC) as a:
                norm(a)
            pool.wait_ge(s["y_kept"], NC)
            pool.wait_ge(s["scatter_ready"], 1)
            pool.wait_ge(s["zeroed"], 16 * (TOKENS // CH) * (2 if layer == 0 else 1))
            for t in range(NT):
                nc.gpsimd.indirect_dma_start(
                    out=slots_in, out_offset=bass.IndirectOffsetOnAxis(ap=scatter_at[:, t:t + 1], axis=0),
                    in_=y_all[:, t, :], in_offset=None).then_inc(s["scattered"], 16)
            pool.wait_ge(s["scattered"], 16 * NT)

            def give_back(e, first=False):
                if not first:
                    pool.wait_ge(s["idled"], e)
                pool.wait_ge(s["to_ready"], e + 1)
                pool.wait_ge(s["done_ready"], e + 1)
                nc.gpsimd.tensor_tensor(pool_idle[:], mem["minus_half"][:, 0:1], mem["minus_half"][:, 0:1],
                                        ALU.mult).then_inc(s["idled"], 1)
                for t in range(TT):
                    nc.gpsimd.indirect_dma_start(
                        out=to_rows, out_offset=bass.IndirectOffsetOnAxis(ap=to[:, t:t + 1], axis=0),
                        in_=part[:, t, :], in_offset=None, **how).then_inc(s["stored"], 16)

            how = dict(compute_op=ALU.add) if last_layer else {}
            if last_layer:
                pool.wait_ge(s["x_out"], 16 * (NC + 1))
            give_back(0, first=True)
            with pool.Fori(1, NE) as e:
                give_back(e)
            pool.wait_ge(s["stored"], 16 * TT * NE)

        @block.vector
        def _(dve):
            v = nc.vector

            def stats_of(a):
                for t in range(TT):
                    i = v.bn_stats(stats[:, t, :], x_all[:, a * TT + t, :])
                i.then_inc(s["stat_chain"], 1)
                wait_carried(nc, dve, idle[:], s["stat_chain"], (a - NORMED) * 2 + 1)
                for t in range(TT):
                    i = v.bn_aggr(mv[:, t, :], stats[:, t, :])
                i.then_inc(s["stat_chain"], 1)
                dve.wait_ge(s["stat_chain"], (a - NORMED) * 2 + 2)
                v.tensor_scalar(var[:, 0, :], mv[:, :, 1], LN_EPS, None, ALU.add)
                v.tensor_scalar(var[:, 1, :], mv[:, :, 1], 1.0 + FFN_EPS, FFN_EPS * LN_EPS, ALU.mult,
                                ALU.add).then_inc(s["var_ready"], 1)

            def y_of(a):
                dve.wait_ge(s["rstd_ready"], a + 1 - NORMED)
                if not (isinstance(a, int) and a == 0):
                    dve.wait_ge(s["turned"], a)
                    dve.wait_ge(s["y_kept"], a)
                for t in range(TT):
                    i = v.tensor_scalar(y[:, t, :], x_all[:, a * TT + t, :], mv[:, t, 0:1], rstd[:, 1, t:t + 1],
                                        ALU.subtract, ALU.mult)
                i.then_inc(s["y_ready"], 1)

            def x_of(a):
                v.tensor_scalar(lin[:, 0, :], rstd[:, 0, :], 0.5, 1.0, ALU.mult, ALU.add)
                v.scalar_tensor_tensor(lin[:, 1, :], mv[:, :, 0], -0.5, rstd[:, 0, :], ALU.mult,
                                       ALU.mult).then_inc(s["lin_ready"], 1)
                dve.wait_ge(s["lin_ready"], a + 1)
                for t in range(TT):
                    v.tensor_scalar(x_all[:, a * TT + t, :], x_all[:, a * TT + t, :], lin[:, 0, t:t + 1],
                                    lin[:, 1, t:t + 1], ALU.mult, ALU.add)

            def logits_of(a):
                dve.wait_ge(s["logits_done"], a + 1)
                v.tensor_copy(logits[:, bass.ds(a * TT, TT), :],
                              m.side[0][:, 0:TT * NG].rearrange("p (t g) -> p t g", g=NG)).then_inc(s["logits_read"], 1)
                dve.wait_ge(s["logits_read"], a + 1)
                v.tensor_tensor(dif[:], logits[:, bass.ds(a * TT, TT), NE], logits[:, bass.ds(a * TT, TT), NE + 1],
                                ALU.subtract).then_inc(s["dif_ready"], 1)

            def mix_of(a):
                dve.wait_ge(s["th_ready"], a + 1)
                v.tensor_scalar(c0[:, bass.ds(a * TT, TT)], th[:], 0.25, 0.25, ALU.mult, ALU.add)
                v.tensor_scalar(c1[:, bass.ds(a * TT, TT)], th[:], -0.25, 0.25, ALU.mult, ALU.add)

            def empty(c):
                dve.wait_ge(m.down_done, c * NK + NK)
                for t in range(TT):
                    i = v.tensor_tensor(part[:, t, :], m.down_ps[t][:, 0:D], b2[:], ALU.add)
                i.then_inc(m.evacuated, 1)
                dve.wait_ge(m.evacuated, c + 1)
                for t in range(TT):
                    i = v.scalar_tensor_tensor(x_all[:, c * TT + t, :], part[:, t, :], c0[:, bass.ds(c * TT + t, 1)],
                                               x_all[:, c * TT + t, :], ALU.mult, ALU.add)
                i.then_inc(s["updated"], 1)

            def rows_T(c):
                return aT_all[:, :, bass.ds(c * CH, CH)]

            def mlp(c, first=False, beside=None, last=False):
                for k in range(NK):
                    if k == NK - 1:
                        dve.wait_ge(*((s["e_aT_ready"], 1) if last else (s["aT_all_ready"], c + 2)))
                        following = aT[:] if last else rows_T(c + 1)
                        m.split_x_hi(dve, c + 1, following)
                    m.split_h(dve, c, k, first)
                    if k == NK - 1:
                        m.split_x_lo(dve, c + 1, following)
                    for f in (beside or {}).get(k, ()):
                        f()
                empty(c)

            def norms(c):
                p, a, b = c * 2, c * 2 + 1, c * 2 + 2
                at = {1: [lambda: y_of(a)], 2: [lambda: logits_of(p), lambda: x_of(a)],
                      4: [lambda: mix_of(p)], 6: [lambda: logits_of(a)]}
                at[0] = [lambda: stats_of(a)]
                if not (isinstance(c, int) and c == 0):
                    at[0].insert(0, lambda: mix_of(p - 1))
                if not (isinstance(c, int) and b == NC):
                    at[4].append(lambda: stats_of(b))
                    at[5] = [lambda: y_of(b)]
                    at[6].append(lambda: x_of(b))
                return at

            if not NORMED:
                dve.wait_ge(x_in[0], 16)
                stats_of(0)
                y_of(0)
            x_of(0)
            for i, (parts, raw) in enumerate(pieces):
                dve.wait_ge(s["w_hid"], i + 1)
                v.tensor_tensor(parts[1], raw, parts[0], ALU.subtract).then_inc(s["w_split"], 1)
                if i == 0:
                    dve.wait_ge(s["aT_all_ready"], 1)
                    m.split_x_hi(dve, 0, rows_T(0))
                    m.split_x_lo(dve, 0, rows_T(0))
            dve.wait_ge(x_in[1], 16)
            dve.wait_ge(x_in[2], 16 * (NC - 2))
            dve.wait_ge(s["b2_in"], 16)
            mlp(0, True, norms(0))
            with dve.Fori(1, 3) as c:
                mlp(c, False, norms(c))
            mlp(3, False, norms(3))

            chain = [0]

            def link(i):
                chain[0] += 1
                i.then_inc(s["gate"], 1)
                dve.wait_ge(s["gate"], chain[0])

            def bc_e(ap):
                return ap.unsqueeze(2).to_broadcast([P, NT, NE])

            rank = mem["rank"][:].unsqueeze(1).to_broadcast([P, NT, NE])
            gates = logits[:, :, 0:NE]

            def choose():
                link(v.tensor_reduce(top[:], gates, AX, ALU.max))
                v.tensor_tensor(lm[:], gates, bc_e(top[:]), ALU.subtract).then_inc(s["lm_ready"], 1)
                link(v.tensor_tensor(eq[:], gates, bc_e(top[:]), ALU.is_equal))
                link(v.tensor_tensor(eq[:], eq[:], rank, ALU.mult))
                link(v.tensor_reduce(best[:], eq[:], AX, ALU.max))
                link(v.tensor_tensor(hot[:], rank, bc_e(best[:]), ALU.is_equal))
                v.tensor_copy(hot16[:], hot[:]).then_inc(s["hot_ready"], 1)
                link(v.tensor_scalar(base[:], best[:], float(-CAP), float(NE * CAP), ALU.mult, ALU.add))

            def place():
                dve.wait_ge(s["counted"], 1)
                before = m.side[0][:, 0:NE * NT].rearrange("p (e t) -> p e t", e=NE)
                total = m.side[1][:, 0:NE * NT].rearrange("p (e t) -> p e t", e=NE)
                flat = "p e t -> p (e t)"
                link(v.tensor_tensor_scan(incl[:].rearrange(flat), mem["same_expert"][:].rearrange(flat),
                                          m.side[1][:, 0:NE * NT], 0.0, ALU.mult, ALU.add))
                link(v.tensor_tensor(locs[:], incl[:], total, ALU.subtract))
                link(v.tensor_tensor(locs[:], locs[:], before, ALU.add))
                link(v.tensor_tensor(eq[:], locs[:].rearrange("p e t -> p t e"), hot[:], ALU.mult))
                link(v.tensor_reduce(loc[:], eq[:], AX, ALU.add))

            def address():
                link(v.tensor_scalar(keep[:], loc[:], float(CAP), None, ALU.is_lt))
                link(v.tensor_tensor(t1[:], loc[:], base[:], ALU.add))
                link(v.tensor_tensor(t1[:], t1[:], mem["spare"][:], ALU.subtract))
                link(v.tensor_tensor(t1[:], t1[:], keep[:], ALU.mult))
                link(v.tensor_tensor(t1[:], t1[:], mem["spare"][:], ALU.add))
                v.tensor_copy(scatter_at[:], t1[:])

            def weigh():
                dve.wait_ge(s["ex_ready"], 1)
                link(v.tensor_reduce(t0[:], ex[:], AX, ALU.add))
                link(v.reciprocal(rec[:], t0[:]))
                v.tensor_tensor(y_all[:, :, D + 1], rec[:], c1[:], ALU.mult).then_inc(s["scatter_ready"], 1)

            mlp(4, False, {0: [lambda: mix_of(NC - 1), choose], 2: [place], 3: [address], 4: [weigh]})
            with dve.Fori(5, NC - 1) as c:
                mlp(c)

            def split_w(e, k):
                HALF = NK // 2
                n = e * NK + k
                k, e = k % NK, e + k // NK
                r, half, q = k % W_RING, k // HALF, k % HALF
                if k % HALF == 0:
                    dve.wait_ge(feed.w_in[half], (e + 1) * 32)
                a1, a2 = feed.raw1[:, half, :, q * P:(q + 1) * P], feed.raw2[:, half, q, :]
                v.tensor_copy(ew1[0][:, r, :, :], a1)
                v.tensor_copy(ew2[0][:, r, :], a2).then_inc(s["e_hid"], 1)
                dve.wait_ge(s["e_hid"], n + 1)
                v.tensor_tensor(ew1[1][:, r, :, :], a1, ew1[0][:, r, :, :], ALU.subtract)
                v.tensor_tensor(ew2[1][:, r, :], a2, ew2[0][:, r, :], ALU.subtract).then_inc(s["e_split"], 1)

            def tokens_of(e):
                dve.wait_ge(feed.rows_in, (e + 1) * 16)
                marks = feed.rows[:, :, D]
                v.tensor_copy(weight[:], feed.rows[:, :, D + 1])
                v.tensor_scalar(vacant[:], marks, 0.0, None, ALU.is_equal).then_inc(s["token_chain"], 1)
                dve.wait_ge(s["token_chain"], e * 2 + 1)
                v.scalar_tensor_tensor(vacant[:], mem["spare"][:, 0:TT], 1.0, vacant[:], ALU.add,
                                       ALU.mult).then_inc(s["token_chain"], 1)
                dve.wait_ge(s["token_chain"], e * 2 + 2)
                v.scalar_tensor_tensor(token[:], marks, -1.0, vacant[:], ALU.add, ALU.add).then_inc(s["token_read"], 1)

            def expert(e, parity, first=False, last=False):
                c = e + NC
                for k in range(NK):
                    if k == 4:
                        dve.wait_ge(s["token_read"], e + 1)
                        if not first:
                            dve.wait_ge(s["stored"], e * 16 * TT)
                        v.tensor_copy(weight_now[:], weight[:])
                        v.tensor_copy(to[:], token[:]).then_inc(s["to_ready"], 1)
                        if not last:
                            dve.wait_ge(s["to_ready"], e + 1)
                            tokens_of(e + 1)
                    if k == NK - 1 and not last:
                        dve.wait_ge(s["e_aT_ready"], e + 2)
                        m.split_x_hi(dve, c + 1, aT[:])
                    m.split_h(dve, c, k, False)
                    if k == NK - 1 and not last:
                        m.split_x_lo(dve, c + 1, aT[:])
                    if not (last and k + W_AHEAD >= NK):
                        if not (first and k + W_AHEAD < W_RING):
                            dve.wait_ge(m.down_done, c * NK + (k + W_AHEAD - W_RING + 1))
                        split_w(e, k + W_AHEAD)
                dve.wait_ge(m.down_done, c * NK + NK)
                dve.wait_ge(eb2_in[parity], (e - parity) * 8 + 16)
                for t in range(TT):
                    i = v.tensor_tensor(part[:, t, :], m.down_ps[t][:, 0:D], eb2[:, parity, :], ALU.add)
                i.then_inc(m.evacuated, 1)
                dve.wait_ge(m.evacuated, c + 1)
                for t in range(TT):
                    i = v.tensor_scalar(part[:, t, :], part[:, t, :], weight_now[:, t:t + 1], None, ALU.mult)
                i.then_inc(s["done_ready"], 1)

            def first_weights(k):
                if k == 0:
                    dve.wait_ge(s["scattered"], 16 * NT)
                split_w(0, k)

            mlp(NC - 1, False, {1: [lambda: tokens_of(0)],
                                **{2 + k: [lambda k=k: first_weights(k)] for k in range(W_AHEAD)}}, last=True)
            expert(0, 0, first=True)
            with dve.Fori(0, NE // 2 - 1) as i:
                expert(i * 2 + 1, 1)
                expert(i * 2 + 2, 0)
            expert(NE - 1, 1, last=True)

        @block.scalar
        def _(act):
            def aT_of(a):
                act.wait_ge(s["turned"], a + 1)
                if not (isinstance(a, int) and a == 0):
                    act.wait_ge(s["logits_done"], a)
                for kd in range(KD):
                    i = nc.scalar.activation(aT_all[:, kd, bass.ds(a * CH, CH)], m.side[kd][:], ACT.Identity,
                                             bias=shift[kd], scale=gain[kd])
                i.then_inc(s["aT_all_ready"], 1)
                for kd in range(KD):
                    i = nc.scalar.activation(aT[:, kd, :], m.side[kd][:], ACT.Identity, bias=shift[kd], scale=gain[kd])
                i.then_inc(s["aT_ready"], 1)

            def th_of(a):
                act.wait_ge(s["dif_ready"], a + 1)
                nc.scalar.activation(th[:], dif[:], ACT.Tanh, scale=0.5).then_inc(s["th_ready"], 1)

            def mlp(c, first=False, beside=None):
                for k in range(NK):
                    m.gelu(act, c, k, b1[k], first)
                    for f in (beside or {}).get(k, ()):
                        f()

            def norms(c):
                p, a, b = c * 2, c * 2 + 1, c * 2 + 2
                at = {3: [lambda: th_of(p)], 4: [lambda: aT_of(a)], 7: [lambda: th_of(a)]}
                if not (isinstance(c, int) and b == NC):
                    at[7].insert(0, lambda: aT_of(b))
                return at

            def ex_all():
                act.wait_ge(s["lm_ready"], 1)
                nc.scalar.activation(ex[:], lm[:], ACT.Exp).then_inc(s["ex_ready"], 1)

            for i, (parts, raw) in enumerate(pieces):
                act.wait_ge(w_in[i], 16)
                nc.scalar.copy(parts[0], raw).then_inc(s["w_hid"], 1)
                if i == 0:
                    aT_of(0)
            mlp(0, True, norms(0))
            with act.Fori(1, 3) as c:
                mlp(c, False, norms(c))
            mlp(3, False, norms(3))
            mlp(4, False, {2: [ex_all]})
            with act.Fori(5, NC - 1) as c:
                mlp(c)

            def slots_T(e, first=False):
                act.wait_ge(s["e_turned"], e + 1)
                if first:
                    act.wait_ge(s["logits_done"], NC)
                else:
                    act.wait_ge(m.x_split, e + NC)
                for kd in range(KD):
                    i = nc.scalar.activation(aT[:, kd, :], m.side[kd][:], ACT.Identity, bias=shift[kd], scale=gain[kd])
                i.then_inc(s["e_aT_ready"], 1)

            def expert(e, last=False):
                for k in range(NK):
                    m.gelu(act, e + NC, k, vecT[:, bass.ds(e * NK + k, 1)], False)
                    if k == 4 and not last:
                        slots_T(e + 1)

            mlp(NC - 1, False, {4: [lambda: slots_T(0, True)]})
            with act.Fori(0, NE - 1) as e:
                expert(e)
            expert(NE - 1, last=True)

        @block.tensor
        def _(pe):
            def turn(a):
                if not (isinstance(a, int) and a < NORMED):
                    pe.wait_ge(s["y_ready"], a + 1 - NORMED)
                if not (isinstance(a, int) and a == 0):
                    pe.wait_ge(s["aT_ready"], a)
                    pe.wait_ge(s["dif_ready"], a)
                for kd in range(KD):
                    for t in range(TT):
                        i = nc.tensor.transpose(m.side[kd][:, t * P:(t + 1) * P], y[:, t, kd * P:(kd + 1) * P],
                                                mem["id32"][:])
                i.then_inc(s["turned"], 1)

            def route(a):
                pe.wait_ge(s["aT_ready"], a + 1)
                for t in range(TT):
                    for kd in range(KD):
                        i = nc.tensor.matmul(m.side[0][:, t * NG:(t + 1) * NG], aT[:, kd, t * P:(t + 1) * P],
                                             wgc[:, kd, :], start=(kd == 0), stop=(kd == KD - 1))
                i.then_inc(s["logits_done"], 1)

            def count():
                pe.wait_ge(s["hot_ready"], 1)
                hot_et = hot16[:].rearrange("p t e -> p e t")
                nc.tensor.matmul(m.side[0][:, 0:NE * NT].rearrange("p (e t) -> p e t", e=NE), mem["before16"][:],
                                 hot_et, start=True, stop=True)
                nc.tensor.matmul(m.side[1][:, 0:NE * NT].rearrange("p (e t) -> p e t", e=NE), mem["ones16"][:],
                                 hot_et, start=True, stop=True).then_inc(s["counted"], 1)

            def weights(pe, k, is_up, first=False):
                if first and k in ((0, NK // 2) if is_up else (0,)):
                    pe.wait_ge(s["w_split"], (1 if k == 0 else 3) if is_up else 2)
                n = slice(k * P, (k + 1) * P)
                return (lambda kd: w1[0][:, kd, n]), (lambda kd: w1[1][:, kd, n]), w2[0][:, k, :], w2[1][:, k, :]

            def norms(c):
                p, a, b = c * 2, c * 2 + 1, c * 2 + 2
                at = {EARLY: lambda: route(p), 2: lambda: turn(a), 4: lambda: route(a)}
                if not (isinstance(c, int) and b == NC):
                    at[6] = lambda: turn(b)
                return at

            turn(0)
            m.tensor_chunk(pe, 0, lambda pe, k, is_up: weights(pe, k, is_up, True), True, norms(0))
            with pe.Fori(1, 3) as c:
                m.tensor_chunk(pe, c, weights, False, norms(c))
            m.tensor_chunk(pe, 3, weights, False, norms(3))
            m.tensor_chunk(pe, 4, weights, False, {1: count})
            with pe.Fori(5, NC - 1) as c:
                m.tensor_chunk(pe, c, weights)

            def turn_slots(e, first=False):
                pe.wait_ge(feed.rows_in, (e + 1) * 16)
                if not first:
                    pe.wait_ge(s["e_aT_ready"], e)
                for kd in range(KD):
                    for t in range(TT):
                        i = nc.tensor.transpose(m.side[kd][:, t * P:(t + 1) * P], feed.rows[:, t, kd * P:(kd + 1) * P],
                                                mem["id32"][:])
                i.then_inc(s["e_turned"], 1)

            def expert(e, last=False):
                def weights(pe, k, is_up):
                    r = k % W_RING
                    if is_up:
                        pe.wait_ge(s["e_split"], e * NK + (k + 1))
                    return (lambda kd: ew1[0][:, r, kd, :]), (lambda kd: ew1[1][:, r, kd, :]), ew2[0][:, r, :], ew2[1][:, r, :]
                m.tensor_chunk(pe, e + NC, weights, False, None if last else {EARLY: lambda: turn_slots(e + 1)})

            m.tensor_chunk(pe, NC - 1, weights, False, {2: lambda: turn_slots(0, True)})
            with pe.Fori(0, NE - 1) as e:
                expert(e)
            expert(NE - 1, last=True)


NP2 = HG // 2
PAIRS = [(c, g, j, hp) for c in range(QC) for g in range(H // HG) for j in range(TT * (c + 1)) for hp in range(NP2)]
P_RING = 4
NPROJ = D + H * DEPTH
V_RING = SEQ // P + 2 * TT
PRODUCTS = ((0, 0), (0, 1), (1, 0))
TH_BEHIND = 3


def first_pair(c):
    return next(i for i, q in enumerate(PAIRS) if q[0] == c)


def features_at(k, ahead):
    return {k + h: [("features", ahead, h)] for h in range(H)}


SIDE = [
    {5: [("output", -1, None)], **features_at(8, 1)},
    {8: [("output", -1, None)], 12: [("turn", 1, None)], 14: [("project", 1, None)], **features_at(24, 1)},
    {8: [("output", -1, None)], 12: [("turn", 1, None)], 14: [("project", 1, None)], **features_at(26, 1),
     40: [("turn", 2, None)], 42: [("project", 2, None)]},
    {6: [("output", -1, None)], 22: [("turn", 2, None)], 24: [("project", 2, None)], **features_at(42, 1)},
]


def attention_block(nc, mem, Wp, bp, Wv, Wo, moe_rows):
    x_all = mem["x_all"]
    with ExitStack() as ctx:
        def sb(name, shape, dt=F32):
            return ctx.enter_context(nc.sbuf_tensor(f"a_{name}", shape, dt))

        def ps(name, shape):
            return ctx.enter_context(nc.psum_tensor(f"a_{name}", shape, F32))

        KT = sb("KT", [P, H, SEQ], F16)
        QT = sb("QT", [P, 2, H, CH], F16)
        V = sb("V", [P, V_RING, D])
        probs = sb("probs", [P, P_RING, 2, CH])
        wvp = sb("wvp", [P, KD, NPROJ])
        raw_o = probs[:, 0].rearrange("p i q -> p (i q)")[:, 0:KD * D].rearrange("p (k n) -> p k n", k=KD)
        wo = [sb(f"wo_{n}", [P, KD, D], F32R) for n in ("hi", "lo")]
        bpb = sb("bpb", [P, H * DEPTH])
        moe = sb("moe", [P, 2, TT, D])
        stats = sb("stats", [P, TT, 6])
        mv, var, rstd, y = mem["mv"], mem["var"][:, 0, :], mem["rstd"][:, 0, :], mem["y"]
        yT = sb("yT", [P, KD, CH])
        z, th = sb("z", [P, TT, H * DEPTH]), sb("th", [P, TT, H * DEPTH])
        mono, coef = sb("mono", [P, TT * H, NF]), sb("coef", [P, NF])
        feat, hl = sb("feat", [P, TT * H, NF]), sb("hl", [P, TT * H, 2, NF], F16)
        Kf, Qf = sb("Kf", [P, TT * H, 4 * NF], F16), sb("Qf", [P, TT * H, 4 * NF], F16)
        cc, dd = sb("cc", [P, H // HG, CH]), sb("dd", [P, H // HG, CH])
        rr = sb("rr", [P, CH])
        ctxn = sb("ctxn", [P, CH])
        ctx_parts = [sb(f"ctx_{n}", [P, H // HG, CH], F32R) for n in ("hi", "lo")]
        S = [ps(f"S{i}", [P, 2, CH]) for i in range(2)]
        cx = [ps(f"cx{i}", [P, CH]) for i in range(2)]
        misc = [ps(f"misc{i}", [P, CH]) for i in range(2)]

        s = split_sems(ctx, nc, "a", "w_in chain combined var_ready rstd_ready y_ready turned yT_ready proj_done "
                       "proj_read th_ready f_ready fT_done feat_read s_done exp_done pv_done "
                       "norm_chain wo_hid wo_split ctxn_ready ctx_hid ctx_ready wo_done added coef_ready f_ready_chain")
        moe_in = [ctx.enter_context(nc.semaphore(f"a_moe_in{i}")) for i in range(2)]
        cx_free = [ctx.enter_context(nc.semaphore(f"a_cx_free{i}")) for i in range(NP2)]
        dn_free = [ctx.enter_context(nc.semaphore(f"a_dn_free{i}")) for i in range(NP2)]
        block = ctx.enter_context(nc.Block())
        NPAIR = len(PAIRS)

        def v_tile(n, t):
            return (n * TT + t) % V_RING

        def side(n):
            return {k: [w for w in what if 0 <= n + w[1] < NC] for k, what in
                    SIDE[n % QC].items()}

        @block.sync
        def _(sp):
            def load_moe(n):
                sp.dma_start(moe[:, n % 2, :, :], moe_rows[n * CH:(n + 1) * CH, :].rearrange("(t p) d -> p t d", p=P)).then_inc(moe_in[n % 2], 16)

            load_moe(0)
            sp.dma_start(wvp[:, :, 0:D], Wv.rearrange("(k p) n -> p k n", p=P)).then_inc(s["w_in"], 16)
            sp.dma_start(wvp[:, :, D:NPROJ], Wp.rearrange("(k p) n -> p k n", p=P)).then_inc(s["w_in"], 16)
            sp.dma_start(raw_o, Wo.rearrange("(k p) n -> p k n", p=P)).then_inc(s["w_in"], 16)
            sp.dma_start(bpb[:], whole(bp, P)).then_inc(s["w_in"], 16)
            load_moe(1)
            for n in range(2, NC):
                sp.wait_ge(s["combined"], n - 1)
                load_moe(n)

        @block.gpsimd
        def _(pool):
            nc.gpsimd.memset(coef[:, 0:1], sqrt(subset_coefficient(0)))
            for m in range(1, DEPTH + 1):
                i = nc.gpsimd.memset(coef[:, 2 ** (m - 1):2 ** m], sqrt(subset_coefficient(m)))
            nc.gpsimd.memset(mono[:, :, 0:1], 1.0).then_inc(s["coef_ready"], 1)
            for n in range(NC):
                pool.wait_ge(s["var_ready"], n + 1)
                nc.gpsimd.tensor_tensor(rstd, var, mem["minus_half"][:, 0:TT], ALU.pow).then_inc(s["rstd_ready"], 1)
            pool.wait_ge(s["var_ready"], NC + 1)
            nc.gpsimd.tensor_tensor(mem["rstd"][:].rearrange("p a t -> p (a t)"), mem["var"][:].rearrange("p a t -> p (a t)"),
                                    mem["minus_half"][:], ALU.pow).then_inc(s["rstd_ready"], 1)

        @block.tensor
        def _(pe):
            def turn(n, _):
                pe.wait_ge(s["y_ready"], n + 1)
                if n % QC >= 2:
                    pe.wait_ge(s["added"], n - 1)
                elif n % QC == 1 and n > 1:
                    pe.wait_ge(s["added"], n - 2)
                elif n == 1:
                    pe.wait_ge(s["proj_read"], n * TT)
                elif n:
                    pe.wait_ge(s["feat_read"], n * H)
                for kd in range(KD):
                    for t in range(TT):
                        i = nc.tensor.transpose(misc[kd][:, t * P:(t + 1) * P], y[:, t, kd * P:(kd + 1) * P],
                                                mem["id32"][:])
                i.then_inc(s["turned"], 1)

            def project(n, _):
                pe.wait_ge(s["yT_ready"], n + 1)
                if n == 0:
                    pe.wait_ge(s["w_in"], 64)
                for t in range(TT):
                    if t >= 2:
                        pe.wait_ge(s["proj_read"], n * TT + (t - 1))
                    for kd in range(KD):
                        i = nc.tensor.matmul(misc[t % 2][:, 0:NPROJ], yT[:, kd, t * P:(t + 1) * P], wvp[:, kd, :],
                                             start=(kd == 0), stop=(kd == KD - 1))
                    i.then_inc(s["proj_done"], 1)

            def turn_features(n, h):
                if h == 0:
                    pe.wait_ge(s["f_ready"], n + 1)
                if h >= 2:
                    pe.wait_ge(s["feat_read"], n * H + (h - 1))
                elif n % QC == 1 and n > 1:
                    pe.wait_ge(s["added"], n - 1)
                else:
                    later = 1 if n % QC == 0 else 0
                    pe.wait_ge(s["proj_read"], (n + later) * TT + (3 + h))
                bank = misc[h % 2][:].bitcast(F16)
                for of, f in enumerate((Kf, Qf)):
                    for t in range(TT):
                        at = of * CH + t * P
                        i = nc.tensor.transpose(bank[:, at:at + P], f[:, t * H + h, :], mem["id16"][:])
                i.then_inc(s["fT_done"], 1)

            def output(n, _):
                if n == 0:
                    pe.wait_ge(s["wo_split"], 1)
                c, more = n % QC, n + 2 < NC
                if n == NC - 1:
                    pe.wait_ge(s["added"], n)
                elif c == QC - 2 and more:
                    pe.wait_ge(s["proj_read"], (n + 3) * TT)
                else:
                    pe.wait_ge(s["feat_read"], (n + 2) * H)
                for t in range(TT):
                    if t % 2 == 0:
                        pe.wait_ge(s["ctx_ready"], (n + 1) * 4 - 1 + t // 2)
                    for a, b in PRODUCTS:
                        for g in range(H // HG):
                            i = nc.tensor.matmul(misc[t // 2][:, (t % 2) * D:(t % 2 + 1) * D],
                                                 ctx_parts[a][:, g, t * P:(t + 1) * P], wo[b][:, g, :],
                                                 start=((a, b, g) == (0, 0, 0)), stop=(a == 1 and g == H // HG - 1))
                i.then_inc(s["wo_done"], 1)

            def scores(b, p):
                c, g, j, hp = PAIRS[p]
                lo = max(j - TT * c, 0) * P
                if j == 0:
                    pe.wait_ge(s["feat_read"], (b * QC + c) * H + g * HG + hp * 2 + 2)
                if b * NPAIR + p >= 2:
                    pe.wait_ge(s["exp_done"], b * NPAIR + (p - 1))
                for i in range(2):
                    h = g * HG + hp * 2 + i
                    out = S[p % 2][:, i, :]
                    diag = j >= TT * c
                    last = nc.tensor.matmul(out[:, lo:CH], KT[:, h, j * P:(j + 1) * P], QT[:, c % 2, h, lo:CH],
                                            start=True, stop=not diag)
                    if diag:
                        last = nc.tensor.matmul(out[:, lo:lo + P], mem["id16"][:], mem["mask16"][:], start=False, stop=True)
                last.then_inc(s["s_done"], 1)

            def contexts(b, p):
                c, g, j, hp = PAIRS[p]
                n = b * QC + c
                lo = max(j - TT * c, 0) * P
                pe.wait_ge(s["exp_done"], b * NPAIR + (p + 1))
                if j == 0 and (n, g) != (0, 0):
                    pe.wait_ge(cx_free[hp], n * 2 + g)
                    pe.wait_ge(dn_free[hp], n * 2 + g)
                flags = dict(start=(j == 0), stop=(j == TT * (c + 1) - 1))
                for what in range(2):
                    for i in range(2):
                        h = g * HG + hp * 2 + i
                        q = 32 * (i + 2 * (what ^ hp))
                        w = mem["ones32"][:] if what else V[:, v_tile(b * QC, j), h * DH:(h + 1) * DH]
                        last = nc.tensor.matmul(cx[hp][q:q + DH, lo:CH], w, probs[:, p % P_RING, i, lo:CH], **flags)
                last.then_inc(s["pv_done"], 1)

            do = dict(turn=turn, project=project, features=turn_features, output=output)
            turn(0, None)
            project(0, None)
            turn(1, None)
            project(1, None)
            for h in range(H):
                turn_features(0, h)
            steps = [(b, p) for b in range(BATCH) for p in range(NPAIR)]
            at = [side(b * QC + PAIRS[p][0]).get(p - first_pair(PAIRS[p][0]), ()) for b, p in steps]
            for q in range(2):
                scores(*steps[q])
            for q, (b, p) in enumerate(steps):
                if q + 2 < len(steps):
                    scores(*steps[q + 2])
                contexts(b, p)
                for what, ahead, h in at[q]:
                    do[what](b * QC + PAIRS[p][0] + ahead, h)
            output(NC - 1, None)

        @block.scalar
        def _(act):
            def yT_of(n):
                act.wait_ge(s["turned"], n + 1)
                for kd in range(KD):
                    i = nc.scalar.copy(yT[:, kd, :], misc[kd][:])
                i.then_inc(s["yT_ready"], 1)

            def th_of(n):
                act.wait_ge(s["proj_read"], (n + 1) * TT)
                nc.scalar.activation(th[:], z[:], ACT.Tanh, scale=0.5).then_inc(s["th_ready"], 1)

            def exps(b, p):
                c, g, j, hp = PAIRS[p]
                if (b, p) == (0, 0):
                    act.wait_ge(s["wo_split"], 1)
                lo = max(j - TT * c, 0) * P
                act.wait_ge(s["s_done"], b * NPAIR + (p + 1))
                if b * NPAIR + p >= P_RING:
                    act.wait_ge(s["pv_done"], b * NPAIR + (p - P_RING + 1))
                nc.scalar.activation(probs[:, p % P_RING, :, lo:CH], S[p % 2][:, :, lo:CH], ACT.Exp).then_inc(s["exp_done"], 1)

            def read_denominators(n, g, hp):
                b, c = n // QC, n % QC
                last = max(i for i, q in enumerate(PAIRS) if q[:2] == (c, g))
                act.wait_ge(s["pv_done"], b * NPAIR + (last - NP2 + 1 + hp + 1))
                if n:
                    act.wait_ge(s["ctx_ready"], ((n - 1) * 2 + g + 1) * 2)
                h = P // 2
                own, other = slice(hp * h, hp * h + h), slice(h - hp * h, P - hp * h)
                nc.scalar.copy(dd[own, g, :], cx[hp][other, :]).then_inc(dn_free[hp], 1)

            for n in range(2):
                yT_of(n)
                th_of(n)
            for n in range(NC):
                at = side(n)
                steps = 4 * TT * (n % QC + 1)
                for k in range(steps):
                    exps(n // QC, first_pair(n % QC) + k)
                    step = k % (steps // 2)
                    if step < NP2 and (n or k >= NP2):
                        read_denominators(*((n - 1, 1) if k < NP2 else (n, 0)), step)
                    for what, ahead, _ in at.get(k - 2, ()):
                        if what == "turn":
                            yT_of(n + ahead)
                    for what, ahead, _ in at.get(k - TH_BEHIND, ()):
                        if what == "project":
                            th_of(n + ahead)
            for hp in range(NP2):
                read_denominators(NC - 1, 1, hp)

        @block.vector
        def _(dve):
            v = nc.vector
            CHAIN, FCHAIN = 2, DEPTH + 3

            def stats_of(n, k):
                for t in range(TT):
                    i = v.bn_stats(stats[:, t, :], x_all[:, n * TT + t, :])
                i.then_inc(s["chain"], 1)
                dve.wait_ge(s["chain"], k * CHAIN + 1)
                for t in range(TT):
                    i = v.bn_aggr(mv[:, t, :], stats[:, t, :])
                i.then_inc(s["chain"], 1)
                dve.wait_ge(s["chain"], k * CHAIN + 2)

            def next_norm():
                stats_of(0, NC)
                v.tensor_scalar(mem["var"][:, 0, :], mv[:, :, 1], LN_EPS, None, ALU.add)
                v.tensor_scalar(mem["var"][:, 1, :], mv[:, :, 1], 1.0 + FFN_EPS, FFN_EPS * LN_EPS, ALU.mult,
                                ALU.add).then_inc(s["var_ready"], 1)
                dve.wait_ge(s["rstd_ready"], NC + 1)
                dve.wait_ge(s["turned"], NC)
                for t in range(TT):
                    v.tensor_scalar(y[:, t, :], x_all[:, t, :], mv[:, t, 0:1], mem["rstd"][:, 1, t:t + 1],
                                    ALU.subtract, ALU.mult)

            def rows_of(n):
                dve.wait_ge(moe_in[n % 2], (n // 2 + 1) * 16)
                rows = x_all[:, n * TT:(n + 1) * TT, :]
                v.tensor_tensor(rows, rows, moe[:, n % 2, :, :], ALU.add).then_inc(s["combined"], 1)
                dve.wait_ge(s["combined"], n + 1)
                stats_of(n, n)
                v.tensor_scalar(var, mv[:, :, 1], LN_EPS, None, ALU.add).then_inc(s["var_ready"], 1)
                dve.wait_ge(s["rstd_ready"], n + 1)
                if n:
                    dve.wait_ge(s["turned"], n)
                for t in range(TT):
                    i = v.tensor_scalar(y[:, t, :], x_all[:, n * TT + t, :], mv[:, t, 0:1], rstd[:, t:t + 1],
                                        ALU.subtract, ALU.mult)
                i.then_inc(s["y_ready"], 1)

            def split_wo():
                dve.wait_ge(s["w_in"], 64)
                v.tensor_copy(wo[0][:], raw_o).then_inc(s["wo_hid"], 1)
                dve.wait_ge(s["wo_hid"], 1)
                v.tensor_tensor(wo[1][:], raw_o, wo[0][:], ALU.subtract).then_inc(s["wo_split"], 1)

            def read_projection(n):
                if n == 0:
                    dve.wait_ge(s["w_in"], 64)
                for t in range(TT):
                    dve.wait_ge(s["proj_done"], n * TT + (t + 1))
                    v.tensor_copy(V[:, v_tile(n, t), :], misc[t % 2][:, 0:D])
                    v.tensor_tensor(z[:, t, :], misc[t % 2][:, D:NPROJ], bpb[:], ALU.add).then_inc(s["proj_read"], 1)

            def features(n):
                dve.wait_ge(s["th_ready"], n + 1)
                if n == 0:
                    dve.wait_ge(s["coef_ready"], 1)
                else:
                    dve.wait_ge(s["fT_done"], n * H)
                k = [0]

                def link(i):
                    k[0] += 1
                    i.then_inc(s["f_ready_chain"], 1)
                    dve.wait_ge(s["f_ready_chain"], n * FCHAIN + k[0])

                thv = th[:].rearrange("p t (h d) -> p (t h) d", d=DEPTH)
                for d in range(DEPTH):
                    w = 2 ** d
                    link(v.tensor_tensor(mono[:, :, w:2 * w], mono[:, :, 0:w],
                                         thv[:, :, d:d + 1].to_broadcast([P, TT * H, w]), ALU.mult))
                link(v.tensor_tensor(feat[:], mono[:], coef[:].unsqueeze(1).to_broadcast([P, TT * H, NF]), ALU.mult))
                link(v.tensor_copy(hl[:, :, 0, :], feat[:]))
                link(v.tensor_tensor(hl[:, :, 1, :], feat[:], hl[:, :, 0, :], ALU.subtract))
                assert k[0] == FCHAIN
                both = hl[:].rearrange("p n a f -> p n (a f)").unsqueeze(2).to_broadcast([P, TT * H, 2, 2 * NF])
                v.tensor_copy(Kf[:].rearrange("p n (r f) -> p n r f", r=2), both)
                for a in range(2):
                    i = v.tensor_copy(Qf[:].rearrange("p n (a r f) -> p n a r f", a=2, r=2)[:, :, a],
                                      hl[:, :, a, :].unsqueeze(2).to_broadcast([P, TT * H, 2, NF]))
                i.then_inc(s["f_ready"], 1)

            def read_features(n):
                c = n % QC
                for h in range(H):
                    dve.wait_ge(s["fT_done"], n * H + (h + 1))
                    bank = misc[h % 2][:].bitcast(F16)
                    v.tensor_copy(KT[:, h, c * CH:(c + 1) * CH], bank[:, 0:CH])
                    v.tensor_copy(QT[:, c % 2, h, :], bank[:, CH:2 * CH]).then_inc(s["feat_read"], 1)

            def read_contexts(n, g):
                b, c = n // QC, n % QC
                last = max(i for i, q in enumerate(PAIRS) if q[:2] == (c, g))
                h = P // 2
                for hp in range(NP2):
                    dve.wait_ge(s["pv_done"], b * NPAIR + (last - NP2 + 1 + hp + 1))
                    own = slice(hp * h, hp * h + h)
                    v.tensor_copy(cc[own, g, :], cx[hp][own, :]).then_inc(cx_free[hp], 1)

            def divide(n, g):
                for hp in range(NP2):
                    dve.wait_ge(cx_free[hp], n * 2 + g + 1)
                    dve.wait_ge(dn_free[hp], n * 2 + g + 1)
                pieces = 2 if (n, g) == (NC - 1, 1) else 1
                for piece in range(pieces):
                    k, up = (n * 2 + g) * 2 + piece, 2 // pieces
                    q = slice(piece * CH // pieces, (piece + 1) * CH // pieces)
                    if k:
                        dve.wait_ge(s["ctx_ready"], k)
                    v.reciprocal(rr[:, q], dd[:, g, q]).then_inc(s["norm_chain"], up)
                    dve.wait_ge(s["norm_chain"], k + up)
                    v.tensor_tensor(ctxn[:, q], cc[:, g, q], rr[:, q], ALU.mult).then_inc(s["ctxn_ready"], up)
                    dve.wait_ge(s["ctxn_ready"], k + up)
                    v.tensor_copy(ctx_parts[0][:, g, q], ctxn[:, q]).then_inc(s["ctx_hid"], up)
                    dve.wait_ge(s["ctx_hid"], k + up)
                    v.tensor_tensor(ctx_parts[1][:, g, q], ctxn[:, q], ctx_parts[0][:, g, q],
                                    ALU.subtract).then_inc(s["ctx_ready"], up)

            def add_output(n):
                dve.wait_ge(s["wo_done"], n + 1)
                for i in range(2):
                    rows = x_all[:, n * TT + 2 * i:n * TT + 2 * i + 2, :]
                    last = v.tensor_tensor(rows, rows, misc[i][:].rearrange("p (t d) -> p t d", d=D), ALU.add)
                last.then_inc(s["added"], 1)

            rows_of(0)
            split_wo()
            rows_of(1)
            read_projection(0)
            features(0)
            read_projection(1)
            read_features(0)
            features(1)
            for n in range(NC):
                c, next_batch = n % QC, n + 2 < NC
                if c == 0:
                    if n:
                        add_output(n - 1)
                elif c < QC - 1:
                    rows_of(n + 1)
                    add_output(n - 1)
                    read_projection(n + 1)
                    if c > 1:
                        features(n + 1)
                else:
                    add_output(n - 1)
                    if next_batch:
                        features(n + 1)
                        rows_of(n + 2)
                        read_projection(n + 2)
                read_contexts(n, 0)
                if c == 1:
                    features(n + 1)
                if c > 1:
                    divide(n, 0)
                if c < QC - 1 or next_batch:
                    read_features(n + 1)
                if c == QC - 1 and next_batch:
                    features(n + 2)
                if c == QC - 2 and next_batch:
                    rows_of(n + 2)
                    read_projection(n + 2)
                if n == NC - 1:
                    next_norm()
                read_contexts(n, 1)
                if c <= 1:
                    divide(n, 0)
                divide(n, 1)
            add_output(NC - 1)


_INS = ["L0_attn_x", "L0_attn_Wp", "L0_attn_bp", "L0_attn_Wv", "L0_attn_Wo", "L0_ffn_attn_nw", "L0_ffn_attn_nb",
        "L0_ffn_wg", "L0_ffn_inter_w", "L0_ffn_inter_b", "L0_ffn_output_w", "L0_ffn_output_b",
        "L0_ffn_res_inter_w", "L0_ffn_res_inter_b", "L0_ffn_res_output_w", "L0_ffn_res_output_b", "L0_ffn_res_coef"]


def kernel(**inputs):
    import numpy as _np
    import concourse.bacc as _bacc
    from concourse import mybir as _mybir
    from concourse.bass_utils import run_bass_kernel_spmd as _run

    nc = _bacc.Bacc("TRN2", target_bir_lowering=False, num_devices=1)
    arrays, args = {}, []
    for name in _INS:
        a = _np.ascontiguousarray(inputs[name])
        arrays[f"in_{name}"] = a
        args.append(nc.dram_tensor(f"in_{name}", a.shape, _mybir.dt.from_np(a.dtype), kind="ExternalInput").ap())
    args.append(nc.dram_tensor("out_0", (TOKENS + CAP, D), _mybir.dt.from_np(_np.dtype("float32")),
                               kind="ExternalOutput").ap())
    macaron(nc, *args)
    r = _run(nc, [arrays], core_ids=[0])
    return r.results[0]["out_0"][:TOKENS].reshape(BATCH, SEQ, D)
```
